# Optimizing a Trainium2 kernel written in Bass

```python
import numpy as np
import jax
import jax.numpy as jnp

def _softmax(x, axis=-1):
    return jax.nn.softmax(x, axis=axis)

def _gelu(x):
    return jax.nn.gelu(x, approximate=True)

def _silu(x):
    return jax.nn.silu(x)

def _sigmoid(x):
    return jax.nn.sigmoid(x)

def _layernorm(x, axis=-1, eps=1e-05):
    m = jnp.mean(x, axis=axis, keepdims=True)
    v = jnp.var(x, axis=axis, keepdims=True)
    return (x - m) / jnp.sqrt(v + eps)

def _scatter_add(tgt, idx, src, axis=0):
    return tgt.at[idx].add(src)

def _segment_sum(src, seg, n):
    return jax.ops.segment_sum(src, seg, n)
kernel_name = 'mk_sandwich_d1_jaxref_r4_9dda8c'

def setup_inputs(seed: int=0):
    np.random.seed(seed)
    _w = jnp.asarray

    def _L0_attn_setup():
        import jax, jax.numpy as jnp
        import numpy as np
        import math
        B, T, C, FFN = (8, 512, 256, 1024)
        LAYER_ID, N_LAYER = (1, 12)

        def layer_norm(x, g, b, eps=1e-05):
            m = jnp.mean(x, axis=-1, keepdims=True)
            v = jnp.mean(jnp.square(x - m), axis=-1, keepdims=True)
            return (x - m) * jax.lax.rsqrt(v + eps) * g + b

        def token_shift(x):
            return jnp.concatenate([jnp.zeros_like(x[:, :1]), x[:, :-1]], axis=1)

        def wkv(w, u, k, v):
            w = -jnp.exp(w)
            kT = jnp.swapaxes(k, 0, 1)
            vT = jnp.swapaxes(v, 0, 1)

            def step(carry, kv_t):
                aa, bb, pp = carry
                kt, vt = kv_t
                ww = u + kt
                p = jnp.maximum(pp, ww)
                e1 = jnp.exp(pp - p)
                e2 = jnp.exp(ww - p)
                y = (e1 * aa + e2 * vt) / (e1 * bb + e2)
                ww2 = pp + w
                p2 = jnp.maximum(ww2, kt)
                e1b = jnp.exp(ww2 - p2)
                e2b = jnp.exp(kt - p2)
                return ((e1b * aa + e2b * vt, e1b * bb + e2b, p2), y)
            z = jnp.zeros((k.shape[0], k.shape[2]), k.dtype)
            init = (z, z, jnp.full_like(z, -1e+38))
            _, yT = jax.lax.scan(step, init, (kT, vT))
            return jnp.swapaxes(yT, 0, 1)
        key = jax.random.key(seed)
        ks = jax.random.split(key, 8)
        x = jax.random.normal(ks[0], (B, T, C), jnp.float32)
        r0 = LAYER_ID / (N_LAYER - 1)
        r1 = 1.0 - LAYER_ID / N_LAYER
        ddd = (jnp.arange(C, dtype=jnp.float32) / C).reshape(1, 1, C)
        att_mix_k = jnp.power(ddd, r1)
        att_mix_v = jnp.power(ddd, r1) + 0.3 * r0
        att_mix_r = jnp.power(ddd, 0.5 * r1)
        h = jnp.arange(C, dtype=jnp.float32)
        time_decay = -5.0 + 8.0 * jnp.power(h / (C - 1), 0.7 + 1.3 * r0)
        zigzag = ((jnp.arange(C) + 1) % 3 - 1).astype(jnp.float32) * 0.5
        time_first = jnp.full((C,), math.log(0.3), jnp.float32) + zigzag
        ffn_mix_k = jnp.power(ddd, r1)
        ffn_mix_r = jnp.power(ddd, r1)
        s = 0.02
        return {'x': x, 'ln1_g': jnp.ones((C,), jnp.float32), 'ln1_b': jnp.zeros((C,), jnp.float32), 'ln2_g': jnp.ones((C,), jnp.float32), 'ln2_b': jnp.zeros((C,), jnp.float32), 'att_mix_k': att_mix_k, 'att_mix_v': att_mix_v, 'att_mix_r': att_mix_r, 'time_decay': time_decay, 'time_first': time_first, 'Wk': s * jax.random.normal(ks[1], (C, C), jnp.float32), 'Wv': s * jax.random.normal(ks[2], (C, C), jnp.float32), 'Wr': s * jax.random.normal(ks[3], (C, C), jnp.float32), 'Wo': s * jax.random.normal(ks[4], (C, C), jnp.float32), 'ffn_mix_k': ffn_mix_k, 'ffn_mix_r': ffn_mix_r, 'Wk_ffn': s * jax.random.normal(ks[5], (FFN, C), jnp.float32), 'Wr_ffn': s * jax.random.normal(ks[6], (C, C), jnp.float32), 'Wv_ffn': s * jax.random.normal(ks[7], (C, FFN), jnp.float32)}
    _L0_attn_in = _L0_attn_setup()

    def _L0_ffn_setup():
        import jax, jax.numpy as jnp
        import numpy as np
        HIDDEN = 256
        INTER = 1024
        N_EXPERTS = 8

        def geglu(x, w1, w2, w3):
            return jax.nn.gelu(x @ w1, approximate=False) * (x @ w2) @ w3
        key = jax.random.key(seed)
        ks = jax.random.split(key, 8)
        s = 0.02
        x = jax.random.normal(ks[0], (2, 512, HIDDEN), dtype=jnp.float32)
        w1s = jax.random.normal(ks[1], (HIDDEN, INTER), dtype=jnp.float32) * s
        w2s = jax.random.normal(ks[2], (HIDDEN, INTER), dtype=jnp.float32) * s
        w3s = jax.random.normal(ks[3], (INTER, HIDDEN), dtype=jnp.float32) * s
        W1 = jax.random.normal(ks[4], (N_EXPERTS, HIDDEN, INTER), dtype=jnp.float32) * s
        W2 = jax.random.normal(ks[5], (N_EXPERTS, HIDDEN, INTER), dtype=jnp.float32) * s
        W3 = jax.random.normal(ks[6], (N_EXPERTS, INTER, HIDDEN), dtype=jnp.float32) * s
        Wg = jax.random.normal(ks[7], (HIDDEN, N_EXPERTS), dtype=jnp.float32) * s
        return {'x': x, 'w1s': w1s, 'w2s': w2s, 'w3s': w3s, 'W1': W1, 'W2': W2, 'W3': W3, 'Wg': Wg}
    _L0_ffn_in = _L0_ffn_setup()
    _d = {'L0_attn_x': _L0_attn_in['x'], 'L0_attn_ln1_g': _L0_attn_in['ln1_g'], 'L0_attn_ln1_b': _L0_attn_in['ln1_b'], 'L0_attn_ln2_g': _L0_attn_in['ln2_g'], 'L0_attn_ln2_b': _L0_attn_in['ln2_b'], 'L0_attn_att_mix_k': _L0_attn_in['att_mix_k'], 'L0_attn_att_mix_v': _L0_attn_in['att_mix_v'], 'L0_attn_att_mix_r': _L0_attn_in['att_mix_r'], 'L0_attn_time_decay': _L0_attn_in['time_decay'], 'L0_attn_time_first': _L0_attn_in['time_first'], 'L0_attn_Wk': _L0_attn_in['Wk'], 'L0_attn_Wv': _L0_attn_in['Wv'], 'L0_attn_Wr': _L0_attn_in['Wr'], 'L0_attn_Wo': _L0_attn_in['Wo'], 'L0_attn_ffn_mix_k': _L0_attn_in['ffn_mix_k'], 'L0_attn_ffn_mix_r': _L0_attn_in['ffn_mix_r'], 'L0_attn_Wk_ffn': _L0_attn_in['Wk_ffn'], 'L0_attn_Wr_ffn': _L0_attn_in['Wr_ffn'], 'L0_attn_Wv_ffn': _L0_attn_in['Wv_ffn'], 'L0_ffn_w1s': _L0_ffn_in['w1s'], 'L0_ffn_w2s': _L0_ffn_in['w2s'], 'L0_ffn_w3s': _L0_ffn_in['w3s'], 'L0_ffn_W1': _L0_ffn_in['W1'], 'L0_ffn_W2': _L0_ffn_in['W2'], 'L0_ffn_W3': _L0_ffn_in['W3'], 'L0_ffn_Wg': _L0_ffn_in['Wg']}
    _x0 = _d['L0_attn_x']
    _d['L0_attn_x'] = jax.random.normal(jax.random.fold_in(jax.random.key(seed), 1), (1, 4096, 256), dtype=_x0.dtype)
    del _x0
    return _d

def reference(L0_attn_x, L0_attn_ln1_g, L0_attn_ln1_b, L0_attn_ln2_g, L0_attn_ln2_b, L0_attn_att_mix_k, L0_attn_att_mix_v, L0_attn_att_mix_r, L0_attn_time_decay, L0_attn_time_first, L0_attn_Wk, L0_attn_Wv, L0_attn_Wr, L0_attn_Wo, L0_attn_ffn_mix_k, L0_attn_ffn_mix_r, L0_attn_Wk_ffn, L0_attn_Wr_ffn, L0_attn_Wv_ffn, L0_ffn_w1s, L0_ffn_w2s, L0_ffn_w3s, L0_ffn_W1, L0_ffn_W2, L0_ffn_W3, L0_ffn_Wg):

    def _L0_attn_ref(x, ln1_g, ln1_b, ln2_g, ln2_b, att_mix_k, att_mix_v, att_mix_r, time_decay, time_first, Wk, Wv, Wr, Wo, ffn_mix_k, ffn_mix_r, Wk_ffn, Wr_ffn, Wv_ffn):
        import jax, jax.numpy as jnp
        import numpy as np
        import math
        B, T, C, FFN = (8, 512, 256, 1024)
        LAYER_ID, N_LAYER = (1, 12)

        def layer_norm(x, g, b, eps=1e-05):
            m = jnp.mean(x, axis=-1, keepdims=True)
            v = jnp.mean(jnp.square(x - m), axis=-1, keepdims=True)
            return (x - m) * jax.lax.rsqrt(v + eps) * g + b

        def token_shift(x):
            return jnp.concatenate([jnp.zeros_like(x[:, :1]), x[:, :-1]], axis=1)

        def wkv(w, u, k, v):
            w = -jnp.exp(w)
            kT = jnp.swapaxes(k, 0, 1)
            vT = jnp.swapaxes(v, 0, 1)

            def step(carry, kv_t):
                aa, bb, pp = carry
                kt, vt = kv_t
                ww = u + kt
                p = jnp.maximum(pp, ww)
                e1 = jnp.exp(pp - p)
                e2 = jnp.exp(ww - p)
                y = (e1 * aa + e2 * vt) / (e1 * bb + e2)
                ww2 = pp + w
                p2 = jnp.maximum(ww2, kt)
                e1b = jnp.exp(ww2 - p2)
                e2b = jnp.exp(kt - p2)
                return ((e1b * aa + e2b * vt, e1b * bb + e2b, p2), y)
            z = jnp.zeros((k.shape[0], k.shape[2]), k.dtype)
            init = (z, z, jnp.full_like(z, -1e+38))
            _, yT = jax.lax.scan(step, init, (kT, vT))
            return jnp.swapaxes(yT, 0, 1)
        xn = layer_norm(x, ln1_g, ln1_b)
        xx = token_shift(xn)
        xk = xn * att_mix_k + xx * (1.0 - att_mix_k)
        xv = xn * att_mix_v + xx * (1.0 - att_mix_v)
        xr = xn * att_mix_r + xx * (1.0 - att_mix_r)
        k = jnp.einsum('btc,dc->btd', xk, Wk)
        v = jnp.einsum('btc,dc->btd', xv, Wv)
        sr = jax.nn.sigmoid(jnp.einsum('btc,dc->btd', xr, Wr))
        rwkv = sr * wkv(time_decay, time_first, k, v)
        x = x + jnp.einsum('btd,cd->btc', rwkv, Wo)
        xn2 = layer_norm(x, ln2_g, ln2_b)
        xx2 = token_shift(xn2)
        xk2 = xn2 * ffn_mix_k + xx2 * (1.0 - ffn_mix_k)
        xr2 = xn2 * ffn_mix_r + xx2 * (1.0 - ffn_mix_r)
        kf = jnp.square(jax.nn.relu(jnp.einsum('btc,fc->btf', xk2, Wk_ffn)))
        kv = jnp.einsum('btf,cf->btc', kf, Wv_ffn)
        x = x + jax.nn.sigmoid(jnp.einsum('btc,dc->btd', xr2, Wr_ffn)) * kv
        return x

    def _L0_ffn_ref(x, w1s, w2s, w3s, W1, W2, W3, Wg):
        import jax, jax.numpy as jnp
        import numpy as np
        HIDDEN = 256
        INTER = 1024
        N_EXPERTS = 8

        def geglu(x, w1, w2, w3):
            return jax.nn.gelu(x @ w1, approximate=False) * (x @ w2) @ w3
        B, T, C = x.shape
        xf = x.reshape(-1, C)
        shared = geglu(xf, w1s, w2s, w3s)
        logits = xf @ Wg
        idx = jnp.argmax(logits, axis=-1)
        final = jnp.zeros_like(xf)
        for e in range(N_EXPERTS):
            y = geglu(xf, W1[e], W2[e], W3[e])
            final = final + jnp.where((idx == e)[:, None], y, 0.0)
        return (shared + final).reshape(B, T, C)
    x = L0_attn_x
    x = x + _layernorm(_L0_attn_ref(_layernorm(x, axis=-1), L0_attn_ln1_g, L0_attn_ln1_b, L0_attn_ln2_g, L0_attn_ln2_b, L0_attn_att_mix_k, L0_attn_att_mix_v, L0_attn_att_mix_r, L0_attn_time_decay, L0_attn_time_first, L0_attn_Wk, L0_attn_Wv, L0_attn_Wr, L0_attn_Wo, L0_attn_ffn_mix_k, L0_attn_ffn_mix_r, L0_attn_Wk_ffn, L0_attn_Wr_ffn, L0_attn_Wv_ffn), axis=-1)
    x = x + _layernorm(_L0_ffn_ref(_layernorm(x, axis=-1), L0_ffn_w1s, L0_ffn_w2s, L0_ffn_w3s, L0_ffn_W1, L0_ffn_W2, L0_ffn_W3, L0_ffn_Wg), axis=-1)
    return x

_drawn_inputs = setup_inputs


def setup_inputs(seed=0):
    import zlib

    import numpy as np

    out = dict(_drawn_inputs(seed))
    spreads = {'L0_attn_ln1_g': (1.0, 0.6),
     'L0_attn_ln1_b': (0.0, 0.317),
     'L0_attn_ln2_g': (1.0, 0.6),
     'L0_attn_ln2_b': (0.0, 0.346)}
    factors = {'L0_attn_att_mix_k': 4.778,
     'L0_attn_att_mix_r': 6.102,
     'L0_attn_time_first': 3.372,
     'L0_attn_Wk': 3.815,
     'L0_attn_Wr': 3.302,
     'L0_attn_ffn_mix_r': 5.66,
     'L0_attn_Wr_ffn': 2.742}
    for name, (base, spread) in spreads.items():
        noise = np.random.default_rng([zlib.crc32(name.encode()), seed]).standard_normal(out[name].shape)
        drawn = base * np.exp(spread * noise) if base else spread * noise
        out[name] = jnp.asarray(drawn.astype(out[name].dtype))
    for name, factor in factors.items():
        out[name] = (out[name] * factor).astype(out[name].dtype)
    return out
```

```python
from contextlib import ExitStack

import concourse.bass as bass
from concourse import mybir

F32 = mybir.dt.float32
F16 = mybir.dt.float16
I32 = mybir.dt.int32
U32 = mybir.dt.uint32
ALU = mybir.AluOpType
ACT = mybir.ActivationFunctionType
AX = mybir.AxisListType

P = 128
T = 4096
C = 256
CT = C // P
F = 1024
FT = F // P
E = 8
CH = 256
TT = CH // P
NC = T // CH
NT = T // P
NS = (T + E * (P - 1)) // P
EPS = 1e-5
WS = 64.0
KS = 64.0
HS = 64.0
PIECE = CT * F
BIG = -1e38


def at_least(eng, sem, value):
    if value > 0:
        eng.wait_ge(sem, value)


def at_least_slot(eng, sem, value):
    if not isinstance(value, int) or value > 0:
        eng.wait_ge(sem, value)


def build(nc, a):
    ctx = ExitStack()
    with ctx:
        def sb(name, shape, dt=F32):
            return ctx.enter_context(nc.sbuf_tensor(name, [P] + list(shape), dt))

        def ps(name, shape):
            return ctx.enter_context(nc.psum_tensor(name, [P] + list(shape), F32))

        sems = {}

        def S(name):
            if name not in sems:
                sems[name] = ctx.enter_context(nc.semaphore(name))
            return sems[name]

        w_split = nc.dram_tensor("w_split", (E, P, 3, 2, PIECE), F16).ap()
        x1_dram = nc.dram_tensor("x1_dram", (T, C), F32).ap()
        shared_dram = nc.dram_tensor("shared_dram", (T, C), F32).ap()
        sorted_x = nc.dram_tensor("sorted_x", (NS * P, C), F32).ap()
        sorted_y = nc.dram_tensor("sorted_y", (NS * P, C), F32).ap()

        small = {n: sb("w_" + n, [2, CT, C], F16) for n in ("k", "v", "r", "o", "fr")}
        w_fk = sb("w_fk", [2, CT, F], F16)
        w_fv = sb("w_fv", [2, FT, C], F16)
        w_gate = sb("w_gate", [2, CT, E], F16)
        arena = sb("arena", [2 * 6 * PIECE], F16)
        raw = [arena[:, b * 2 * PIECE:(b + 1) * 2 * PIECE].bitcast(F32) for b in range(2)]
        cut = arena[:, 4 * PIECE:6 * PIECE].rearrange("p (h n) -> p h n", h=2)
        shared_w = arena[:, 6 * PIECE:].rearrange("p (m h n) -> p m h n", m=3, h=2)
        expert_w = [arena[:, b * 6 * PIECE:(b + 1) * 6 * PIECE].rearrange("p (m h n) -> p m h n", m=3, h=2)
                    for b in range(2)]

        ident = sb("ident", [P])
        vec = sb("vec", [9, CT])
        G1, B1, G2, B2, MK, MV, MR, FK, FR = range(9)
        rec_vec = sb("rec_vec", [3, CT])
        neg_decay = sb("neg_decay", [CT, CH])
        neg_half = sb("neg_half", [TT])
        ones_row = sb("ones_row", [NT])
        iota_e = sb("iota_e", [E])
        iota_s = sb("iota_s", [NS + 1])
        below = sb("below", [P], F16)
        ones = sb("ones", [P], F16)

        tok = [TT, C]
        chan = [CT, CH]
        x_in = sb("x_in", tok)
        x_res = sb("x_res", tok)
        xa = [sb(f"xa{b}", tok) for b in range(3)]
        normed = sb("normed", tok)
        normed2 = sb("normed2", tok)
        xnT = [sb(f"xnT{b}", [CT, CH + 1]) for b in range(2)]
        xn2T = [sb(f"xn2T{b}", [CT, CH + 1]) for b in range(2)]
        delta = sb("delta", chan)
        delta2 = sb("delta2", chan)
        mixed = [sb(f"mixed{b}", chan) for b in range(2)]
        mix_s = [sb(f"mix_s{m}", [2] + chan, F16) for m in range(3)]
        mix2_s = [sb(f"mix2_s{m}", [2] + chan, F16) for m in range(2)]
        key = sb("key", chan)
        val = sb("val", chan)
        er = sb("er", chan)
        top = sb("top", [CT, CH + 1])
        aa = sb("aa", [CT, CH + 1])
        bb = sb("bb", [CT, CH + 1])
        dist = sb("dist", chan)
        ex = sb("ex", [4, CT, CH])
        rw_s = sb("rw_s", [2] + chan, F16)
        x2 = sb("x2", tok)
        gate_r = sb("gate_r", tok)
        relu_k = [sb(f"relu_k{b}", chan) for b in range(2)]
        mixed2 = relu_k
        kf_s = sb("kf_s", [2, FT, CH], F16)
        x1 = sb("x1", tok)
        xf = sb("xf", [NT, C])
        xf_s = sb("xf_s", [2] + chan, F16)
        gu = [sb(f"gu{b}", [CH]) for b in range(2)]
        sh_s = kf_s
        y_sh = sb("y_sh", tok)
        stats = [sb(f"stats{n}", [TT, 6]) for n in range(4)]
        mv = [sb(f"mv{n}", [TT, 2]) for n in range(4)]
        inv = [sb(f"inv{n}", [6, TT]) for n in range(4)]
        logit = sb("logit", [TT, E])
        best = sb("best", [TT, 8])
        best_at = sb("best_at", [TT, 8], U32)
        best_f = sb("best_f", [TT])
        onehot = sb("onehot", [NT, E], F16)

        tp = [ps(f"tp{b}", [CT, CH]) for b in range(2)]
        up = [ps(f"up{b}", [2, CH]) for b in range(3)]
        yp = [ps(f"yp{b}", tok) for b in range(2)]

        up.append(ps("up3", [2, CH]))

        per_tile = sb("per_tile", [NT, E])
        through = sb("through", [NT, E])
        place = sb("place", [NT, E])
        expert_row = sb("expert_row", [5, E])
        expert_int = sb("expert_int", [2, E], I32)
        row_f = sb("row_f", [NT])
        row_of = sb("row_of", [NT], U32)
        slot_f = sb("slot_f", [NS])
        slot_expert = sb("slot_expert", [NS], I32)

        slot_x = [normed[:, 0, :], normed2[:, 0, :]]
        slot_xs = [mix_s[b][:, :, :, 0:P] for b in range(2)]
        slot_g = [ex[:, b].rearrange("p k n -> p (k n)") for b in range(2)]
        slot_h = [kf_s[:, :, :, b * P:(b + 1) * P] for b in range(2)]
        slot_y = [x1[:, 0, :], y_sh[:, 0, :]]
        RING = 3
        fin_y = [xa[0], xa[1], xa[2]]
        fin_s = [x_in, x_res, x2]
        fin_x = [gate_r, relu_k[0], relu_k[1]]
        fin_x[1:] = [r[:].rearrange("p k n -> p (k n)").rearrange("p (t n) -> p t n", t=TT) for r in relu_k]

        x_tok = a["x"].rearrange("o (c t p) d -> (o c) p t d", c=NC, p=P)
        x1_tok = x1_dram.rearrange("(c t p) d -> c p t d", c=NC, p=P)
        sh_tok = shared_dram.rearrange("(c t p) d -> c p t d", c=NC, p=P)

        def rows(w, k):
            return w.rearrange("(k p) n -> p k n", p=P)

        PRE = [("fkT", w_fk, CT, F), ("fvT", w_fv, FT, C)]
        pieces = []
        for n, w in (("kT", "k"), ("vT", "v"), ("rT", "r"), ("oT", "o"), ("frT", "fr")):
            pieces.append((rows(a[n], CT), CT, C, small[w][:, :, :, :].rearrange("p h k n -> p h (k n)"), None))
        pieces.append((rows(a["gate"], CT), CT, E, w_gate[:, :, :, :].rearrange("p h k n -> p h (k n)"), None))
        for n, w, k, width in PRE:
            pieces.append((rows(a[n], k), k, width, w[:, :, :, :].rearrange("p h k n -> p h (k n)"), None))
        for m, n in enumerate(("w1s", "w2s", "w3s")):
            k = CT if m < 2 else FT
            pieces.append((rows(a[n], k), k, F if m < 2 else C, shared_w[:, m], None))
        N_OWN = len(pieces)
        for e in range(E):
            for m, n in enumerate(("W1", "W2", "W3")):
                k = CT if m < 2 else FT
                pieces.append((rows(a[n][e], k), k, F if m < 2 else C, None, (e, m)))
        NP = len(pieces)
        N_EXP = NP - N_OWN

        def pieces_of(i):
            return range(N_OWN + 2 * i, min(N_OWN + 2 * i + 2, NP)) if i >= 0 else range(0)

        STEPS = range(-1, NC + 2)

        def on(c):
            return 0 <= c < NC

        out_tok = a["out"].rearrange("o (c t p) d -> (o c) p t d", c=NC, p=P)
        zero_rows = sorted_x.rearrange("(g n p) d -> g p n d", p=P, n=NS // 3)
        slot_rows_x = sorted_x.rearrange("(s p) d -> s p d", p=P)
        slot_rows_y = sorted_y.rearrange("(s p) d -> s p d", p=P)

        def slot_steps(eng, step):
            turns = (NS - 5) // 2
            for j in range(-1, 4):
                step(j, j % 2, j // 2)
            with eng.Fori(0, turns) as turn:
                step(2 * turn + 4, 0, turn + 2)
                step(2 * turn + 5, 1, turn + 2)
            for j in range(4 + 2 * turns, NS + 1):
                step(j, j % 2, j // 2)

        def in_range(j):
            return not isinstance(j, int) or 0 <= j < NS

        block = ctx.enter_context(nc.Block())

        @block.sync
        def _(sp):
            for n, name in enumerate(("g1", "b1", "g2", "b2", "mk", "mv", "mr", "fk", "fr")):
                sp.dma_start(vec[:, n, :], a["v_" + name]).then_inc(S("vec_in"), 16)
            sp.dma_start(rec_vec[:, 0, :], a["v_decay"]).then_inc(S("vec_in"), 16)
            sp.dma_start(rec_vec[:, 2, :], a["v_first"]).then_inc(S("vec_in"), 16)

            sp.wait_ge(S("zeros"), 1)
            for g in range(3):
                sp.dma_start(zero_rows[g], xf[:, 0:NS // 3, :]).then_inc(S("zeroed"), 16)

            def load_piece(n):
                src, k, width, _, _ = pieces[n]
                at_least(sp, S("piece_lo"), n - 1)
                at_least(sp, S("piece_hi"), n - 1)
                sp.dma_start(raw[n % 2][:, 0:k * width].rearrange("p (k n) -> p k n", k=k),
                             src).then_inc(S(f"piece_in{n % 2}"), 16)

            def store_piece(n):
                e, m = pieces[n][4]
                sp.wait_ge(S("piece_lo"), n + 1)
                sp.wait_ge(S("piece_hi"), n + 1)
                sp.dma_start(w_split[e, :, m], cut).then_inc(S("piece_out"), 16)

            def load_x(c):
                at_least(sp, S("normed"), TT * c)
                sp.dma_start(x_in[:], x_tok[c]).then_inc(S("x_in"), 16)

            sp.dma_start(x_in[:], x_tok[0]).then_inc(S("x_in"), 16)
            for n in range(N_OWN):
                load_piece(n)
            for i in STEPS:
                if on(i + 2):
                    load_x(i + 2)
                for n in pieces_of(i):
                    load_piece(n)
                if on(i - 1):
                    at_least(sp, S("x1"), i - 1)
                    sp.dma_start(x_res[:], x_tok[i - 1]).then_inc(S("x_res"), 16)
                for n in pieces_of(i):
                    store_piece(n)
                if on(i - 2):
                    sp.wait_ge(S("y_sh"), i - 1)
                    sp.dma_start(sh_tok[i - 2], y_sh[:]).then_inc(S("y_sh_out"), 16)
                if on(i - 1):
                    sp.wait_ge(S("x1"), i)
                    sp.dma_start(x1_tok[i - 1], x1[:]).then_inc(S("x1_out"), 16)

            for c in range(NC):
                if c >= RING:
                    sp.wait_ge(S("fin"), c - RING + 1)
                sp.dma_start(fin_s[c % RING][:], sh_tok[c]).then_inc(S(f"fin_s_in{c % RING}"), 16)
                if c >= RING:
                    sp.wait_ge(S(f"fin_out{c % RING}"), 16 * (c // RING))
                sp.dma_start(fin_x[c % RING][:] if c % RING == 0 else fin_x[c % RING],
                             x1_tok[c]).then_inc(S(f"fin_x_in{c % RING}"), 16)

        def three(pe, out, stat, mov, n, first, last):
            pe.matmul(out, stat(0), mov(0), start=first, stop=False)
            pe.matmul(out, stat(0), mov(1), start=False, stop=False)
            return pe.matmul(out, stat(1), mov(0), start=False, stop=last)

        @block.tensor
        def _(pe):
            def transposes(bank, src, done):
                for t in range(TT):
                    for k in range(CT):
                        m = pe.transpose(bank[:, k, t * P:(t + 1) * P], src[:, t, k * P:(k + 1) * P], ident[:])
                m.then_inc(S(done), 1)

            def channel_major(bank, w, x, done, outs=None):
                for j, (lhs, half) in enumerate(outs):
                    for k in range(CT):
                        m = three(pe, bank[:, half, :], lambda s: lhs(s, k), lambda s: x[:, s, k, :], CH,
                                  k == 0, k == CT - 1)
                m.then_inc(S(done), 1)

            def token_major(bank, x, w, tiles, done):
                for t in range(TT):
                    for k in range(tiles):
                        m = three(pe, bank[:, t, :], lambda s: x[:, s, k, t * P:(t + 1) * P],
                                  lambda s: w(s, k), C, k == 0, k == tiles - 1)
                m.then_inc(S(done), 1)

            pe.wait_ge(S("ident"), 2)
            for i in STEPS:
                c0, c1, c2 = i, i - 1, i - 2
                if on(c1):
                    pe.wait_ge(S("rw_lo"), c1 + 1)
                    pe.wait_ge(S("rw_hi"), c1 + 1)
                    at_least(pe, S("gate_e"), c1)
                    token_major(yp[0], rw_s, lambda s, k: small["o"][:, s, k, :], CT, "wo_mm")
                if on(c2):
                    pe.wait_ge(S("xf"), TT * (c2 + 1))
                    at_least(pe, S("logit"), c2)
                    transposes(tp[0], xf[:, c2 * TT:(c2 + 1) * TT, :], "t4_mm")
                if on(c0):
                    if i == 0:
                        pe.wait_ge(S("piece_lo"), 6)
                        pe.wait_ge(S("piece_hi"), 6)
                    for m, name in enumerate(("k", "v", "r")):
                        pe.wait_ge(S("mix_lo"), 3 * c0 + m + 1)
                        pe.wait_ge(S("mix_hi"), 3 * c0 + m + 1)
                        at_least(pe, S("relu"), 4 * (c1 - 1) + m + 2)
                        if c0 == 1:
                            pe.wait_ge(S("er"), 1)
                        w = small[name]
                        channel_major(up[m], w, mix_s[m], name + "_mm",
                                      [((lambda s, k, j=j, w=w: w[:, s, k, j * P:(j + 1) * P]), j) for j in range(CT)])
                if on(c1):
                    pe.wait_ge(S("normed2"), TT * (c1 + 1))
                    pe.wait_ge(S("xnT"), CT * min(c0 + 1, NC))
                    transposes(tp[1], normed2, "t2_mm")
                if on(c2):
                    pe.wait_ge(S("xf_lo"), c2 + 1)
                    if c2 == 0:
                        pe.wait_ge(S("piece_lo"), N_OWN)
                        pe.wait_ge(S("piece_hi"), N_OWN)
                    for t in range(TT):
                        for k in range(CT):
                            m = three(pe, tp[0][:, 0, t * E:(t + 1) * E],
                                      lambda s: xf_s[:, s, k, t * P:(t + 1) * P],
                                      lambda s: w_gate[:, s, k, :], E, k == 0, k == CT - 1)
                    m.then_inc(S("gate_mm"), 1)
                    for f in range(FT):
                        n = 3 + f
                        if f < 3:
                            pe.wait_ge(S(("key", "val", "er")[f]), min(c0 + 1, NC))
                            at_least(pe, S("relu"), 4 * (c1) if not on(c0) else 0)
                        else:
                            pe.wait_ge(S("gu"), FT * c2 + f - 2)
                        channel_major(up[n % 3], None, xf_s, "sh_up_mm",
                                      [((lambda s, k, m=m, f=f: shared_w[:, m, s, k * F + f * P:k * F + (f + 1) * P]), m)
                                       for m in range(2)])
                    if c2 == NC - 1:
                        pe.wait_ge(S("onehot"), NT)
                        pe.wait_ge(S("triangle"), 3)
                        rows_of = onehot[:, :, :].rearrange("p t e -> p (t e)")
                        pe.matmul(up[3][:, 0, :], below[:], rows_of, start=True, stop=True)
                        pe.matmul(up[3][:, 1, :], ones[:], rows_of, start=True, stop=True).then_inc(S("rank_mm"), 1)
                    pe.wait_ge(S("sh_lo"), FT * (c2 + 1))
                    pe.wait_ge(S("sh_hi"), FT * (c2 + 1))
                    at_least(pe, S("x3a"), c1)
                    token_major(yp[1], sh_s, lambda s, k: shared_w[:, 2, s, k * C:(k + 1) * C], FT, "sh_dn_mm")
                if on(i + 1):
                    pe.wait_ge(S("normed"), TT * (i + 2))
                    at_least(pe, S("xn2T"), CT * c0)
                    transposes(tp[1], normed, "t0_mm")
                if on(c1):
                    if i == 1:
                        pe.wait_ge(S("piece_lo"), N_OWN)
                        pe.wait_ge(S("piece_hi"), N_OWN)
                    for m in range(2):
                        pe.wait_ge(S("mix2_lo"), 2 * c1 + m + 1)
                        pe.wait_ge(S("mix2_hi"), 2 * c1 + m + 1)
                    pe.wait_ge(S("x2"), c1 + 1)
                    token_major(yp[0], mix2_s[1], lambda s, k: small["fr"][:, s, k, :], CT, "r2_mm")
                    for q in range(4):
                        n = 11 + q
                        if q == 3:
                            pe.wait_ge(S("relu"), 4 * c1 + 1)
                        elif c2 >= 0:
                            pe.wait_ge(S("gu"), FT * c2 + 6 + q)
                        else:
                            pe.wait_ge(S("er"), c0 + 1)
                        channel_major(up[n % 3], None, mix2_s[0], "fk_mm",
                                      [((lambda s, k, j=j, q=q: w_fk[:, s, k, (2 * q + j) * P:(2 * q + j + 1) * P]), j)
                                       for j in range(2)])
                    pe.wait_ge(S("kf_lo"), 4 * (c1 + 1))
                    pe.wait_ge(S("kf_hi"), 4 * (c1 + 1))
                    at_least(pe, S("y_sh"), c1)
                    token_major(yp[1], kf_s, lambda s, k: w_fv[:, s, k, :], FT, "fv_mm")

            def slot_products(j, b, h):
                if in_range(j + 1):
                    pe.wait_ge(S(f"slot_x_in{1 - b}"), 16 * (h + b + 1))
                    at_least_slot(pe, S("slot_x_lo"), j)
                    for k in range(CT):
                        m = pe.transpose(tp[1 - b][:, k, 0:P], slot_x[1 - b][:, k * P:(k + 1) * P], ident[:])
                    m.then_inc(S("slot_t"), 1)
                if in_range(j):
                    pe.wait_ge(S(f"slot_w12_{b}"), 16 * (h + 1))
                    pe.wait_ge(S("slot_x_lo"), j + 1)
                    for q in range(2):
                        at_least_slot(pe, S("slot_g"), 2 * j + q - 1)
                        for m in range(2):
                            for g in range(FT // 2):
                                f = q * FT // 2 + g
                                for k in range(CT):
                                    mm = three(pe, up[2 * q + m][:].rearrange("p k n -> p (k n)")[:, g * P:(g + 1) * P],
                                               lambda s: expert_w[b][:, m, s, k * F + f * P:k * F + (f + 1) * P],
                                               lambda s: slot_xs[b][:, s, k, :], P, k == 0, k == CT - 1)
                        mm.then_inc(S("slot_up"), 1)
                if in_range(j - 1):
                    pe.wait_ge(S(f"slot_w3_{1 - b}"), 16 * (h + b))
                    pe.wait_ge(S("slot_h_hi"), 2 * j)
                    pe.wait_ge(S("slot_h_lo"), 2 * j)
                    at_least_slot(pe, S("slot_y"), j - 2)
                    for f in range(FT):
                        mm = three(pe, yp[1 - b][:, 0, :], lambda s: slot_h[1 - b][:, s, f, :],
                                   lambda s: expert_w[1 - b][:, 2, s, f * C:(f + 1) * C], C, f == 0, f == FT - 1)
                    mm.then_inc(S("slot_dn"), 1)

            pe.wait_ge(S("logit"), NC)
            pe.wait_ge(S("y_sh"), NC)
            pe.wait_ge(S("gu"), NC * FT)
            pe.wait_ge(S("routed"), 1)
            slot_steps(pe, slot_products)

        def sh_hi(act, c, f):
            act.wait_ge(S("gu"), FT * c + f + 1)
            at_least(act, S("sh_dn_mm"), c)
            at_least(act, S("fv_mm"), c + 1)
            act.activation(sh_s[:, 0, f, :], gu[f % 2][:], ACT.Copy).then_inc(S("sh_hi"), 1)

        def kf_hi(act, c, q):
            act.wait_ge(S("kf"), 4 * c + q + 1)
            at_least(act, S("fv_mm"), c)
            at_least(act, S("sh_dn_mm"), c)
            act.activation(kf_s[:, 0, 2 * q:2 * q + 2, :], relu_k[q % 2][:], ACT.Copy).then_inc(S("kf_hi"), 1)

        @block.scalar
        def _(act):
            act.wait_ge(S("vec_in"), 16 * 11)
            act.activation(rec_vec[:, 1, :], rec_vec[:, 0, :], ACT.Exp).then_inc(S("decay"), 1)

            def piece_hi(n):
                _, k, width, dst, _ = pieces[n]
                act.wait_ge(S(f"piece_in{n % 2}"), 16 * (n // 2 + 1))
                if dst is None:
                    at_least(act, S("piece_out"), 16 * (n - N_OWN))
                    dst = cut
                act.activation(dst[:, 0, :], raw[n % 2][:, 0:k * width], ACT.Copy,
                               scale=WS).then_inc(S("piece_hi"), 1)

            for n in range(N_OWN):
                piece_hi(n)

            def channel_norm(dst, bank, g, b, c, mm, done, mixes, n_mix, halo):
                act.wait_ge(S(mm), c + 1)
                at_least(act, S(mixes), n_mix * CT * (c - 1))
                act.wait_ge(S("state0"), 5)
                at_least(act, S(halo), c)
                for k in range(CT):
                    act.activation(dst[:, k, 1:CH + 1], bank[:, k, :], ACT.Identity, bias=vec[:, b, k:k + 1],
                                   scale=vec[:, g, k:k + 1]).then_inc(S(done), 1)

            for i in STEPS:
                c0, c1, c2 = i, i - 1, i - 2
                if on(c2):
                    act.wait_ge(S("t4_mm"), c2 + 1)
                    at_least(act, S("sh_up_mm"), FT * c2)
                    act.activation(xf_s[:, 0], tp[0][:], ACT.Copy).then_inc(S("xf_hi"), 1)
                if on(c0):
                    for m, (dst, name, read) in enumerate(((key, "k", "decays"), (val, "v", "rw_lo"))):
                        act.wait_ge(S(name + "_mm"), c0 + 1)
                        at_least(act, S("rw_lo"), c0)
                        at_least(act, S("rw_hi"), c0)
                        act.activation(dst[:], up[m][:], ACT.Copy, scale=1 / WS).then_inc(S(("key", "val")[m]), 1)
                    act.wait_ge(S("r_mm"), c0 + 1)
                    act.activation(er[:], up[2][:], ACT.Exp, scale=-1 / WS).then_inc(S("er"), 1)
                if on(c1):
                    channel_norm(xn2T[c1 % 2], tp[1], G2, B2, c1, "t2_mm", "xn2T", "mix2", 2, "halo2")
                if on(c2):
                    for f in range(FT):
                        act.wait_ge(S("sh_up_mm"), FT * c2 + f + 1)
                        at_least(act, S("sh_lo"), FT * c2 + f - 1)
                        at_least(act, S("sh_hi"), FT * c2 + f - 1)
                        act.activation(gu[f % 2][:], up[(3 + f) % 3][:, 0, :], ACT.Gelu,
                                       scale=1 / WS).then_inc(S("gelu"), 1)
                        if f >= 1:
                            sh_hi(act, c2, f - 1)
                    sh_hi(act, c2, FT - 1)
                if on(i + 1):
                    channel_norm(xnT[(i + 1) % 2], tp[1], G1, B1, i + 1, "t0_mm", "xnT", "mix", 3, "halo")
                if on(c0):
                    act.wait_ge(S("clamps"), 8 * (c0 + 1))
                    act.activation(ex[:, 0:2], ex[:, 0:2], ACT.Exp).then_inc(S("exps"), 1)
                    act.activation(ex[:, 2:4], ex[:, 2:4], ACT.Exp, scale=-1.0).then_inc(S("exps"), 1)
                if on(c1):
                    for m in range(2):
                        act.wait_ge(S("mix2"), CT * (2 * c1 + m + 1))
                        at_least(act, S("fk_mm"), 4 * c1)
                        act.activation(mix2_s[m][:, 0], mixed2[m][:], ACT.Copy).then_inc(S("mix2_hi"), 1)
                if on(i + 1):
                    for m in range(3):
                        n = 3 * (i + 1) + m
                        act.wait_ge(S("mix"), CT * (n + 1))
                        at_least(act, S(("k", "v", "r")[m] + "_mm"), i + 1)
                        act.activation(mix_s[m][:, 0], mixed[n % 2][:], ACT.Copy).then_inc(S("mix_hi"), 1)
                if on(c2):
                    act.wait_ge(S("sh_dn_mm"), c2 + 1)
                    at_least(act, S("y_sh_out"), 16 * c2)
                    act.activation(y_sh[:], yp[1][:], ACT.Copy, scale=1 / (WS * HS)).then_inc(S("y_sh"), 1)
                if on(c1):
                    act.wait_ge(S("r2_mm"), c1 + 1)
                    at_least(act, S("x1"), c1)
                    act.activation(gate_r[:], yp[0][:], ACT.Exp, scale=-1 / WS).then_inc(S("gate_e"), 1)
                    for q in range(4):
                        act.wait_ge(S("fk_mm"), 4 * c1 + q + 1)
                        n = 4 * c1 + q
                        at_least(act, S("kf_lo"), n - 1)
                        at_least(act, S("kf_hi"), n - 1)
                        act.activation(relu_k[q % 2][:], up[(11 + q) % 3][:], ACT.Relu,
                                       scale=KS ** 0.5 / WS).then_inc(S("relu"), 1)
                        if q >= 1:
                            kf_hi(act, c1, q - 1)
                    kf_hi(act, c1, 3)
                if on(c0):
                    act.wait_ge(S("rw"), c0 + 1)
                    at_least(act, S("wo_mm"), c0)
                    act.activation(rw_s[:, 0], val[:], ACT.Copy).then_inc(S("rw_hi"), 1)
                for n in pieces_of(i):
                    piece_hi(n)

            def slot_loads(j, b, h):
                n, nb = j + 1, 1 - b
                if in_range(n):
                    e = act.value_load(slot_expert[0:1, bass.ds(n, 1)], min_val=0, max_val=E - 1)
                    fresh = None
                    if not isinstance(n, int) or n >= 2:
                        old = act.value_load(slot_expert[0:1, bass.ds(n - 2, 1)], min_val=0, max_val=E - 1)
                        fresh = e != old
                    at_least_slot(act, S("slot_up"), 2 * (n - 1))
                    act.dma_start(expert_w[nb][:, 0:2], w_split[bass.ds(e, 1), :, 0:2],
                                 cond=fresh).then_inc(S(f"slot_w12_{nb}"), 16)
                if in_range(j):
                    e = act.value_load(slot_expert[0:1, bass.ds(j, 1)], min_val=0, max_val=E - 1)
                    fresh = None
                    if not isinstance(j, int) or j >= 2:
                        old = act.value_load(slot_expert[0:1, bass.ds(j - 2, 1)], min_val=0, max_val=E - 1)
                        fresh = e != old
                    at_least_slot(act, S("slot_dn"), j - 1)
                    act.dma_start(expert_w[b][:, 2:3], w_split[bass.ds(e, 1), :, 2:3],
                                 cond=fresh).then_inc(S(f"slot_w3_{b}"), 16)

            def slot_act(j, b, h):
                slot_loads(j, b, h)
                if in_range(j + 1):
                    act.wait_ge(S("slot_t"), j + 2)
                    at_least_slot(act, S("slot_up"), 2 * j)
                    act.activation(slot_xs[1 - b][:, 0], tp[1 - b][:, :, 0:P], ACT.Copy).then_inc(S("slot_x_hi"), 1)
                if in_range(j):
                    for q in range(2):
                        act.wait_ge(S("slot_up"), 2 * j + q + 1)
                        at_least_slot(act, S("slot_h_hi"), 2 * j + q - 1)
                        at_least_slot(act, S("slot_h_lo"), 2 * j + q - 1)
                        act.activation(slot_g[q], up[2 * q][:].rearrange("p k n -> p (k n)"), ACT.Gelu,
                                       scale=1 / WS).then_inc(S("slot_gelu"), 1)
                    for q in range(2):
                        act.wait_ge(S("slot_g"), 2 * j + q + 1)
                        at_least_slot(act, S("slot_dn"), j - 1)
                        act.activation(slot_h[b][:, 0, q * FT // 2:(q + 1) * FT // 2, :],
                                       slot_g[q].rearrange("p (f n) -> p f n", n=P),
                                       ACT.Copy).then_inc(S("slot_h_hi"), 1)
                if in_range(j - 1):
                    act.wait_ge(S("slot_dn"), j)
                    at_least_slot(act, S(f"slot_y_out{1 - b}"), 16 * (h + b - 1))
                    act.activation(slot_y[1 - b], yp[1 - b][:, 0, :], ACT.Copy,
                                   scale=1 / (WS * HS)).then_inc(S("slot_y"), 1)
                    act.wait_ge(S("slot_y"), j)
                    act.dma_start(slot_rows_y[bass.ds(j - 1, 1)], slot_y[1 - b]).then_inc(S(f"slot_y_out{1 - b}"), 16)

            act.wait_ge(S("slot_table"), 1)
            act.wait_ge(S("piece_out"), 16 * N_EXP)
            act.wait_ge(S("sh_dn_mm"), NC)

            act.wait_ge(S("rw"), NC)
            act.wait_ge(S("x1_out"), 16 * NC)
            act.wait_ge(S("y_sh_out"), 16 * NC)
            slot_steps(act, slot_act)
            for c in range(NC):
                act.wait_ge(S("fin"), c + 1)
                x = fin_x[c % RING]
                act.dma_start(out_tok[c], x[:] if c % RING == 0 else x).then_inc(S(f"fin_out{c % RING}"), 16)
            for b in range(RING):
                act.wait_ge(S(f"fin_out{b}"), 16 * len(range(b, NC, RING)))

        @block.vector
        def _(dve):
            dve.memset(neg_half[:], -0.5).then_inc(S("const"), 1)
            dve.memset(top[:], BIG).then_inc(S("state0"), 1)
            dve.memset(aa[:], 0.0).then_inc(S("state0"), 1)
            dve.memset(bb[:], 0.0).then_inc(S("state0"), 1)
            dve.memset(xnT[1][:], 0.0).then_inc(S("state0"), 1)
            dve.memset(xn2T[1][:], 0.0).then_inc(S("state0"), 1)
            dve.memset(neg_decay[:], 0.0).then_inc(S("neg0"), 1)
            dve.wait_ge(S("decay"), 1)
            dve.wait_ge(S("neg0"), 1)
            for k in range(CT):
                dve.tensor_scalar(neg_decay[:, k, :], neg_decay[:, k, :], rec_vec[:, 1, k:k + 1], None,
                                  ALU.subtract).then_inc(S("neg_decay"), 1)
            dve.wait_ge(S("state0"), 5)
            dve.wait_ge(S("neg_decay"), CT)

            def piece_lo(n):
                _, k, width, dst, _ = pieces[n]
                dve.wait_ge(S("piece_hi"), n + 1)
                if dst is None:
                    dst = cut
                dve.scalar_tensor_tensor(out=dst[:, 1, :], in0=raw[n % 2][:, 0:k * width], scalar=WS,
                                         in1=dst[:, 0, :], op0=ALU.mult,
                                         op1=ALU.subtract).then_inc(S("piece_lo"), 1)

            def moments(n, src, c):
                for t in range(TT):
                    dve.bn_stats(stats[n][:, t, :], src[:, t, :]).then_inc(S(f"stats{n}"), 1)
                for t in range(TT):
                    dve.wait_ge(S(f"stats{n}"), TT * c + t + 1)
                    if t == 0:
                        at_least(dve, S(f"inv{n}"), c)
                    dve.bn_aggr(mv[n][:, t, :], stats[n][:, t, :]).then_inc(S(f"mv{n}"), 1)

            def ln0(c):
                dve.wait_ge(S("x_in"), 16 * (c + 1))
                moments(0, x_in, c)
                dve.wait_ge(S("inv0"), c + 1)
                for t in range(TT):
                    dve.tensor_scalar(xa[c % 3][:, t, :], x_in[:, t, :], mv[0][:, t, 0:1], inv[0][:, 1, t:t + 1],
                                      ALU.subtract, ALU.mult).then_inc(S("xa"), 1)
                at_least(dve, S("t0_mm"), c)
                for t in range(TT):
                    dve.tensor_scalar(normed[:, t, :], x_in[:, t, :], mv[0][:, t, 0:1], inv[0][:, 5, t:t + 1],
                                      ALU.subtract, ALU.mult).then_inc(S("normed"), 1)

            def halo(buf, c, done, norm):
                dve.wait_ge(S(norm), CT * (c + 1))
                at_least(dve, S(norm), CT * c)
                dve.tensor_copy(buf[c % 2][:, :, 0:1], buf[1 - c % 2][:, :, CH:CH + 1]).then_inc(S(done), 1)

            def mix0(c):
                x = xnT[c % 2]
                if c == 0:
                    dve.tensor_copy(x[:, :, 0:1], xnT[1][:, :, 0:1]).then_inc(S("halo"), 1)
                else:
                    halo(xnT, c, "halo", "xnT")
                dve.wait_ge(S("delta"), c + 1)
                for m in range(3):
                    n = 3 * c + m
                    at_least(dve, S("mix_lo"), n - 1)
                    at_least(dve, S("mix_hi"), n - 1)
                    for k in range(CT):
                        dve.scalar_tensor_tensor(out=mixed[n % 2][:, k, :], in0=delta[:, k, :],
                                                 scalar=vec[:, MK + m, k:k + 1], in1=x[:, k, 0:CH],
                                                 op0=ALU.mult, op1=ALU.add).then_inc(S("mix"), 1)
                    if m >= 1:
                        mix_lo(n - 1)
                mix_lo(3 * c + 2)

            def mix_lo(n):
                dve.wait_ge(S("mix_hi"), n + 1)
                dve.tensor_tensor(mix_s[n % 3][:, 1], mixed[n % 2][:], mix_s[n % 3][:, 0],
                                  ALU.subtract).then_inc(S("mix_lo"), 1)

            def mix2(c):
                x = xn2T[c % 2]
                if c == 0:
                    dve.tensor_copy(x[:, :, 0:1], xn2T[1][:, :, 0:1]).then_inc(S("halo2"), 1)
                else:
                    halo(xn2T, c, "halo2", "xn2T")
                dve.wait_ge(S("delta2"), c + 1)
                for m in range(2):
                    at_least(dve, S("mix2_hi"), 2 * c)
                    at_least(dve, S("kf_hi"), 4 * c)
                    at_least(dve, S("kf_lo"), 4 * c)
                    for k in range(CT):
                        dve.scalar_tensor_tensor(out=mixed2[m][:, k, :], in0=delta2[:, k, :],
                                                 scalar=vec[:, FK + m, k:k + 1], in1=x[:, k, 0:CH],
                                                 op0=ALU.mult, op1=ALU.add).then_inc(S("mix2"), 1)

            def mix2_lo(c):
                for m in range(2):
                    dve.wait_ge(S("mix2_hi"), 2 * c + m + 1)
                    dve.tensor_tensor(mix2_s[m][:, 1], mixed2[m][:], mix2_s[m][:, 0],
                                      ALU.subtract).then_inc(S("mix2_lo"), 1)

            def wkv_before(c):
                yield
                dve.wait_ge(S("key"), c + 1)
                for st, name in ((top, "top"), (aa, "aa"), (bb, "bb")):
                    if c:
                        dve.tensor_copy(st[:, :, 0:1], st[:, :, CH:CH + 1]).then_inc(S("carry"), 1)
                    else:
                        dve.tensor_copy(st[:, :, 0:1], st[:, :, CH:CH + 1]).then_inc(S("carry"), 1)
                dve.wait_ge(S("carry"), 3 * (c + 1))
                yield
                for k in range(CT):
                    dve.tensor_tensor_scan(out=top[:, k, 1:CH + 1], data0=neg_decay[:, k, :], data1=key[:, k, :],
                                           initial=top[:, k, 0:1], op0=ALU.add, op1=ALU.max).then_inc(S("top"), 1)
                yield
                dve.wait_ge(S("top"), CT * (c + 1))
                dve.tensor_tensor(dist[:], key[:], top[:, :, 0:CH], ALU.subtract).then_inc(S("dist"), 1)
                yield
                dve.wait_ge(S("dist"), c + 1)
                for n, (v, op) in enumerate(((2, ALU.min), (1, ALU.min), (2, ALU.max), (1, ALU.max))):
                    for k in range(CT):
                        dve.tensor_scalar(ex[:, n, k, :], dist[:, k, :], rec_vec[:, v, k:k + 1], 0.0,
                                          ALU.add, op).then_inc(S("clamps"), 1)
                    yield

            E_NOW, E_KEEP, E_OLD, E_DECAY = range(4)

            def wkv_after(c):
                dve.wait_ge(S("exps"), 2 * (c + 1))
                dve.wait_ge(S("val"), c + 1)
                dve.tensor_tensor(dist[:], ex[:, E_KEEP], val[:], ALU.mult).then_inc(S("kept"), 1)
                for k in range(CT):
                    dve.tensor_tensor_scan(out=bb[:, k, 1:CH + 1], data0=ex[:, E_DECAY, k, :],
                                           data1=ex[:, E_KEEP, k, :], initial=bb[:, k, 0:1], op0=ALU.mult,
                                           op1=ALU.add).then_inc(S("bb"), 1)
                dve.wait_ge(S("kept"), c + 1)
                for k in range(CT):
                    dve.tensor_tensor_scan(out=aa[:, k, 1:CH + 1], data0=ex[:, E_DECAY, k, :],
                                           data1=dist[:, k, :], initial=aa[:, k, 0:1], op0=ALU.mult,
                                           op1=ALU.add).then_inc(S("aa"), 1)
                dve.tensor_tensor(val[:], ex[:, E_NOW], val[:], ALU.mult).then_inc(S("now"), 1)
                dve.wait_ge(S("aa"), CT * (c + 1))
                dve.tensor_tensor(dist[:], ex[:, E_OLD], aa[:, :, 0:CH], ALU.mult).then_inc(S("old"), 1)
                dve.wait_ge(S("bb"), CT * (c + 1))
                dve.tensor_tensor(ex[:, E_OLD], ex[:, E_OLD], bb[:, :, 0:CH], ALU.mult).then_inc(S("old_den"), 1)
                dve.wait_ge(S("old"), c + 1)
                dve.wait_ge(S("now"), c + 1)
                dve.tensor_tensor(val[:], val[:], dist[:], ALU.add).then_inc(S("num"), 1)
                dve.wait_ge(S("old_den"), c + 1)
                dve.tensor_tensor(ex[:, E_NOW], ex[:, E_OLD], ex[:, E_NOW], ALU.add).then_inc(S("den"), 1)
                dve.wait_ge(S("den"), c + 1)
                dve.wait_ge(S("er"), c + 1)
                dve.scalar_tensor_tensor(out=er[:], in0=er[:], scalar=1.0, in1=ex[:, E_NOW], op0=ALU.add,
                                         op1=ALU.mult).then_inc(S("den_sig"), 1)
                dve.wait_ge(S("den_sig"), c + 1)
                dve.reciprocal(er[:], er[:]).then_inc(S("rec"), 1)
                dve.wait_ge(S("rec"), c + 1)
                dve.wait_ge(S("num"), c + 1)
                dve.tensor_tensor(val[:], val[:], er[:], ALU.mult).then_inc(S("rw"), 1)
                dve.wait_ge(S("rw_hi"), c + 1)
                dve.tensor_tensor(rw_s[:, 1], val[:], rw_s[:, 0], ALU.subtract).then_inc(S("rw_lo"), 1)

            def ln2(c):
                dve.wait_ge(S("wo_mm"), c + 1)
                dve.scalar_tensor_tensor(out=x2[:], in0=yp[0][:], scalar=1 / WS, in1=xa[c % 3][:], op0=ALU.mult,
                                         op1=ALU.add).then_inc(S("x2"), 1)
                dve.wait_ge(S("x2"), c + 1)
                moments(1, x2, c)
                dve.wait_ge(S("inv1"), c + 1)
                at_least(dve, S("t2_mm"), c)
                for t in range(TT):
                    dve.tensor_scalar(normed2[:, t, :], x2[:, t, :], mv[1][:, t, 0:1], inv[1][:, 1, t:t + 1],
                                      ALU.subtract, ALU.mult).then_inc(S("normed2"), 1)

            def last_norms(c):
                dve.wait_ge(S("gate_e"), c + 1)
                dve.tensor_scalar(gate_r[:], gate_r[:], 1.0, None, ALU.add).then_inc(S("gate_1"), 1)
                dve.wait_ge(S("gate_1"), c + 1)
                dve.reciprocal(gate_r[:], gate_r[:]).then_inc(S("gate_rec"), 1)
                dve.wait_ge(S("gate_rec"), c + 1)
                dve.wait_ge(S("fv_mm"), c + 1)
                dve.scalar_tensor_tensor(out=gate_r[:], in0=yp[1][:], scalar=1 / (WS * KS), in1=gate_r[:],
                                         op0=ALU.mult, op1=ALU.mult).then_inc(S("x3a"), 1)
                dve.wait_ge(S("x3a"), c + 1)
                dve.tensor_tensor(gate_r[:], gate_r[:], x2[:], ALU.add).then_inc(S("x3"), 1)
                dve.wait_ge(S("x3"), c + 1)
                moments(2, gate_r, c)
                dve.wait_ge(S("inv2"), c + 1)
                for t in range(TT):
                    dve.tensor_scalar(gate_r[:, t, :], gate_r[:, t, :], mv[2][:, t, 0:1], inv[2][:, 1, t:t + 1],
                                      ALU.subtract, ALU.mult).then_inc(S("x3n"), 1)
                dve.wait_ge(S("x3n"), TT * (c + 1))
                dve.wait_ge(S("x_res"), 16 * (c + 1))
                at_least(dve, S("x1_out"), 16 * c)
                dve.tensor_tensor(x1[:], gate_r[:], x_res[:], ALU.add).then_inc(S("x1"), 1)
                dve.wait_ge(S("x1"), c + 1)
                moments(3, x1, c)
                dve.wait_ge(S("inv3"), c + 1)
                for t in range(TT):
                    dve.tensor_scalar(xf[:, TT * c + t, :], x1[:, t, :], mv[3][:, t, 0:1], inv[3][:, 1, t:t + 1],
                                      ALU.subtract, ALU.mult).then_inc(S("xf"), 1)

            def gate(c):
                dve.wait_ge(S("gate_mm"), c + 1)
                dve.tensor_copy(logit[:], tp[0][:, 0, 0:TT * E]).then_inc(S("logit"), 1)
                dve.wait_ge(S("logit"), c + 1)
                for t in range(TT):
                    dve.max(best[:, t, :], logit[:, t, :]).then_inc(S("best"), 1)
                for t in range(TT):
                    dve.wait_ge(S("best"), TT * c + t + 1)
                    dve.max_index(best_at[:, t, :], best[:, t, :], logit[:, t, :]).then_inc(S("best_at"), 1)
                dve.wait_ge(S("best_at"), TT * (c + 1))
                dve.tensor_copy(best_f[:], best_at[:, :, 0]).then_inc(S("best_f"), 1)
                dve.wait_ge(S("best_f"), c + 1)
                for t in range(TT):
                    dve.tensor_scalar(onehot[:, TT * c + t, :], iota_e[:], best_f[:, t:t + 1], None,
                                      ALU.is_equal).then_inc(S("onehot"), 1)

            for n in range(6):
                piece_lo(n)
            ln0(0)
            for n in range(6, N_OWN):
                piece_lo(n)
            dve.wait_ge(S("iotas"), 3)
            dve.wait_ge(S("zeroed"), 16 * 3)
            for i in STEPS:
                c0, c1, c2 = i, i - 1, i - 2
                if on(c1):
                    ln2(c1)
                if on(c2):
                    dve.wait_ge(S("xf_hi"), c2 + 1)
                    dve.tensor_tensor(xf_s[:, 1], tp[0][:], xf_s[:, 0], ALU.subtract).then_inc(S("xf_lo"), 1)
                    gate(c2)
                if on(c1):
                    mix2(c1)
                before = wkv_before(c0) if on(c0) else iter(())
                next(before, None)
                for f in range(FT):
                    if on(c2):
                        dve.wait_ge(S("gelu"), FT * c2 + f + 1)
                        dve.scalar_tensor_tensor(out=gu[f % 2][:], in0=up[(3 + f) % 3][:, 1, :], scalar=HS / WS,
                                                 in1=gu[f % 2][:], op0=ALU.mult, op1=ALU.mult).then_inc(S("gu"), 1)
                    if f == 3 and on(c1):
                        pass
                    next(before, None)
                for _ in before:
                    pass
                if on(c1):
                    mix2_lo(c1)
                if on(i + 1):
                    mix0(i + 1)
                if on(i + 2):
                    ln0(i + 2)
                if on(c0):
                    wkv_after(c0)
                if on(c1):
                    last_norms(c1)
                for n in pieces_of(i):
                    piece_lo(n)

            s = S("route")
            count = [0]

            def then(ins):
                count[0] += 1
                ins.then_inc(s, 1)

            def before():
                dve.wait_ge(s, count[0])

            dve.wait_ge(S("rank_mm"), 1)
            flat = up[3][:].rearrange("p h (t e) -> p h t e", e=E)
            then(dve.tensor_copy(per_tile[:], flat[:, 1]))
            before()
            for e in range(E):
                then(dve.tensor_tensor_scan(out=through[:, :, e], data0=ones_row[:], data1=per_tile[:, :, e],
                                            initial=0.0, op0=ALU.mult, op1=ALU.add))
            before()
            SLOTS, ENDS, FIRST, TOKENS = range(4)
            then(dve.tensor_tensor(per_tile[:], through[:], per_tile[:], ALU.subtract))
            then(dve.tensor_scalar(expert_row[:, TOKENS, :], through[:, NT - 1, :], float(P - 1), None, ALU.add))
            before()
            then(dve.tensor_tensor(place[:], flat[:, 0], per_tile[:], ALU.add))
            then(dve.tensor_copy(expert_int[:, 0, :], expert_row[:, TOKENS, :]))
            before()
            then(dve.tensor_scalar(expert_int[:, 1, :], expert_int[:, 0, :], P.bit_length() - 1, None,
                                   ALU.arith_shift_right))
            before()
            then(dve.tensor_copy(expert_row[:, SLOTS, :], expert_int[:, 1, :]))
            before()
            then(dve.tensor_tensor_scan(out=expert_row[:, ENDS, :], data0=ones_row[:, 0:E],
                                        data1=expert_row[:, SLOTS, :], initial=0.0, op0=ALU.mult, op1=ALU.add))
            before()
            then(dve.tensor_tensor(expert_row[:, FIRST, :], expert_row[:, ENDS, :], expert_row[:, SLOTS, :],
                                   ALU.subtract))
            then(dve.tensor_scalar(slot_f[:], iota_s[:, 0:NS], expert_row[:, ENDS, 0:1], None, ALU.is_ge))
            before()
            then(dve.tensor_scalar(expert_row[:, FIRST, :], expert_row[:, FIRST, :], float(P), None, ALU.mult))
            for e in range(1, E - 1):
                before()
                then(dve.scalar_tensor_tensor(out=slot_f[:], in0=iota_s[:, 0:NS], scalar=expert_row[:, ENDS, e:e + 1],
                                              in1=slot_f[:], op0=ALU.is_ge, op1=ALU.add))
            before()
            dve.tensor_copy(slot_expert[:], slot_f[:]).then_inc(S("slot_table"), 1)
            for e in range(E):
                then(dve.scalar_tensor_tensor(out=place[:, :, e], in0=place[:, :, e],
                                              scalar=expert_row[:, FIRST, e:e + 1], in1=onehot[:, :, e],
                                              op0=ALU.add, op1=ALU.mult))
            before()
            then(dve.tensor_reduce(row_f[:], place[:], AX.X, ALU.add))
            before()
            dve.tensor_copy(row_of[:], row_f[:]).then_inc(S("routed"), 1)

            def slot_dve(j, b, h):
                if in_range(j + 1):
                    dve.wait_ge(S("slot_x_hi"), j + 2)
                    dve.tensor_tensor(slot_xs[1 - b][:, 1], tp[1 - b][:, :, 0:P], slot_xs[1 - b][:, 0],
                                      ALU.subtract).then_inc(S("slot_x_lo"), 1)
                if in_range(j):
                    for q in range(2):
                        dve.wait_ge(S("slot_gelu"), 2 * j + q + 1)
                        dve.scalar_tensor_tensor(out=slot_g[q], in0=up[2 * q + 1][:].rearrange("p k n -> p (k n)"),
                                                 scalar=HS / WS, in1=slot_g[q], op0=ALU.mult,
                                                 op1=ALU.mult).then_inc(S("slot_g"), 1)

            slot_steps(dve, slot_dve)

            def fin_sum(c):
                y, sh = fin_y[c % RING], fin_s[c % RING]
                dve.wait_ge(S(f"fin_y_in{c % RING}"), 16 * TT * (c // RING + 1))
                dve.wait_ge(S(f"fin_s_in{c % RING}"), 16 * (c // RING + 1))
                dve.tensor_tensor(sh[:], sh[:], y[:], ALU.add).then_inc(S("fin_sum"), 1)
                dve.wait_ge(S("fin_sum"), c + 1)
                n = c % 2
                for t in range(TT):
                    dve.bn_stats(stats[n][:, t, :], sh[:, t, :]).then_inc(S("fin_stats"), 1)
                dve.wait_ge(S("fin_stats"), TT * (c + 1))
                if c >= 2:
                    dve.wait_ge(S("fin_inv"), c - 1)
                for t in range(TT):
                    dve.bn_aggr(mv[n][:, t, :], stats[n][:, t, :]).then_inc(S("fin_mv"), 1)

            def fin_norm(c):
                sh, n, x = fin_s[c % RING], c % 2, fin_x[c % RING]
                dve.wait_ge(S("fin_inv"), c + 1)
                for t in range(TT):
                    dve.tensor_scalar(sh[:, t, :], sh[:, t, :], mv[n][:, t, 0:1], inv[n][:, 1, t:t + 1],
                                      ALU.subtract, ALU.mult).then_inc(S("fin_n"), 1)
                dve.wait_ge(S("fin_n"), TT * (c + 1))
                dve.wait_ge(S(f"fin_x_in{c % RING}"), 16 * (c // RING + 1))
                x = x[:] if c % RING == 0 else x
                dve.tensor_tensor(x, x, sh[:], ALU.add).then_inc(S("fin"), 1)

            fin_sum(0)
            for c in range(NC):
                if c + 1 < NC:
                    fin_sum(c + 1)
                fin_norm(c)

        @block.gpsimd
        def _(pool):
            pool.memset(ident[:], 0.0).then_inc(S("ident"), 1)
            pool.wait_ge(S("ident"), 1)
            pool.affine_select(out=ident[:], in_=ident[:], compare_op=ALU.not_equal, fill=1.0, base=0,
                               pattern=[[-1, P]], channel_multiplier=1).then_inc(S("ident"), 1)
            pool.iota(iota_e[:], [[1, E]], base=0, channel_multiplier=0,
                      allow_small_or_imprecise_dtypes=True).then_inc(S("iotas"), 1)
            pool.memset(xf[:, 0:NS // 3, :], 0.0).then_inc(S("zeros"), 1)
            pool.iota(iota_s[:], [[1, NS + 1]], base=0, channel_multiplier=0,
                      allow_small_or_imprecise_dtypes=True).then_inc(S("iotas"), 1)
            pool.memset(ones_row[:], 1.0).then_inc(S("iotas"), 1)
            pool.memset(ones[:], 1.0).then_inc(S("triangle"), 1)
            pool.memset(below[:], 1.0).then_inc(S("triangle"), 1)
            pool.wait_ge(S("triangle"), 2)
            pool.affine_select(out=below[:], in_=below[:], compare_op=ALU.is_gt, fill=0.0, base=0,
                               pattern=[[1, P]], channel_multiplier=-1).then_inc(S("triangle"), 1)
            pool.wait_ge(S("const"), 1)

            def inverse(n, c, twice=False):
                v = inv[n]
                s = S(f"inv{n}_s")
                k = (6 if twice else 1) * c
                pool.wait_ge(S(f"mv{n}"), TT * (c + 1))
                done = S(f"inv{n}")
                pool.tensor_scalar(v[:, 0, :], mv[n][:, :, 1], EPS, None, ALU.add).then_inc(s, 1)
                pool.wait_ge(s, k + 1)
                if not twice:
                    pool.tensor_tensor(v[:, 1, :], v[:, 0, :], neg_half[:], ALU.pow).then_inc(done, 1)
                    return
                pool.tensor_tensor(v[:, 1, :], v[:, 0, :], neg_half[:], ALU.pow).then_inc(s, 1)
                pool.wait_ge(s, k + 2)
                pool.tensor_tensor(v[:, 2, :], v[:, 1, :], v[:, 1, :], ALU.mult).then_inc(s, 1)
                pool.wait_ge(s, k + 3)
                pool.tensor_tensor(v[:, 3, :], v[:, 2, :], mv[n][:, :, 1], ALU.mult).then_inc(s, 1)
                pool.wait_ge(s, k + 4)
                pool.tensor_scalar(v[:, 2, :], v[:, 3, :], EPS, None, ALU.add).then_inc(s, 1)
                pool.wait_ge(s, k + 5)
                pool.tensor_tensor(v[:, 4, :], v[:, 2, :], neg_half[:], ALU.pow).then_inc(s, 1)
                pool.wait_ge(s, k + 6)
                pool.tensor_tensor(v[:, 5, :], v[:, 4, :], v[:, 1, :], ALU.mult).then_inc(done, 1)

            def difference(out, x, c, halo_done, mixes, done, norm, n_mix, all_done):
                pool.wait_ge(S(halo_done), c + 1)
                pool.wait_ge(S(norm), CT * (c + 1))
                at_least(pool, S(mixes), CT * n_mix * c)
                pool.tensor_tensor(out[:], x[:, :, 1:CH + 1], x[:, :, 0:CH], ALU.subtract).then_inc(S(done), 1)

            inverse(0, 0, True)
            for i in STEPS:
                c0, c1, c2 = i, i - 1, i - 2
                if on(c1):
                    inverse(1, c1)
                if on(c1):
                    difference(delta2, xn2T[c1 % 2], c1, "halo2", "mix2", "delta2", "xn2T", 2, None)
                if on(c2):
                    at_least(pool, S("fv_mm"), c2 + 1)
                    for f in range(FT):
                        pool.wait_ge(S("sh_hi"), FT * c2 + f + 1)
                        pool.tensor_tensor(sh_s[:, 1, f, :], gu[f % 2][:], sh_s[:, 0, f, :],
                                           ALU.subtract).then_inc(S("sh_lo"), 1)
                if on(i + 1):
                    difference(delta, xnT[(i + 1) % 2], i + 1, "halo", "mix", "delta", "xnT", 3, None)
                if on(i + 2):
                    inverse(0, i + 2, True)
                if on(c1):
                    for q in range(4):
                        pool.wait_ge(S("relu"), 4 * c1 + q + 1)
                        r = relu_k[q % 2]
                        pool.tensor_tensor(r[:], r[:], r[:], ALU.mult).then_inc(S("kf"), 1)
                        pool.wait_ge(S("kf_hi"), 4 * c1 + q + 1)
                        pool.tensor_tensor(kf_s[:, 1, 2 * q:2 * q + 2, :], r[:], kf_s[:, 0, 2 * q:2 * q + 2, :],
                                           ALU.subtract).then_inc(S("kf_lo"), 1)
                    inverse(2, c1)
                    inverse(3, c1)

            pool.wait_ge(S("routed"), 1)
            pool.wait_ge(S("zeroed"), 16 * 3)
            for t in range(NT):
                pool.indirect_dma_start(out=sorted_x, out_offset=bass.IndirectOffsetOnAxis(ap=row_of[:, t:t + 1], axis=0),
                                        in_=xf[:, t, :], in_offset=None).then_inc(S("scattered"), 16)
            pool.wait_ge(S("scattered"), 16 * NT)

            def slot_pool(j, b, h):
                if in_range(j + 1):
                    at_least_slot(pool, S("slot_t"), j)
                    pool.dma_start(slot_x[1 - b], slot_rows_x[bass.ds(j + 1, 1)]).then_inc(S(f"slot_x_in{1 - b}"), 16)
                if in_range(j):
                    for q in range(2):
                        pool.wait_ge(S("slot_h_hi"), 2 * j + q + 1)
                        h = slot_h[b][:, :, q * FT // 2:(q + 1) * FT // 2, :]
                        pool.tensor_tensor(h[:, 1], slot_g[q].rearrange("p (f n) -> p f n", n=P), h[:, 0],
                                           ALU.subtract).then_inc(S("slot_h_lo"), 1)

            slot_steps(pool, slot_pool)

            pool.wait_ge(S("slot_y_out0"), 16 * ((NS + 1) // 2))
            pool.wait_ge(S("slot_y_out1"), 16 * (NS // 2))

            def fetch(c):
                if c >= RING:
                    pool.wait_ge(S("fin_sum"), c - RING + 1)
                for t in range(TT):
                    n = TT * c + t
                    pool.indirect_dma_start(out=fin_y[c % RING][:, t, :], out_offset=None, in_=sorted_y,
                                            in_offset=bass.IndirectOffsetOnAxis(ap=row_of[:, n:n + 1], axis=0)
                                            ).then_inc(S(f"fin_y_in{c % RING}"), 16)

            for c in range(RING):
                fetch(c)
            for c in range(NC):
                n = c % 2
                pool.wait_ge(S("fin_mv"), TT * (c + 1))
                if c >= 2:
                    pool.wait_ge(S("fin_n"), TT * (c - 1))
                pool.tensor_scalar(inv[n][:, 0, :], mv[n][:, :, 1], EPS, None, ALU.add).then_inc(S("fin_eps"), 1)
                pool.wait_ge(S("fin_eps"), c + 1)
                pool.tensor_tensor(inv[n][:, 1, :], inv[n][:, 0, :], neg_half[:], ALU.pow).then_inc(S("fin_inv"), 1)
                if c + RING < NC:
                    fetch(c + RING)


_COLUMNS = {"g1": "ln1_g", "b1": "ln1_b", "g2": "ln2_g", "b2": "ln2_b", "mk": "att_mix_k", "mv": "att_mix_v",
            "mr": "att_mix_r", "fk": "ffn_mix_k", "fr": "ffn_mix_r", "decay": "time_decay", "first": "time_first"}
_TRANSPOSED = {"kT": "Wk", "vT": "Wv", "rT": "Wr", "oT": "Wo", "fkT": "Wk_ffn", "frT": "Wr_ffn", "fvT": "Wv_ffn"}


def kernel(**inputs):
    import numpy as _np
    import concourse.bacc as _bacc
    from concourse.bass_utils import run_bass_kernel_spmd as _run

    given = {"x": inputs["L0_attn_x"], "gate": inputs["L0_ffn_Wg"]}
    for short, name in _COLUMNS.items():
        given["v_" + short] = _np.asarray(inputs["L0_attn_" + name]).reshape(CT, P).T
    for short, name in _TRANSPOSED.items():
        given[short] = _np.asarray(inputs["L0_attn_" + name]).T
    for name in ("w1s", "w2s", "w3s", "W1", "W2", "W3"):
        given[name] = inputs["L0_ffn_" + name]
    nc = _bacc.Bacc("TRN2", target_bir_lowering=False, num_devices=1)
    arrays, aps = {}, {}
    for name, value in given.items():
        value = _np.ascontiguousarray(value)
        arrays[f"in_{name}"] = value
        aps[name] = nc.dram_tensor(f"in_{name}", value.shape, mybir.dt.from_np(value.dtype),
                                   kind="ExternalInput").ap()
    aps["out"] = nc.dram_tensor("out_0", (1, T, C), F32, kind="ExternalOutput").ap()
    build(nc, aps)
    r = _run(nc, [arrays], core_ids=[0])
    return r.results[0]["out_0"]
```

```python
from contextlib import ExitStack

import concourse.bass as bass
from concourse import mybir

F32 = mybir.dt.float32
F16 = mybir.dt.float16
I32 = mybir.dt.int32
U32 = mybir.dt.uint32
ALU = mybir.AluOpType
ACT = mybir.ActivationFunctionType
AX = mybir.AxisListType

P = 128
T = 4096
C = 256
CT = C // P
F = 1024
FT = F // P
E = 8
CH = 256
TT = CH // P
NC = T // CH
NS = (T + E * (P - 1)) // P
REGION = T + P
ROW = 3 * C + 4
XF, SHARED, X1, ID = 0, C, 2 * C, 3 * C
NO_TOKEN = 2 * T
EPS = 1e-5
WS = 64.0
KS = 64.0
HS = 64.0
PIECE = CT * F
BIG = -1e38
GUS = 4


def wait(eng, sem, value):
    if not isinstance(value, int) or value > 0:
        eng.wait_ge(sem, value)


def build(nc, a):
    ctx = ExitStack()
    with ctx:
        def sb(name, shape, dt=F32):
            return ctx.enter_context(nc.sbuf_tensor(name, [P] + list(shape), dt))

        def ps(name, shape):
            return ctx.enter_context(nc.psum_tensor(name, [P] + list(shape), F32))

        sems = {}

        def S(name):
            if name not in sems:
                sems[name] = ctx.enter_context(nc.semaphore(name))
            return sems[name]

        w_split = nc.dram_tensor("w_split", (E, P, 3, 2, PIECE), F16).ap()
        routed_rows = nc.dram_tensor("routed_rows", (E * REGION, ROW), F32).ap()

        small = {n: sb("w_" + n, [2, CT, C], F16) for n in ("k", "v", "r", "o", "fr")}
        w_fk = sb("w_fk", [2, CT, F], F16)
        w_fv = sb("w_fv", [2, FT, C], F16)
        w_gate = sb("w_gate", [2, CT, E], F16)
        arena = sb("arena", [14 * PIECE], F16)
        raw = [arena[:, b * 2 * PIECE:(b + 1) * 2 * PIECE].bitcast(F32) for b in range(3)]
        cut = arena[:, 6 * PIECE:8 * PIECE].rearrange("p (h n) -> p h n", h=2)
        shared_w = arena[:, 8 * PIECE:].rearrange("p (m h n) -> p m h n", m=3, h=2)
        expert_w = [arena[:, b * 6 * PIECE:(b + 1) * 6 * PIECE].rearrange("p (m h n) -> p m h n", m=3, h=2)
                    for b in range(2)]

        ident = sb("ident", [P])
        vec = sb("vec", [9, CT])
        G1, B1, G2, B2, MK, MV, MR, FK, FR = range(9)
        rec_vec = sb("rec_vec", [3, CT])
        neg_decay = sb("neg_decay", [CT, CH])
        neg_half = sb("neg_half", [TT])
        eps = sb("eps", [TT])
        iota_e = sb("iota_e", [E])
        iota_s = sb("iota_s", [NS])
        region_row = sb("region_row", [TT, E])
        below = sb("below", [P], F16)
        ones = sb("ones", [P], F16)
        zero_row = sb("zero_row", [ROW])

        tok = [TT, C]
        chan = [CT, CH]
        x_in = sb("x_in", tok)
        x_res = sb("x_res", tok)
        xa = [sb(f"xa{b}", tok) for b in range(2)]
        normed = sb("normed", tok)
        normed2 = sb("normed2", tok)
        xnT = [sb(f"xnT{b}", [CT, CH + 1]) for b in range(2)]
        xn2T = [sb(f"xn2T{b}", [CT, CH + 1]) for b in range(2)]
        delta = sb("delta", chan)
        delta2 = sb("delta2", chan)
        mixed = [sb(f"mixed{m}", chan) for m in range(3)]
        mix_s = [sb(f"mix_s{m}", [2] + chan, F16) for m in range(3)]
        mix2_s = [sb(f"mix2_s{m}", [2] + chan, F16) for m in range(2)]
        key = sb("key", chan)
        val = sb("val", chan)
        er = sb("er", chan)
        top = sb("top", [CT, CH + 1])
        aa = sb("aa", [CT, CH + 1])
        bb = sb("bb", [CT, CH + 1])
        dist = sb("dist", chan)
        ex = sb("ex", [4, CT, CH])
        rw_s = sb("rw_s", [2] + chan, F16)
        x2 = sb("x2", tok)
        gate_r = sb("gate_r", tok)
        relu_k = [sb(f"relu_k{b}", chan) for b in range(2)]
        mixed2 = relu_k
        kf_s = sb("kf_s", [2, FT, CH], F16)
        sh_s = sb("sh_s", [2, FT, CH], F16)
        rows = [sb(f"rows{b}", [TT, ROW]) for b in range(2)]
        xf_s = sb("xf_s", [2] + chan, F16)
        gu = [sb(f"gu{b}", [CH]) for b in range(GUS)]
        stats = [sb(f"stats{n}", [TT, 6]) for n in range(4)]
        mv = [sb(f"mv{n}", [TT, 2]) for n in range(4)]
        inv = [sb(f"inv{n}", [6, TT]) for n in range(4)]
        logit = sb("logit", [TT, E])
        best = sb("best", [TT, 8])
        best_at = sb("best_at", [TT, 8], U32)
        best_f = sb("best_f", [TT])
        onehot = sb("onehot", [TT, E], F16)
        next_row = sb("next_row", [TT, E])
        place = sb("place", [TT, E])
        row_f = sb("row_f", [TT])
        row_of = [sb(f"row_of{b}", [TT], U32) for b in range(2)]
        hold_dve = sb("hold_dve", [1])
        hold_pool = sb("hold_pool", [1])

        expert_row = sb("expert_row", [4, E])
        expert_int = sb("expert_int", [2, E], I32)
        zero_at = sb("zero_at", [E], I32)
        ones_row = sb("ones_row", [E])
        slot_f = sb("slot_f", [3, NS])
        slot_expert = sb("slot_expert", [NS], I32)
        slot_row = sb("slot_row", [NS], I32)

        slot_x = [normed[:, 0, :], normed2[:, 0, :]]
        slot_rest = [rows[b][:, 1, SHARED:] for b in range(2)]
        slot_xs = [mix_s[b][:, :, :, 0:P] for b in range(2)]
        slot_g = [ex[:, b].rearrange("p k n -> p (k n)") for b in range(2)]
        slot_h = [kf_s[:, :, :, b * P:(b + 1) * P] for b in range(2)]
        slot_sum = [xa[b][:, 0, :] for b in range(2)]
        slot_out = [xa[b][:, 1, :] for b in range(2)]
        slot_id = [row_of[b][:, 0:1] for b in range(2)]

        tp = [ps(f"tp{b}", [CT, CH]) for b in range(2)]
        up = [ps(f"up{b}", [2, CH]) for b in range(4)]
        yp = [ps(f"yp{b}", tok) for b in range(2)]

        x_tok = a["x"].rearrange("o (c t p) d -> (o c) p t d", c=NC, p=P)
        out_rows = a["out"].rearrange("o t d -> (o t) d")

        def tiles(w):
            return w.rearrange("(k p) n -> p k n", p=P)

        def flat(w):
            return w[:, :, :, :].rearrange("p h k n -> p h (k n)")

        pieces = [(tiles(a[n]), CT, C, flat(small[w]))
                  for n, w in (("kT", "k"), ("vT", "v"), ("rT", "r"), ("oT", "o"), ("frT", "fr"))]
        pieces.append((tiles(a["gate"]), CT, E, flat(w_gate)))
        pieces.append((tiles(a["fkT"]), CT, F, flat(w_fk)))
        pieces.append((tiles(a["fvT"]), FT, C, flat(w_fv)))
        for m, n in enumerate(("w1s", "w2s", "w3s")):
            pieces.append((tiles(a[n]), (CT, CT, FT)[m], (F, F, C)[m], shared_w[:, m]))
        N_OWN = len(pieces)
        NEEDS_KVR, NEEDS_ATT, NEEDS_FFN = 3, 4, 8
        OWN_AT = {-2: (0, 3), -1: (3, 5), 0: (5, 8), 1: (8, 11)}
        EXPERTS_FROM = 2

        def own_pieces(i):
            return range(*OWN_AT[i]) if isinstance(i, int) and i in OWN_AT else range(0)

        def expert_pieces(i, p, h):
            e = h - EXPERTS_FROM // 2
            if isinstance(i, int) and not 0 <= e < E:
                return []
            return [(e, m) for m in ((0, 1) if p == 0 else (2,))]

        def own_in_raw(b):
            return len(range(b, N_OWN, 3))

        def on(c):
            return not isinstance(c, int) or 0 <= c < NC

        def chunk_steps(eng, step):
            for i in range(-1, NC + 2):
                step(i, i % 2, i // 2)

        def slot_steps(eng, step):
            turns = (NS - 7) // 2
            for j in range(-1, 4):
                step(j, j % 2, j // 2)
            with eng.Fori(0, turns) as turn:
                step(2 * turn + 4, 0, turn + 2)
                step(2 * turn + 5, 1, turn + 2)
            for j in range(4 + 2 * turns, NS + 2):
                step(j, j % 2, j // 2)

        def is_slot(j):
            return not isinstance(j, int) or 0 <= j < NS

        block = ctx.enter_context(nc.Block())

        E_NOW, E_KEEP, E_OLD, E_DECAY = range(4)

        @block.sync
        def _(sp):
            def load_own(n):
                src, k, width, _ = pieces[n]
                wait(sp, S("piece_lo"), n - 2)
                wait(sp, S("piece_hi"), n - 2)
                sp.dma_start(raw[n % 3][:, 0:k * width].rearrange("p (k n) -> p k n", k=k),
                             src).then_inc(S(f"piece_in{n % 3}"), 16)

            def load_expert(e, m):
                src = tiles(a[("W1", "W2", "W3")[m]][bass.ds(e, 1)].rearrange("e k n -> (e k) n"))
                wait(sp, S("piece_lo"), N_OWN + 3 * e + (m - 2 if not isinstance(e, int) or e else 0))
                sp.dma_start(raw[m].rearrange("p (k n) -> p k n", k=(CT, CT, FT)[m]),
                             src).then_inc(S(f"piece_in{m}"), 16)

            def store_expert(e, m):
                wait(sp, S("piece_lo"), N_OWN + 3 * e + m + 1)
                sp.dma_start(w_split[bass.ds(e, 1), :, m], cut).then_inc(S("piece_out"), 16)

            sp.dma_start(x_in[:], x_tok[0]).then_inc(S("x_in"), 16)
            for n, name in enumerate(("g1", "b1", "g2", "b2", "mk", "mv", "mr", "fk", "fr")):
                sp.dma_start(vec[:, n, :], a["v_" + name]).then_inc(S("vec_in"), 16)
            sp.dma_start(rec_vec[:, 0, :], a["v_decay"]).then_inc(S("vec_in"), 16)
            sp.dma_start(rec_vec[:, 2, :], a["v_first"]).then_inc(S("vec_in"), 16)
            for n in range(3):
                load_own(n)

            def step(i, p, h):
                for n in own_pieces(i + 0):
                    load_own(n)
                todo = expert_pieces(i, p, h)
                for e, m in todo:
                    load_expert(e, m)
                if on(i - 1):
                    wait(sp, S("x1"), i - 1)
                    sp.dma_start(x_res[:], x_tok[bass.ds(i - 1, 1)]).then_inc(S("x_res"), 16)
                if on(i + 2):
                    wait(sp, S("normed"), TT * (i + 2))
                    sp.dma_start(x_in[:], x_tok[bass.ds(i + 2, 1)]).then_inc(S("x_in"), 16)
                for e, m in todo:
                    store_expert(e, m)

            chunk_steps(sp, step)

            sp.wait_ge(S("zero_at"), 1)
            sp.wait_ge(S("zero_row"), 1)
            for e in range(E):
                at = sp.value_load(zero_at[0:1, e:e + 1], min_val=0, max_val=E * REGION - P)
                sp.dma_start(routed_rows[bass.ds(at, P)], zero_row[:]).then_inc(S("zeroed"), 16)
            sp.wait_ge(S("zeroed"), 16 * E)

        def three(pe, out, stat, mov, first, last):
            pe.matmul(out, stat(0), mov(0), start=first, stop=False)
            pe.matmul(out, stat(0), mov(1), start=False, stop=False)
            return pe.matmul(out, stat(1), mov(0), start=False, stop=last)

        @block.tensor
        def _(pe):
            def transposes(bank, src, done):
                for t in range(TT):
                    for k in range(CT):
                        m = pe.transpose(bank[:, k, t * P:(t + 1) * P], src[:, t, k * P:(k + 1) * P], ident[:])
                m.then_inc(S(done), 1)

            def channel_major(bank, weights, x, done):
                for j in range(2):
                    for k in range(CT):
                        m = three(pe, bank[:, j, :], lambda s: weights(j, s, k), lambda s: x[:, s, k, :],
                                  k == 0, k == CT - 1)
                m.then_inc(S(done), 1)

            def token_major(bank, x, w, tiles, done):
                for t in range(TT):
                    for k in range(tiles):
                        m = three(pe, bank[:, t, :], lambda s: x[:, s, k, t * P:(t + 1) * P],
                                  lambda s: w(s, k), k == 0, k == tiles - 1)
                m.then_inc(S(done), 1)

            pe.wait_ge(S("ident"), 2)
            pe.wait_ge(S("triangle"), 3)

            def step(i, p, h):
                c0, c1, c2 = i, i - 1, i - 2

                def projection(m):
                    name = ("k", "v", "r")[m]
                    w = small[name]
                    wait(pe, S("mix_lo"), 3 * c0 + m + 1)
                    wait(pe, S("relu"), 4 * c1 + m - 2)
                    channel_major(up[m], lambda j, s, k: w[:, s, k, j * P:(j + 1) * P], mix_s[m], name + "_mm")

                def shared_up(f):
                    if f == 0:
                        wait(pe, S("relu"), 4 * c1 - 3 if on(c1 - 1) else 0)
                        wait(pe, S("relu"), 4 * c1 if not on(c0) else 0)
                    elif f < 4:
                        wait(pe, S(("key", "val", "er")[f - 1]), c0 + 1 if on(c0) else NC)
                    else:
                        wait(pe, S("gu"), FT * c2 + f - 3)
                    channel_major(up[(3 + f) % 4],
                                  lambda m, s, k: shared_w[:, m, s, k * F + f * P:k * F + (f + 1) * P],
                                  xf_s, "sh_up_mm")

                if on(c0):
                    if i == 0:
                        pe.wait_ge(S("piece_lo"), NEEDS_KVR)
                    projection(0)
                    projection(1)
                if on(c1):
                    if i == 1:
                        pe.wait_ge(S("piece_lo"), NEEDS_ATT)
                    wait(pe, S("rw_lo"), c1 + 1)
                    wait(pe, S("sig"), c1)
                    token_major(yp[0], rw_s, lambda s, k: small["o"][:, s, k, :], CT, "wo_mm")
                if on(c2):
                    wait(pe, S("xf"), TT * (c2 + 1))
                    wait(pe, S("placed"), c2)
                    transposes(tp[0], rows[p][:, :, XF:XF + C], "t4_mm")
                if on(c0):
                    projection(2)
                if on(c2):
                    if i == 2:
                        pe.wait_ge(S("piece_lo"), N_OWN)
                    wait(pe, S("xf_lo"), c2 + 1)
                    for t in range(TT):
                        for k in range(CT):
                            m = three(pe, tp[0][:, 0, t * E:(t + 1) * E],
                                      lambda s: xf_s[:, s, k, t * P:(t + 1) * P],
                                      lambda s: w_gate[:, s, k, :], k == 0, k == CT - 1)
                    m.then_inc(S("gate_mm"), 1)
                    for f in range(3):
                        shared_up(f)
                if on(c1):
                    wait(pe, S("normed2"), TT * (c1 + 1))
                    wait(pe, S("xnT"), CT * (c0 + 1) if on(c0) else CT * NC)
                    transposes(tp[1], normed2, "t2_mm")
                if on(c2):
                    shared_up(3)
                    wait(pe, S("onehot"), TT * (c2 + 1))
                    rank = tp[0][:, 1, 0:TT * E].rearrange("p (t e) -> p t e", t=TT)
                    total = tp[0][:, 1, TT * E:2 * TT * E].rearrange("p (t e) -> p t e", t=TT)
                    for t in range(TT):
                        for before in range(t):
                            pe.matmul(rank[:, t, :], ones[:], onehot[:, before, :], start=(before == 0), stop=False)
                        pe.matmul(rank[:, t, :], below[:], onehot[:, t, :], start=(t == 0), stop=True)
                    for t in range(TT):
                        for s in range(TT):
                            m = pe.matmul(total[:, t, :], ones[:], onehot[:, s, :], start=(s == 0), stop=(s == TT - 1))
                    m.then_inc(S("rank_mm"), 1)
                    for f in range(4, FT):
                        shared_up(f)
                if on(c1):
                    if i == 1:
                        pe.wait_ge(S("piece_lo"), NEEDS_FFN)
                    wait(pe, S("mix2_lo"), 2 * c1 + 1)
                    wait(pe, S("x2"), c1 + 1)
                    token_major(yp[0], mix2_s[1], lambda s, k: small["fr"][:, s, k, :], CT, "r2_mm")
                    for q in range(4):
                        if on(c2):
                            wait(pe, S("gu"), FT * c2 + 5 + q)
                        elif q:
                            wait(pe, S("er"), c0 + 1)
                        if q == 0:
                            wait(pe, S("mix2_lo"), 2 * (c1 + 1))
                        channel_major(up[(11 + q) % 4],
                                      lambda j, s, k: w_fk[:, s, k, (2 * q + j) * P:(2 * q + j + 1) * P],
                                      mix2_s[0], "fk_mm")
                if on(c2):
                    wait(pe, S("sh_lo"), FT * (c2 + 1))
                    wait(pe, S("x3a"), c1)
                    token_major(yp[1], sh_s, lambda s, k: shared_w[:, 2, s, k * C:(k + 1) * C], FT, "sh_dn_mm")
                if on(i + 1):
                    wait(pe, S("normed"), TT * (i + 2))
                    wait(pe, S("xn2T"), CT * c0)
                    transposes(tp[1], normed, "t0_mm")
                if on(c1):
                    wait(pe, S("kf_lo"), 4 * (c1 + 1))
                    wait(pe, S("y_sh"), c1)
                    token_major(yp[1], kf_s, lambda s, k: w_fv[:, s, k, :], FT, "fv_mm")

            chunk_steps(pe, step)

            def slot_step(j, b, h):
                if is_slot(j + 1):
                    wait(pe, S(f"slot_x_in{1 - b}"), 16 * (h + b + 1))
                    wait(pe, S("slot_x_lo"), j)
                    for k in range(CT):
                        m = pe.transpose(tp[1 - b][:, k, 0:P], slot_x[1 - b][:, k * P:(k + 1) * P], ident[:])
                    m.then_inc(S("slot_t"), 1)
                if is_slot(j):
                    wait(pe, S(f"slot_w12_{b}"), 16 * (h + 1))
                    wait(pe, S("slot_x_lo"), j + 1)
                    for q in range(2):
                        wait(pe, S("slot_g"), 2 * j + q - 1)
                        for m in range(2):
                            for g in range(FT // 2):
                                f = q * FT // 2 + g
                                for k in range(CT):
                                    mm = three(pe, up[2 * q + m][:].rearrange("p k n -> p (k n)")[:, g * P:(g + 1) * P],
                                               lambda s: expert_w[b][:, m, s, k * F + f * P:k * F + (f + 1) * P],
                                               lambda s: slot_xs[b][:, s, k, :], k == 0, k == CT - 1)
                        mm.then_inc(S("slot_up"), 1)
                if is_slot(j - 1):
                    wait(pe, S(f"slot_w3_{1 - b}"), 16 * (h + b))
                    wait(pe, S("slot_h_lo"), 2 * j)
                    wait(pe, S("slot_sum"), j - 2)
                    for f in range(FT):
                        mm = three(pe, yp[1 - b][:, 0, :], lambda s: slot_h[1 - b][:, s, f, :],
                                   lambda s: expert_w[1 - b][:, 2, s, f * C:(f + 1) * C], f == 0, f == FT - 1)
                    mm.then_inc(S("slot_dn"), 1)

            pe.wait_ge(S("placed"), NC)
            pe.wait_ge(S("y_sh"), NC)
            slot_steps(pe, slot_step)

        @block.scalar
        def _(act):
            act.wait_ge(S("vec_in"), 16 * 11)
            act.activation(rec_vec[:, 1, :], rec_vec[:, 0, :], ACT.Exp).then_inc(S("decay"), 1)

            def own_hi(n):
                _, k, width, dst = pieces[n]
                act.wait_ge(S(f"piece_in{n % 3}"), 16 * (n // 3 + 1))
                act.activation(dst[:, 0, :], raw[n % 3][:, 0:k * width], ACT.Copy,
                               scale=WS).then_inc(S("piece_hi"), 1)

            def expert_hi(e, m):
                wait(act, S(f"piece_in{m}"), 16 * (own_in_raw(m) + e + 1))
                wait(act, S("piece_out"), 16 * (3 * e + m))
                act.activation(cut[:, 0, :], raw[m], ACT.Copy, scale=WS).then_inc(S("piece_hi"), 1)

            def channel_norm(dst, bank, g, b, c, mm, done, mixes, n_mix, halo):
                wait(act, S(mm), c + 1)
                wait(act, S(mixes), n_mix * CT * (c - 1))
                wait(act, S(halo), c)
                for k in range(CT):
                    act.activation(dst[:, k, 1:CH + 1], bank[:, k, :], ACT.Identity, bias=vec[:, b, k:k + 1],
                                   scale=vec[:, g, k:k + 1]).then_inc(S(done), 1)

            for n in own_pieces(-2):
                own_hi(n)
            act.wait_ge(S("state0"), 6)

            def step(i, p, h):
                c0, c1, c2 = i, i - 1, i - 2

                def sh_hi(f):
                    wait(act, S("gu"), FT * c2 + f + 1)
                    wait(act, S("sh_dn_mm"), c2)
                    act.activation(sh_s[:, 0, f, :], gu[f % GUS][:], ACT.Copy).then_inc(S("sh_hi"), 1)

                def gelu(f):
                    wait(act, S("sh_up_mm"), FT * c2 + f + 1)
                    wait(act, S("sh_lo"), FT * c2 + f + 1 - GUS)
                    act.activation(gu[f % GUS][:], up[(3 + f) % 4][:, 0, :], ACT.Gelu,
                                   scale=1 / WS).then_inc(S("gelu"), 1)
                    if f >= 1:
                        sh_hi(f - 1)

                def kf(q):
                    n = 4 * c1 + q
                    r = relu_k[q % 2]
                    wait(act, S("fk_mm"), n + 1)
                    wait(act, S("kf_lo"), n - 1)
                    act.activation(r[:], up[(11 + q) % 4][:], ACT.Relu, scale=KS ** 0.5 / WS).then_inc(S("relu"), 1)
                    wait(act, S("relu"), n + 1)
                    act.activation(r[:], r[:], ACT.Square).then_inc(S("kf"), 1)
                    wait(act, S("kf"), n + 1)
                    wait(act, S("fv_mm"), c1)
                    act.activation(kf_s[:, 0, 2 * q:2 * q + 2, :], r[:], ACT.Copy).then_inc(S("kf_hi"), 1)

                if on(c0):
                    wait(act, S("rw_lo"), c0)
                    wait(act, S("k_mm"), c0 + 1)
                    act.activation(key[:], up[0][:], ACT.Copy, scale=1 / WS).then_inc(S("key"), 1)
                    wait(act, S("v_mm"), c0 + 1)
                    act.activation(val[:], up[1][:], ACT.Copy, scale=1 / WS).then_inc(S("val"), 1)
                if on(c2):
                    wait(act, S("t4_mm"), c2 + 1)
                    wait(act, S("sh_up_mm"), FT * c2)
                    act.activation(xf_s[:, 0], tp[0][:], ACT.Copy).then_inc(S("xf_hi"), 1)
                if on(c0):
                    wait(act, S("r_mm"), c0 + 1)
                    act.activation(er[:], up[2][:], ACT.Exp, scale=-1 / WS).then_inc(S("er"), 1)
                if on(c2):
                    for f in range(3):
                        gelu(f)
                if on(c1):
                    channel_norm(xn2T[1 - p], tp[1], G2, B2, c1, "t2_mm", "xn2T", "mix2", 2, "halo2")
                if on(c2):
                    for f in range(3, FT):
                        gelu(f)
                        if f == 5 and on(c1):
                            mix2_hi(c1)
                    sh_hi(FT - 1)
                elif on(c1):
                    mix2_hi(c1)
                if on(c0):
                    wait(act, S("dist"), c0 + 1)
                    for n, v in ((E_OLD, 2), (E_DECAY, 1)):
                        for k in range(CT):
                            act.activation(ex[:, n, k, :], dist[:, k, :], ACT.Relu,
                                           bias=rec_vec[:, v, k:k + 1]).then_inc(S("above"), 1)
                    wait(act, S("below0"), 4 * (c0 + 1))
                    act.activation(ex[:, 0:2], ex[:, 0:2], ACT.Exp).then_inc(S("exps"), 1)
                    wait(act, S("above"), 4 * (c0 + 1))
                    act.activation(ex[:, 2:4], ex[:, 2:4], ACT.Exp, scale=-1.0).then_inc(S("exps"), 1)
                if on(c1):
                    wait(act, S("r2_mm"), c1 + 1)
                    wait(act, S("x1"), c1)
                    act.activation(gate_r[:], yp[0][:], ACT.Tanh, scale=0.5 / WS).then_inc(S("sig"), 1)
                    for q in range(4):
                        kf(q)
                todo = expert_pieces(i, p, h)
                for e, m in todo[:1]:
                    expert_hi(e, m)
                for n in own_pieces(i):
                    own_hi(n)
                if on(c2):
                    wait(act, S("sh_dn_mm"), c2 + 1)
                    wait(act, S(f"scattered{p}"), 16 * TT * (h - 1))
                    act.activation(rows[p][:, :, SHARED:SHARED + C], yp[1][:], ACT.Copy,
                                   scale=1 / (WS * HS)).then_inc(S("y_sh"), 1)
                if on(i + 1):
                    channel_norm(xnT[1 - p], tp[1], G1, B1, i + 1, "t0_mm", "xnT", "mix", 3, "halo")
                    for m in range(3):
                        wait(act, S("mix"), CT * (3 * (i + 1) + m + 1))
                        wait(act, S(("k", "v", "r")[m] + "_mm"), i + 1)
                        act.activation(mix_s[m][:, 0], mixed[m][:], ACT.Copy).then_inc(S("mix_hi"), 1)
                if on(c0):
                    wait(act, S("rw"), c0 + 1)
                    wait(act, S("wo_mm"), c0)
                    act.activation(rw_s[:, 0], val[:], ACT.Copy).then_inc(S("rw_hi"), 1)
                for e, m in todo[1:]:
                    expert_hi(e, m)

            def mix2_hi(c1):
                wait(act, S("fk_mm"), 4 * c1)
                for m in (1, 0):
                    wait(act, S("mix2"), CT * (2 * c1 + 2 - m))
                    act.activation(mix2_s[m][:, 0], mixed2[m][:], ACT.Copy).then_inc(S("mix2_hi"), 1)

            chunk_steps(act, step)

            act.wait_ge(S("slot_table"), 2)
            act.wait_ge(S("piece_out"), 16 * 3 * E)
            act.wait_ge(S("sh_dn_mm"), NC)
            act.wait_ge(S("t2_mm"), NC)

            def expert_of(n):
                return act.value_load(slot_expert[0:1, bass.ds(n, 1)], min_val=0, max_val=E - 1)

            def rows_of(n):
                return bass.ds(act.value_load(slot_row[0:1, bass.ds(n, 1)], min_val=0, max_val=E * REGION - P), P)

            def load_weights(n, b, first, last, sem, used, value):
                e = expert_of(n)
                fresh = None
                if not isinstance(n, int) or n >= 2:
                    fresh = e != expert_of(n - 2)
                wait(act, S(used), value)
                act.dma_start(expert_w[b][:, first:last], w_split[bass.ds(e, 1), :, first:last],
                                     cond=fresh).then_inc(S(f"{sem}_{b}"), 16)

            def load_x(n, b):
                act.dma_start(slot_x[b], routed_rows[rows_of(n), XF:XF + C]).then_inc(S(f"slot_x_in{b}"), 16)

            def slot_step(j, b, h):
                if is_slot(j + 1):
                    load_weights(j + 1, 1 - b, 0, 2, "slot_w12", "slot_up", 2 * j)
                    wait(act, S("slot_t"), j + 2)
                    act.activation(slot_xs[1 - b][:, 0], tp[1 - b][:, :, 0:P], ACT.Copy).then_inc(S("slot_x_hi"), 1)
                if is_slot(j + 3):
                    load_x(j + 3, 1 - b)
                if is_slot(j):
                    load_weights(j, b, 2, 3, "slot_w3", "slot_dn", j - 1)
                    at = rows_of(j)
                    wait(act, S("slot_done"), j - 1)
                    act.dma_start(slot_rest[b], routed_rows[at, SHARED:]).then_inc(S(f"slot_rest_in{b}"), 16)
                    for q in range(2):
                        wait(act, S("slot_up"), 2 * j + q + 1)
                        wait(act, S("slot_h_lo"), 2 * j + q - 1)
                        act.activation(slot_g[q], up[2 * q][:].rearrange("p k n -> p (k n)"), ACT.Gelu,
                                       scale=1 / WS).then_inc(S("slot_gelu"), 1)
                        wait(act, S("slot_g"), 2 * j + q + 1)
                        wait(act, S("slot_dn"), j - 1)
                        act.activation(slot_h[b][:, 0, q * FT // 2:(q + 1) * FT // 2, :],
                                       slot_g[q].rearrange("p (f n) -> p f n", n=P),
                                       ACT.Copy).then_inc(S("slot_h_hi"), 1)

            act.wait_ge(S("zeroed"), 16 * E)
            for b in range(2):
                act.wait_ge(S(f"scattered{b}"), 16 * TT * (NC // 2))
            for n in range(2):
                load_x(n, n)
            slot_steps(act, slot_step)


        @block.vector
        def _(dve):
            def held(sem, value):
                wait(dve, sem, value)
                if not isinstance(value, int):
                    dve.memset(hold_dve[:], 0.0)

            dve.memset(neg_half[:], -0.5).then_inc(S("const"), 1)
            dve.memset(eps[:], EPS).then_inc(S("const"), 1)
            dve.memset(top[:], BIG).then_inc(S("state0"), 1)
            dve.memset(aa[:], 0.0).then_inc(S("state0"), 1)
            dve.memset(bb[:], 0.0).then_inc(S("state0"), 1)
            dve.memset(xnT[1][:], 0.0).then_inc(S("state0"), 1)
            dve.memset(xn2T[1][:], 0.0).then_inc(S("state0"), 1)
            dve.memset(neg_decay[:], 0.0).then_inc(S("state0"), 1)

            def own_lo(n):
                _, k, width, dst = pieces[n]
                dve.wait_ge(S("piece_hi"), n + 1)
                dve.scalar_tensor_tensor(out=dst[:, 1, :], in0=raw[n % 3][:, 0:k * width], scalar=WS,
                                         in1=dst[:, 0, :], op0=ALU.mult,
                                         op1=ALU.subtract).then_inc(S("piece_lo"), 1)

            def expert_lo(e, m):
                wait(dve, S("piece_hi"), N_OWN + 3 * e + m + 1)
                dve.scalar_tensor_tensor(out=cut[:, 1, :], in0=raw[m], scalar=WS, in1=cut[:, 0, :], op0=ALU.mult,
                                         op1=ALU.subtract).then_inc(S("piece_lo"), 1)

            def moments(n, src, c):
                for t in range(TT):
                    dve.bn_stats(stats[n][:, t, :], src[:, t, :]).then_inc(S(f"stats{n}"), 1)
                held(S(f"stats{n}"), TT * (c + 1))
                for t in range(TT):
                    dve.bn_aggr(mv[n][:, t, :], stats[n][:, t, :]).then_inc(S(f"mv{n}"), 1)

            def normalized(dst, src, n, factor, done):
                for t in range(TT):
                    dve.tensor_scalar(dst[:, t, :], src[:, t, :], mv[n][:, t, 0:1], inv[n][:, factor, t:t + 1],
                                      ALU.subtract, ALU.mult).then_inc(S(done), 1)

            def ln0_moments(c):
                wait(dve, S("x_in"), 16 * (c + 1))
                moments(0, x_in, c)

            def ln0(c, b):
                wait(dve, S("inv0"), c + 1)
                normalized(xa[b], x_in, 0, 1, "xa")
                wait(dve, S("t0_mm"), c)
                normalized(normed, x_in, 0, 5, "normed")

            def halo(buf, c, b, done, norm):
                wait(dve, S(norm), CT * (c + 1))
                last = 0 if isinstance(c, int) and c == 0 else CH
                dve.tensor_copy(buf[b][:, :, 0:1], buf[1 - b][:, :, last:last + 1]).then_inc(S(done), 1)

            def mix0(c, b):
                x = xnT[b]
                halo(xnT, c, b, "halo", "xnT")
                wait(dve, S("delta"), c + 1)
                for m in range(3):
                    for k in range(CT):
                        dve.scalar_tensor_tensor(out=mixed[m][:, k, :], in0=delta[:, k, :],
                                                 scalar=vec[:, MK + m, k:k + 1], in1=x[:, k, 0:CH],
                                                 op0=ALU.mult, op1=ALU.add).then_inc(S("mix"), 1)
                    if m:
                        mix_lo(c, m - 1)
                mix_lo(c, 2)

            def mix_lo(c, m):
                wait(dve, S("mix_hi"), 3 * c + m + 1)
                dve.tensor_tensor(mix_s[m][:, 1], mixed[m][:], mix_s[m][:, 0],
                                  ALU.subtract).then_inc(S("mix_lo"), 1)

            def mix2(c, b):
                x = xn2T[b]
                halo(xn2T, c, b, "halo2", "xn2T")
                wait(dve, S("delta2"), c + 1)
                wait(dve, S("kf_lo"), 4 * c)
                for m in (1, 0):
                    for k in range(CT):
                        dve.scalar_tensor_tensor(out=mixed2[m][:, k, :], in0=delta2[:, k, :],
                                                 scalar=vec[:, FK + m, k:k + 1], in1=x[:, k, 0:CH],
                                                 op0=ALU.mult, op1=ALU.add).then_inc(S("mix2"), 1)

            def mix2_lo(c):
                for m in (1, 0):
                    wait(dve, S("mix2_hi"), 2 * c + 2 - m)
                    dve.tensor_tensor(mix2_s[m][:, 1], mixed2[m][:], mix2_s[m][:, 0],
                                      ALU.subtract).then_inc(S("mix2_lo"), 1)

            def carry_and_top(c):
                for st in (top, aa, bb):
                    dve.tensor_copy(st[:, :, 0:1], st[:, :, CH:CH + 1]).then_inc(S("carry"), 1)
                wait(dve, S("key"), c + 1)
                wait(dve, S("carry"), 3 * (c + 1))
                for k in range(CT):
                    dve.tensor_tensor_scan(out=top[:, k, 1:CH + 1], data0=neg_decay[:, k, :], data1=key[:, k, :],
                                           initial=top[:, k, 0:1], op0=ALU.add, op1=ALU.max).then_inc(S("top"), 1)

            def distances(c):
                wait(dve, S("top"), CT * (c + 1))
                dve.tensor_tensor(dist[:], key[:], top[:, :, 0:CH], ALU.subtract).then_inc(S("dist"), 1)
                wait(dve, S("dist"), c + 1)
                for n, v in ((E_NOW, 2), (E_KEEP, 1)):
                    for k in range(CT):
                        dve.tensor_scalar(ex[:, n, k, :], dist[:, k, :], rec_vec[:, v, k:k + 1], 0.0,
                                          ALU.add, ALU.min).then_inc(S("below0"), 1)

            def recurrence(c):
                wait(dve, S("exps"), 2 * (c + 1))
                wait(dve, S("val"), c + 1)
                dve.tensor_tensor(dist[:], ex[:, E_KEEP], val[:], ALU.mult).then_inc(S("kept"), 1)
                for k in range(CT):
                    dve.tensor_tensor_scan(out=bb[:, k, 1:CH + 1], data0=ex[:, E_DECAY, k, :],
                                           data1=ex[:, E_KEEP, k, :], initial=bb[:, k, 0:1], op0=ALU.mult,
                                           op1=ALU.add).then_inc(S("bb"), 1)
                wait(dve, S("kept"), c + 1)
                for k in range(CT):
                    dve.tensor_tensor_scan(out=aa[:, k, 1:CH + 1], data0=ex[:, E_DECAY, k, :],
                                           data1=dist[:, k, :], initial=aa[:, k, 0:1], op0=ALU.mult,
                                           op1=ALU.add).then_inc(S("aa"), 1)
                dve.tensor_tensor(val[:], ex[:, E_NOW], val[:], ALU.mult).then_inc(S("now"), 1)
                wait(dve, S("aa"), CT * (c + 1))
                dve.tensor_tensor(dist[:], ex[:, E_OLD], aa[:, :, 0:CH], ALU.mult).then_inc(S("old"), 1)
                wait(dve, S("bb"), CT * (c + 1))
                dve.tensor_tensor(ex[:, E_OLD], ex[:, E_OLD], bb[:, :, 0:CH], ALU.mult).then_inc(S("old_den"), 1)
                wait(dve, S("old"), c + 1)
                wait(dve, S("now"), c + 1)
                dve.tensor_tensor(val[:], val[:], dist[:], ALU.add).then_inc(S("num"), 1)
                wait(dve, S("old_den"), c + 1)
                dve.tensor_tensor(ex[:, E_NOW], ex[:, E_OLD], ex[:, E_NOW], ALU.add).then_inc(S("den"), 1)
                wait(dve, S("den"), c + 1)
                wait(dve, S("er"), c + 1)
                dve.scalar_tensor_tensor(out=er[:], in0=er[:], scalar=1.0, in1=ex[:, E_NOW], op0=ALU.add,
                                         op1=ALU.mult).then_inc(S("den_sig"), 1)
                wait(dve, S("den_sig"), c + 1)
                dve.reciprocal(er[:], er[:]).then_inc(S("rec"), 1)
                wait(dve, S("rec"), c + 1)
                wait(dve, S("num"), c + 1)
                dve.tensor_tensor(val[:], val[:], er[:], ALU.mult).then_inc(S("rw"), 1)

            def rw_lo(c):
                wait(dve, S("rw_hi"), c + 1)
                dve.tensor_tensor(rw_s[:, 1], val[:], rw_s[:, 0], ALU.subtract).then_inc(S("rw_lo"), 1)

            def ln2_moments(c, b):
                wait(dve, S("wo_mm"), c + 1)
                dve.scalar_tensor_tensor(out=x2[:], in0=yp[0][:], scalar=1 / WS, in1=xa[b][:], op0=ALU.mult,
                                         op1=ALU.add).then_inc(S("x2"), 1)
                wait(dve, S("x2"), c + 1)
                moments(1, x2, c)

            def ln2(c):
                wait(dve, S("inv1"), c + 1)
                wait(dve, S("t2_mm"), c)
                normalized(normed2, x2, 1, 1, "normed2")

            def last_norms(c, b, h):
                wait(dve, S("sig"), c + 1)
                wait(dve, S("fv_mm"), c + 1)
                dve.scalar_tensor_tensor(out=gate_r[:], in0=gate_r[:], scalar=1.0, in1=yp[1][:],
                                         op0=ALU.add, op1=ALU.mult).then_inc(S("x3a"), 1)
                wait(dve, S("x3a"), c + 1)
                dve.scalar_tensor_tensor(out=gate_r[:], in0=gate_r[:], scalar=0.5 / (WS * KS), in1=x2[:],
                                         op0=ALU.mult, op1=ALU.add).then_inc(S("x3"), 1)
                wait(dve, S("x3"), c + 1)
                moments(2, gate_r, c)
                wait(dve, S("inv2"), c + 1)
                normalized(gate_r, gate_r, 2, 1, "x3n")
                wait(dve, S("x3n"), TT * (c + 1))
                wait(dve, S("x_res"), 16 * (c + 1))
                wait(dve, S(f"scattered{b}"), 16 * TT * h)
                x1 = rows[b][:, :, X1:X1 + C]
                dve.tensor_tensor(x1, gate_r[:], x_res[:], ALU.add).then_inc(S("x1"), 1)
                wait(dve, S("x1"), c + 1)
                moments(3, x1, c)
                if not isinstance(c, int) or c >= 2:
                    dve.tensor_scalar(rows[b][:, :, ID:ID + 1], rows[b][:, :, ID:ID + 1], float(2 * CH), None,
                                      ALU.add).then_inc(S("ids"), 1)
                wait(dve, S("inv3"), c + 1)
                normalized(rows[b][:, :, XF:XF + C], x1, 3, 1, "xf")

            def gate(c):
                wait(dve, S("gate_mm"), c + 1)
                dve.tensor_copy(logit[:], tp[0][:, 0, 0:TT * E]).then_inc(S("logit"), 1)
                held(S("logit"), c + 1)
                for t in range(TT):
                    dve.max(best[:, t, :], logit[:, t, :]).then_inc(S("best"), 1)
                held(S("best"), TT * (c + 1))
                for t in range(TT):
                    dve.max_index(best_at[:, t, :], best[:, t, :], logit[:, t, :]).then_inc(S("best_at"), 1)
                wait(dve, S("best_at"), TT * (c + 1))
                dve.tensor_copy(best_f[:], best_at[:, :, 0]).then_inc(S("best_f"), 1)
                wait(dve, S("best_f"), c + 1)
                for t in range(TT):
                    dve.tensor_scalar(onehot[:, t, :], iota_e[:], best_f[:, t:t + 1], None,
                                      ALU.is_equal).then_inc(S("onehot"), 1)

            def placing(c, b, h):
                flat_rank = tp[0][:, 1, 0:TT * E].rearrange("p (t e) -> p t e", t=TT)
                total = tp[0][:, 1, TT * E:2 * TT * E].rearrange("p (t e) -> p t e", t=TT)
                wait(dve, S("rank_mm"), c + 1)
                wait(dve, S("next_row"), c)
                dve.tensor_tensor(place[:], flat_rank, next_row[:], ALU.add).then_inc(S("place"), 1)
                dve.tensor_tensor(next_row[:], total, next_row[:], ALU.add).then_inc(S("next_row"), 1)
                wait(dve, S("place"), 2 * c + 1)
                dve.tensor_tensor(place[:], place[:], onehot[:], ALU.mult).then_inc(S("place"), 1)
                wait(dve, S("place"), 2 * c + 2)
                dve.tensor_reduce(row_f[:], place[:], AX.X, ALU.add).then_inc(S("row_f"), 1)
                wait(dve, S("row_f"), c + 1)
                wait(dve, S(f"scattered{b}"), 16 * TT * h)
                dve.tensor_copy(row_of[b][:], row_f[:]).then_inc(S("placed"), 1)

            dve.wait_ge(S("decay"), 1)
            dve.wait_ge(S("state0"), 6)
            for k in range(CT):
                dve.tensor_scalar(neg_decay[:, k, :], neg_decay[:, k, :], rec_vec[:, 1, k:k + 1], None,
                                  ALU.subtract).then_inc(S("neg_decay"), 1)
            ln0_moments(0)
            ln0(0, 0)
            for n in own_pieces(-2):
                own_lo(n)
            dve.wait_ge(S("iotas"), 4)
            dve.wait_ge(S("neg_decay"), CT)
            dve.tensor_copy(next_row[:], region_row[:]).then_inc(S("first_rows"), 1)
            dve.wait_ge(S("first_rows"), 1)

            def step(i, p, h):
                c0, c1, c2 = i, i - 1, i - 2
                todo = expert_pieces(i, p, h)
                if on(c2):
                    last_norms(c2, p, h - 1)
                if on(c1):
                    ln2_moments(c1, 1 - p)
                if on(c2):
                    wait(dve, S("xf_hi"), c2 + 1)
                    dve.tensor_tensor(xf_s[:, 1], tp[0][:], xf_s[:, 0], ALU.subtract).then_inc(S("xf_lo"), 1)
                if on(c1):
                    ln2(c1)
                if on(c0):
                    carry_and_top(c0)

                def shared(f):
                    if on(c2):
                        wait(dve, S("gelu"), FT * c2 + f + 1)
                        dve.scalar_tensor_tensor(out=gu[f % GUS][:], in0=up[(3 + f) % 4][:, 1, :], scalar=HS / WS,
                                                 in1=gu[f % GUS][:], op0=ALU.mult, op1=ALU.mult).then_inc(S("gu"), 1)

                if on(c2):
                    gate(c2)
                shared(0)
                if on(c0):
                    distances(c0)
                shared(1)
                if on(i + 1) and i >= 0 if isinstance(i, int) else True:
                    ln0_moments(i + 1)
                shared(2)
                if on(i + 1) and i >= 0 if isinstance(i, int) else True:
                    ln0(i + 1, 1 - p)
                shared(3)
                if on(c1):
                    mix2(c1, 1 - p)
                shared(4)
                if on(c2):
                    placing(c2, p, h - 1)
                shared(5)
                if on(c1):
                    mix2_lo(c1)
                shared(6)
                shared(7)
                if on(c0):
                    recurrence(c0)
                for e, m in todo[:1]:
                    expert_lo(e, m)
                for n in own_pieces(i):
                    own_lo(n)
                if on(i + 1):
                    mix0(i + 1, 1 - p)
                if on(c0):
                    rw_lo(c0)
                for e, m in todo[1:]:
                    expert_lo(e, m)

            chunk_steps(dve, step)

            route = S("route")
            count = [0]

            def then(ins):
                count[0] += 1
                ins.then_inc(route, 1)

            def before():
                dve.wait_ge(route, count[0])

            SLOTS, ENDS, GAP, TOKENS = range(4)
            EXPERT, FIRST, SCRATCH = range(3)
            dve.wait_ge(S("next_row"), NC)
            dve.tensor_copy(zero_at[:], next_row[:, 0, :]).then_inc(S("zero_at"), 1)
            then(dve.tensor_tensor(expert_row[:, TOKENS, :], next_row[:, 0, :], region_row[:, 0, :], ALU.subtract))
            before()
            then(dve.tensor_scalar(expert_row[:, TOKENS, :], expert_row[:, TOKENS, :], float(P - 1), None, ALU.add))
            before()
            then(dve.tensor_copy(expert_int[:, 0, :], expert_row[:, TOKENS, :]))
            before()
            then(dve.tensor_scalar(expert_int[:, 1, :], expert_int[:, 0, :], P.bit_length() - 1, None,
                                   ALU.arith_shift_right))
            before()
            then(dve.tensor_copy(expert_row[:, SLOTS, :], expert_int[:, 1, :]))
            before()
            then(dve.tensor_tensor_scan(out=expert_row[:, ENDS, :], data0=ones_row[:],
                                        data1=expert_row[:, SLOTS, :], initial=0.0, op0=ALU.mult, op1=ALU.add))
            then(dve.tensor_scalar(expert_row[:, GAP, :], expert_row[:, SLOTS, :], float(-P), float(REGION),
                                   ALU.mult, ALU.add))
            then(dve.tensor_scalar(slot_f[:, FIRST, :], iota_s[:], float(P), None, ALU.mult))
            then(dve.tensor_scalar(slot_f[:, EXPERT, :], iota_s[:], 0.0, None, ALU.mult))
            for e in range(E - 1):
                before()
                then(dve.scalar_tensor_tensor(out=slot_f[:, EXPERT, :], in0=iota_s[:],
                                              scalar=expert_row[:, ENDS, e:e + 1], in1=slot_f[:, EXPERT, :],
                                              op0=ALU.is_ge, op1=ALU.add))
                then(dve.tensor_scalar(slot_f[:, SCRATCH, :], iota_s[:], expert_row[:, ENDS, e:e + 1],
                                       expert_row[:, GAP, e:e + 1], ALU.is_ge, ALU.mult))
                before()
                then(dve.tensor_tensor(slot_f[:, FIRST, :], slot_f[:, FIRST, :], slot_f[:, SCRATCH, :], ALU.add))
            before()
            then(dve.tensor_scalar(slot_f[:, SCRATCH, :], slot_f[:, FIRST, :], next_row[:, 0, E - 1:E], None,
                                   ALU.subtract))
            before()
            then(dve.scalar_tensor_tensor(out=slot_f[:, SCRATCH, :], in0=iota_s[:],
                                          scalar=expert_row[:, ENDS, E - 1:E], in1=slot_f[:, SCRATCH, :],
                                          op0=ALU.is_ge, op1=ALU.mult))
            before()
            then(dve.tensor_tensor(slot_f[:, FIRST, :], slot_f[:, FIRST, :], slot_f[:, SCRATCH, :], ALU.subtract))
            before()
            dve.tensor_copy(slot_expert[:], slot_f[:, EXPERT, :]).then_inc(S("slot_table"), 1)
            dve.tensor_copy(slot_row[:], slot_f[:, FIRST, :]).then_inc(S("slot_table"), 1)

            def slot_step(j, b, h):
                if is_slot(j - 2):
                    n = j - 2
                    wait(dve, S("slot_inv"), n + 1)
                    wait(dve, S(f"slot_stored{b}"), 16 * (h - 1))
                    dve.tensor_scalar(slot_sum[b], slot_sum[b], mv[b][:, 0, 0:1], inv[b][:, 1, 0:1],
                                      ALU.subtract, ALU.mult).then_inc(S("slot_norm"), 1)
                    wait(dve, S("slot_norm"), n + 1)
                    dve.tensor_tensor(slot_out[b], slot_sum[b], slot_rest[b][:, X1 - SHARED:X1 - SHARED + C],
                                      ALU.add).then_inc(S("slot_out"), 1)
                    dve.tensor_scalar(slot_id[b], slot_rest[b][:, ID - SHARED:ID - SHARED + 1], float(NO_TOKEN), None,
                                      ALU.add).then_inc(S("slot_done"), 1)
                if is_slot(j + 1):
                    wait(dve, S("slot_x_hi"), j + 2)
                    dve.tensor_tensor(slot_xs[1 - b][:, 1], tp[1 - b][:, :, 0:P], slot_xs[1 - b][:, 0],
                                      ALU.subtract).then_inc(S("slot_x_lo"), 1)
                if is_slot(j):
                    for q in range(2):
                        wait(dve, S("slot_gelu"), 2 * j + q + 1)
                        dve.scalar_tensor_tensor(out=slot_g[q], in0=up[2 * q + 1][:].rearrange("p k n -> p (k n)"),
                                                 scalar=HS / WS, in1=slot_g[q], op0=ALU.mult,
                                                 op1=ALU.mult).then_inc(S("slot_g"), 1)
                if is_slot(j - 1):
                    n, o = j - 1, 1 - b
                    wait(dve, S("slot_dn"), n + 1)
                    wait(dve, S(f"slot_rest_in{o}"), 16 * (h + b))
                    dve.scalar_tensor_tensor(out=slot_sum[o], in0=yp[o][:, 0, :], scalar=1 / (WS * HS),
                                             in1=slot_rest[o][:, 0:C], op0=ALU.mult,
                                             op1=ALU.add).then_inc(S("slot_sum"), 1)
                    wait(dve, S("slot_sum"), n + 1)
                    dve.bn_stats(stats[o][:, 0, :], slot_sum[o]).then_inc(S("slot_stats"), 1)
                    held(S("slot_stats"), n + 1)
                    dve.bn_aggr(mv[o][:, 0, :], stats[o][:, 0, :]).then_inc(S("slot_mv"), 1)

            slot_steps(dve, slot_step)

        @block.gpsimd
        def _(pool):
            def held(sem, value):
                wait(pool, sem, value)
                if not isinstance(value, int):
                    pool.tensor_tensor(hold_pool[:], eps[:, 0:1], eps[:, 1:2], ALU.add)

            pool.memset(ident[:], 0.0).then_inc(S("ident"), 1)
            pool.wait_ge(S("ident"), 1)
            pool.affine_select(out=ident[:], in_=ident[:], compare_op=ALU.not_equal, fill=1.0, base=0,
                               pattern=[[-1, P]], channel_multiplier=1).then_inc(S("ident"), 1)
            pool.wait_ge(S("const"), 2)

            def inverse(n, c, twice=False):
                v = inv[n]
                s = S(f"inv{n}_s")
                k = (6 if twice else 1) * c
                wait(pool, S(f"mv{n}"), TT * (c + 1))
                done = S(f"inv{n}")
                pool.tensor_tensor(v[:, 0, :], mv[n][:, :, 1], eps[:], ALU.add).then_inc(s, 1)
                wait(pool, s, k + 1)
                if not twice:
                    pool.tensor_tensor(v[:, 1, :], v[:, 0, :], neg_half[:], ALU.pow).then_inc(done, 1)
                    return
                pool.tensor_tensor(v[:, 1, :], v[:, 0, :], neg_half[:], ALU.pow).then_inc(s, 1)
                wait(pool, s, k + 2)
                pool.tensor_tensor(v[:, 2, :], v[:, 1, :], v[:, 1, :], ALU.mult).then_inc(s, 1)
                wait(pool, s, k + 3)
                pool.tensor_tensor(v[:, 3, :], v[:, 2, :], mv[n][:, :, 1], ALU.mult).then_inc(s, 1)
                wait(pool, s, k + 4)
                pool.tensor_tensor(v[:, 2, :], v[:, 3, :], eps[:], ALU.add).then_inc(s, 1)
                wait(pool, s, k + 5)
                pool.tensor_tensor(v[:, 4, :], v[:, 2, :], neg_half[:], ALU.pow).then_inc(s, 1)
                wait(pool, s, k + 6)
                pool.tensor_tensor(v[:, 5, :], v[:, 4, :], v[:, 1, :], ALU.mult).then_inc(done, 1)

            def difference(out, x, c, halo_done, mixes, n_mix, norm, done):
                wait(pool, S(halo_done), c + 1)
                wait(pool, S(norm), CT * (c + 1))
                wait(pool, S(mixes), CT * n_mix * c)
                pool.tensor_tensor(out[:], x[:, :, 1:CH + 1], x[:, :, 0:CH], ALU.subtract).then_inc(S(done), 1)

            inverse(0, 0, True)
            small_ints = dict(allow_small_or_imprecise_dtypes=True)
            pool.iota(iota_e[:], [[1, E]], base=0, channel_multiplier=0, **small_ints).then_inc(S("iotas"), 1)
            pool.iota(iota_s[:], [[1, NS]], base=0, channel_multiplier=0, **small_ints).then_inc(S("iotas"), 1)
            pool.iota(region_row[:], [[0, TT], [REGION, E]], base=0, channel_multiplier=0,
                      **small_ints).then_inc(S("iotas"), 1)
            pool.memset(ones_row[:], 1.0).then_inc(S("iotas"), 1)
            for b in range(2):
                pool.memset(rows[b][:, :, ID:ROW], 0.0).then_inc(S("rows0"), 1)
            pool.wait_ge(S("rows0"), 2)
            for b in range(2):
                pool.iota(rows[b][:, :, ID:ID + 1], [[P, TT], [0, 1]], base=b * CH - NO_TOKEN, channel_multiplier=1,
                          **small_ints).then_inc(S("rows0"), 1)
            pool.memset(zero_row[:], 0.0).then_inc(S("zero_row"), 1)
            pool.memset(ones[:], 1.0).then_inc(S("triangle"), 1)
            pool.memset(below[:], 1.0).then_inc(S("triangle"), 1)
            pool.wait_ge(S("triangle"), 2)
            pool.affine_select(out=below[:], in_=below[:], compare_op=ALU.is_gt, fill=0.0, base=0,
                               pattern=[[1, P]], channel_multiplier=-1).then_inc(S("triangle"), 1)
            pool.wait_ge(S("rows0"), 4)

            def step(i, p, h):
                c0, c1, c2 = i, i - 1, i - 2

                def sh_lo(f):
                    wait(pool, S("sh_hi"), FT * c2 + f + 1)
                    pool.tensor_tensor(sh_s[:, 1, f, :], gu[f % GUS][:], sh_s[:, 0, f, :],
                                       ALU.subtract).then_inc(S("sh_lo"), 1)

                if on(c2):
                    inverse(2, c2)
                    inverse(3, c2)
                if on(c1):
                    inverse(1, c1)
                if on(c2):
                    sh_lo(0)
                    sh_lo(1)
                if (on(i + 1) and i >= 0) if isinstance(i, int) else True:
                    inverse(0, i + 1, True)
                if on(c1):
                    difference(delta2, xn2T[1 - p], c1, "halo2", "mix2", 2, "xn2T", "delta2")
                if on(c2):
                    for f in range(2, FT):
                        sh_lo(f)
                if on(c1):
                    for q in range(4):
                        wait(pool, S("kf_hi"), 4 * c1 + q + 1)
                        pool.tensor_tensor(kf_s[:, 1, 2 * q:2 * q + 2, :], relu_k[q % 2][:],
                                           kf_s[:, 0, 2 * q:2 * q + 2, :], ALU.subtract).then_inc(S("kf_lo"), 1)
                if on(i + 1):
                    difference(delta, xnT[1 - p], i + 1, "halo", "mix", 3, "xnT", "delta")
                if on(c2):
                    wait(pool, S("placed"), c2 + 1)
                    wait(pool, S("xf"), TT * (c2 + 1))
                    held(S("y_sh"), c2 + 1)
                    for t in range(TT):
                        pool.indirect_dma_start(
                            out=routed_rows, out_offset=bass.IndirectOffsetOnAxis(ap=row_of[p][:, t:t + 1], axis=0),
                            in_=rows[p][:, t, :], in_offset=None).then_inc(S(f"scattered{p}"), 16)

            chunk_steps(pool, step)

            def slot_step(j, b, h):
                if is_slot(j - 2):
                    n = j - 2
                    wait(pool, S("slot_mv"), n + 1)
                    pool.tensor_tensor(inv[b][:, 0, 0:1], mv[b][:, 0, 1:2], eps[:, 0:1],
                                       ALU.add).then_inc(S("slot_eps"), 1)
                    wait(pool, S("slot_eps"), n + 1)
                    pool.tensor_tensor(inv[b][:, 1, 0:1], inv[b][:, 0, 0:1], neg_half[:, 0:1],
                                       ALU.pow).then_inc(S("slot_inv"), 1)
                    wait(pool, S("slot_out"), n + 1)
                    held(S("slot_done"), n + 1)
                    pool.indirect_dma_start(
                        out=out_rows, out_offset=bass.IndirectOffsetOnAxis(ap=slot_id[b], axis=0),
                        in_=slot_out[b], in_offset=None, bounds_check=T - 1,
                        oob_is_err=False).then_inc(S(f"slot_stored{b}"), 16)
                if is_slot(j):
                    for q in range(2):
                        wait(pool, S("slot_h_hi"), 2 * j + q + 1)
                        hs = slot_h[b][:, :, q * FT // 2:(q + 1) * FT // 2, :]
                        pool.tensor_tensor(hs[:, 1], slot_g[q].rearrange("p (f n) -> p f n", n=P), hs[:, 0],
                                           ALU.subtract).then_inc(S("slot_h_lo"), 1)

            slot_steps(pool, slot_step)
            for b in range(2):
                pool.wait_ge(S(f"slot_stored{b}"), 16 * len(range(b, NS, 2)))


_COLUMNS = {"g1": "ln1_g", "b1": "ln1_b", "g2": "ln2_g", "b2": "ln2_b", "mk": "att_mix_k", "mv": "att_mix_v",
            "mr": "att_mix_r", "fk": "ffn_mix_k", "fr": "ffn_mix_r", "decay": "time_decay", "first": "time_first"}
_TRANSPOSED = {"kT": "Wk", "vT": "Wv", "rT": "Wr", "oT": "Wo", "fkT": "Wk_ffn", "frT": "Wr_ffn", "fvT": "Wv_ffn"}


def kernel(**inputs):
    import numpy as _np
    import concourse.bacc as _bacc
    from concourse.bass_utils import run_bass_kernel_spmd as _run

    given = {"x": inputs["L0_attn_x"], "gate": inputs["L0_ffn_Wg"]}
    for short, name in _COLUMNS.items():
        given["v_" + short] = _np.asarray(inputs["L0_attn_" + name]).reshape(CT, P).T
    for short, name in _TRANSPOSED.items():
        given[short] = _np.asarray(inputs["L0_attn_" + name]).T
    for name in ("w1s", "w2s", "w3s", "W1", "W2", "W3"):
        given[name] = inputs["L0_ffn_" + name]
    nc = _bacc.Bacc("TRN2", target_bir_lowering=False, num_devices=1)
    arrays, aps = {}, {}
    for name, value in given.items():
        value = _np.ascontiguousarray(value)
        arrays[f"in_{name}"] = value
        aps[name] = nc.dram_tensor(f"in_{name}", value.shape, mybir.dt.from_np(value.dtype),
                                   kind="ExternalInput").ap()
    aps["out"] = nc.dram_tensor("out_0", (1, T, C), F32, kind="ExternalOutput").ap()
    build(nc, aps)
    r = _run(nc, [arrays], core_ids=[0])
    return r.results[0]["out_0"]
```

```python
from contextlib import ExitStack

import concourse.bass as bass
from concourse import mybir

F32 = mybir.dt.float32
F16 = mybir.dt.float16
I32 = mybir.dt.int32
U32 = mybir.dt.uint32
ALU = mybir.AluOpType
ACT = mybir.ActivationFunctionType
AX = mybir.AxisListType

P = 128
T = 4096
C = 256
CT = C // P
F = 1024
FT = F // P
E = 8
CH = 256
TT = CH // P
NC = T // CH
NS = (T + E * (P - 1)) // P
REGION = T + CH + P
PART = C + 4
ROW = 3 * PART
XF, SHARED, X1, ID = 0, PART, PART + C, PART + 2 * C
NO_TOKEN = 2 * T
EPS = 1e-5
WS = 64.0
KS = 64.0
HS = 64.0
PIECE = CT * F
BIG = -1e38
GUS = 4


def wait(eng, sem, value):
    if not isinstance(value, int) or value > 0:
        eng.wait_ge(sem, value)


def build(nc, a):
    ctx = ExitStack()
    with ctx:
        def sb(name, shape, dt=F32):
            return ctx.enter_context(nc.sbuf_tensor(name, [P] + list(shape), dt))

        def ps(name, shape):
            return ctx.enter_context(nc.psum_tensor(name, [P] + list(shape), F32))

        sems = {}

        def S(name):
            if name not in sems:
                sems[name] = ctx.enter_context(nc.semaphore(name))
            return sems[name]

        w_split = nc.dram_tensor("w_split", (E, P, 3, 2, PIECE), F16).ap()
        routed_rows = nc.dram_tensor("routed_rows", (E * REGION, ROW), F32).ap()

        small = {n: sb("w_" + n, [2, CT, C], F16) for n in ("k", "v", "r", "o", "fr")}
        w_fk = sb("w_fk", [2, CT, F], F16)
        w_fv = sb("w_fv", [2, FT, C], F16)
        w_gate = sb("w_gate", [2, CT, E], F16)
        arena = sb("arena", [16 * PIECE], F16)
        raw = [arena[:, b * 2 * PIECE:(b + 1) * 2 * PIECE].bitcast(F32) for b in range(3)]
        cut = [arena[:, b * 2 * PIECE:(b + 1) * 2 * PIECE].rearrange("p (h n) -> p h n", h=2) for b in (3, 4)]
        shared_w = arena[:, 10 * PIECE:].rearrange("p (m h n) -> p m h n", m=3, h=2)
        expert_w = [arena[:, b * 6 * PIECE:(b + 1) * 6 * PIECE].rearrange("p (m h n) -> p m h n", m=3, h=2)
                    for b in range(2)]

        ident = sb("ident", [P])
        G1, B1, G2, B2, MK, MV, MR, FK, FR, TIME_DECAY, TIME_FIRST, DECAY, COLUMNS = range(13)
        vec = sb("vec", [COLUMNS, CT])
        neg_decay = sb("neg_decay", [CT, CH])
        neg_half = sb("neg_half", [TT])
        eps = sb("eps", [TT])
        iota_e = sb("iota_e", [E])
        iota_s = sb("iota_s", [NS, E])
        region_row = sb("region_row", [TT, E])
        below = sb("below", [P], F16)
        ones = sb("ones", [P], F16)

        tok = [TT, C]
        chan = [CT, CH]
        x_in = sb("x_in", tok)
        x_res = sb("x_res", tok)
        xa = [sb(f"xa{b}", tok) for b in range(2)]
        normed = sb("normed", tok)
        normed2 = sb("normed2", tok)
        xnT = [sb(f"xnT{b}", [CT, CH + 1]) for b in range(2)]
        xn2T = [sb(f"xn2T{b}", [CT, CH + 1]) for b in range(2)]
        delta = sb("delta", chan)
        delta2 = sb("delta2", chan)
        mixed = [sb(f"mixed{m}", chan) for m in range(3)]
        mix_s = [sb(f"mix_s{m}", [2] + chan, F16) for m in range(3)]
        mix2_s = [sb(f"mix2_s{m}", [2] + chan, F16) for m in range(2)]
        key = sb("key", chan)
        val = sb("val", chan)
        er = sb("er", chan)
        top = sb("top", [CT, CH + 1])
        aa = sb("aa", [CT, CH + 1])
        bb = sb("bb", [CT, CH + 1])
        dist = sb("dist", chan)
        den, now = mixed[0:2]
        ex = sb("ex", [4, CT, CH])
        rw_s = sb("rw_s", [2] + chan, F16)
        x2 = sb("x2", tok)
        gate_r = sb("gate_r", tok)
        relu_k = [sb(f"relu_k{b}", chan) for b in range(2)]
        zero_row = ex.rearrange("p n k c -> p (n k c)")[:, 0:ROW]
        mixed2 = relu_k
        kf_s = sb("kf_s", [2, FT, CH], F16)
        sh_s = sb("sh_s", [2, FT, CH], F16)
        rows = [sb(f"rows{b}", [TT, ROW]) for b in range(2)]
        xf_s = sb("xf_s", [2] + chan, F16)
        gu = [sb(f"gu{b}", [CH]) for b in range(GUS)]
        stats = [sb(f"stats{n}", [TT, 6]) for n in range(4)]
        mv = [sb(f"mv{n}", [TT, 2]) for n in range(4)]
        inv = [sb(f"inv{n}", [6, TT]) for n in range(4)]
        logit = sb("logit", [TT, E])
        best = sb("best", [TT, 8])
        best_at = sb("best_at", [TT, 8], U32)
        best_f = sb("best_f", [TT])
        onehot = sb("onehot", [TT, E], F16)
        next_row = sb("next_row", [TT, E])
        place = sb("place", [TT, E])
        row_f = sb("row_f", [TT])
        row_of = [sb(f"row_of{b}", [TT], U32) for b in range(2)]
        part_of = sb("part_of", [3, TT], U32)
        part_f = sb("part_f", [3, TT])
        hold_dve = sb("hold_dve", [1])
        hold_pool = sb("hold_pool", [1])
        warm = sb("warm", [1])

        expert_row = sb("expert_row", [4, E])
        expert_int = sb("expert_int", [2, E], I32)
        zero_at = sb("zero_at", [E], I32)
        ones_row = sb("ones_row", [E])
        slot_f = sb("slot_f", [3, NS])
        behind, skipped = (b.rearrange("p k n -> p (k n)")[:, 0:NS * E].rearrange("p (s e) -> p s e", e=E)
                           for b in (key, val))
        slot_expert = sb("slot_expert", [NS], I32)
        slot_row = sb("slot_row", [NS], I32)

        slot_x = [normed[:, 0, :], normed2[:, 0, :]]
        slot_rest = [rows[b][:, 1, SHARED:] for b in range(2)]
        slot_xs = [mix_s[b][:, :, :, 0:P] for b in range(2)]
        slot_g = [ex[:, b].rearrange("p k n -> p (k n)") for b in range(2)]
        slot_h = [kf_s[:, :, :, b * P:(b + 1) * P] for b in range(2)]
        slot_sum = [xa[b][:, 0, :] for b in range(2)]
        slot_out = [xa[b][:, 1, :] for b in range(2)]
        slot_id = [row_of[b][:, 0:1] for b in range(2)]

        tp = [ps(f"tp{b}", [CT, CH]) for b in range(2)]
        up = [ps(f"up{b}", [2, CH]) for b in range(4)]
        yp = [ps(f"yp{b}", tok) for b in range(2)]

        x_tok = a["x"].rearrange("o (c t p) d -> (o c) p t d", c=NC, p=P)
        out_rows = a["out"].rearrange("o t d -> (o t) d")

        def tiles(w):
            return w.rearrange("(k p) n -> p k n", p=P)

        def flat(w):
            return w[:, :, :, :].rearrange("p h k n -> p h (k n)")

        pieces = [(tiles(a[n]), CT, C, flat(small[w]))
                  for n, w in (("kT", "k"), ("vT", "v"), ("rT", "r"), ("oT", "o"), ("frT", "fr"))]
        pieces.append((tiles(a["gate"]), CT, E, flat(w_gate)))
        pieces.append((tiles(a["fkT"]), CT, F, flat(w_fk)))
        pieces.append((tiles(a["fvT"]), FT, C, flat(w_fv)))
        for m, n in enumerate(("w1s", "w2s", "w3s")):
            pieces.append((tiles(a[n]), (CT, CT, FT)[m], (F, F, C)[m], shared_w[:, m]))
        N_OWN = len(pieces)
        NEEDS_KVR, NEEDS_ATT, NEEDS_FFN, NEEDS_SHARED = 3, 4, 8, 10
        OWN_HI = {(-2, 0): (0, 3), (-1, 2): (3, 5), (0, 0): (5, 7), (0, 2): (7, 8), (1, 1): (8, 10),
                  (1, 2): (10, 11)}
        OWN_LO = {(-2, 0): (0, 3), (-1, 1): (3, 5), (0, 0): (5, 7), (0, 1): (7, 8), (1, 1): (8, 10),
                  (1, 2): (10, 11)}
        OWN_LOADS = {(-1, 0): (5, 8), (0, 0): (8, 11)}
        OWN_BUFFER = [0, 1, 2, 3, 4, 0, 1, 2, 3, 4, 2]
        own_raw = raw + [c.rearrange("p h n -> p (h n)").bitcast(F32) for c in cut]

        def own_pieces(when, i, part=0):
            return range(*when.get((i, part), (0, 0))) if isinstance(i, int) else ()

        def early_piece(i, p, h):
            return [(h - 1, 0 if p == 0 else 2)] if not isinstance(i, int) or 0 <= h - 1 < E else []

        def late_piece(i, p, h):
            return [(h - 1, 1)] if p == 0 and (not isinstance(i, int) or 0 <= h - 1 < E) else []

        def own_in_raw(b, until=N_OWN):
            return OWN_BUFFER[:until].count(b)

        def on(c):
            return not isinstance(c, int) or 0 <= c < NC

        def at_step(i, n):
            return isinstance(i, int) and i == n

        def chunk_steps(eng, step):
            turns = (NC - 4) // 2 - 1
            for i in range(-1, 4):
                step(i, i % 2, i // 2)
            with eng.Fori(0, turns) as turn:
                step(2 * turn + 4, 0, turn + 2)
                step(2 * turn + 5, 1, turn + 2)
            for i in range(4 + 2 * turns, NC + 2):
                step(i, i % 2, i // 2)

        def slot_steps(eng, step):
            turns = (NS - 7) // 2
            for j in range(-1, 4):
                step(j, j % 2, j // 2)
            with eng.Fori(0, turns) as turn:
                step(2 * turn + 4, 0, turn + 2)
                step(2 * turn + 5, 1, turn + 2)
            for j in range(4 + 2 * turns, NS + 2):
                step(j, j % 2, j // 2)

        def is_slot(j):
            return not isinstance(j, int) or 0 <= j < NS

        block = ctx.enter_context(nc.Block())

        E_NOW, E_KEEP, E_OLD, E_DECAY = range(4)


        @block.sync
        def _(sp):
            def load_own(n):
                src, k, width, _ = pieces[n]
                b = OWN_BUFFER[n]
                if b in OWN_BUFFER[:n]:
                    sp.wait_ge(S("piece_lo"), max(o for o in range(n) if OWN_BUFFER[o] == b) + 1)
                sp.dma_start(own_raw[b][:, 0:k * width].rearrange("p (k n) -> p k n", k=k),
                             src).then_inc(S(f"piece_in{b}"), 16)

            def load_expert(e, m):
                src = tiles(a[("W1", "W2", "W3")[m]][bass.ds(e, 1)].rearrange("e k n -> (e k) n"))
                if isinstance(e, int) and e == 0:
                    sp.wait_ge(S("piece_lo"), max(n for n in range(N_OWN) if OWN_BUFFER[n] == m) + 1)
                wait(sp, S(f"expert_lo{m}"), e)
                sp.dma_start(raw[m].rearrange("p (k n) -> p k n", k=(CT, CT, FT)[m]),
                             src).then_inc(S(f"piece_in{m}"), 16)

            def store_expert(e, m):
                wait(sp, S(f"expert_lo{m}"), e + 1)
                sp.dma_start(w_split[bass.ds(e, 1), :, m], cut[m % 2]).then_inc(S(f"expert_out{m}"), 16)

            sp.dma_start(x_in[:], x_tok[0]).then_inc(S("x_in"), 16)
            for n in range(5):
                load_own(n)

            def zeros_behind_tokens():
                sp.wait_ge(S("zero_at"), 1)
                sp.wait_ge(S("zero_row"), 1)
                n = CH // P + 1
                for e in range(E):
                    at = sp.value_load(zero_at[0:1, e:e + 1], min_val=0, max_val=E * REGION - n * P)
                    sp.dma_start(routed_rows[bass.ds(at, n * P)].rearrange("(n p) d -> p n d", p=P),
                                 zero_row.unsqueeze(1).broadcast_to([P, n, ROW])).then_inc(S("zeroed"), 16)

            def step(i, p, h):
                for n in own_pieces(OWN_LOADS, i):
                    load_own(n)
                if on(i - 1):
                    wait(sp, S("x1"), i - 1)
                    sp.dma_start(x_res[:], x_tok[bass.ds(i - 1, 1)]).then_inc(S("x_res"), 16)
                if on(i + 2):
                    wait(sp, S("normed"), TT * (i + 2))
                    sp.dma_start(x_in[:], x_tok[bass.ds(i + 2, 1)]).then_inc(S("x_in"), 16)
                for e, m in early_piece(i + 1, 1 - p, h + p) + late_piece(i + 1, 1 - p, h + p):
                    load_expert(e, m)
                for e, m in early_piece(i, p, h) + late_piece(i, p, h):
                    if at_step(i, NC) and m == 1:
                        zeros_behind_tokens()
                    store_expert(e, m)

            chunk_steps(sp, step)

            sp.wait_ge(S("zeroed"), 16 * E)

        def three(pe, out, stat, mov, first, last):
            pe.matmul(out, stat(0), mov(0), start=first, stop=False)
            pe.matmul(out, stat(0), mov(1), start=False, stop=False)
            return pe.matmul(out, stat(1), mov(0), start=False, stop=last)

        @block.tensor
        def _(pe):
            def transposes(bank, src, done):
                for t in range(TT):
                    for k in range(CT):
                        m = pe.transpose(bank[:, k, t * P:(t + 1) * P], src[:, t, k * P:(k + 1) * P], ident[:])
                m.then_inc(S(done), 1)

            def channel_major(bank, weights, x, done):
                for j in range(2):
                    for k in range(CT):
                        m = three(pe, bank[:, j, :], lambda s: weights(j, s, k), lambda s: x[:, s, k, :],
                                  k == 0, k == CT - 1)
                m.then_inc(S(done), 1)

            def token_major(bank, x, w, tiles, done):
                for t in range(TT):
                    for k in range(tiles):
                        m = three(pe, bank[:, t, :], lambda s: x[:, s, k, t * P:(t + 1) * P],
                                  lambda s: w(s, k), k == 0, k == tiles - 1)
                m.then_inc(S(done), 1)

            pe.wait_ge(S("ident"), 2)

            def step(i, p, h):
                c0, c1, c2 = i, i - 1, i - 2

                def projection(m):
                    name = ("k", "v", "r")[m]
                    w = small[name]
                    wait(pe, S("mix_lo"), 3 * c0 + m + 1)
                    channel_major(up[m], lambda j, s, k: w[:, s, k, j * P:(j + 1) * P], mix_s[m], name + "_mm")

                def shared_up(f):
                    if f > 3:
                        if on(c1):
                            wait(pe, S("relu"), 4 * c1 + f - 3)
                        else:
                            wait(pe, S("gu"), FT * c2 + f - 3)
                    elif f and on(c0):
                        wait(pe, S(("key", "val", "er")[f - 1]), c0 + 1)
                    channel_major(up[(3 + f) % 4],
                                  lambda m, s, k: shared_w[:, m, s, k * F + f * P:k * F + (f + 1) * P],
                                  xf_s, "sh_up_mm")

                def channel_mix_up(q):
                    if on(c2):
                        wait(pe, S("gu"), FT * c2 + q + 1)
                    elif q and on(c0):
                        wait(pe, S(("key", "val", "er")[q - 1]), c0 + 1)
                    channel_major(up[(3 + q) % 4],
                                  lambda j, s, k: w_fk[:, s, k, (2 * q + j) * P:(2 * q + j + 1) * P],
                                  mix2_s[0], "fk_mm")

                def ranks():
                    if at_step(i, 2):
                        pe.wait_ge(S("triangle"), 3)
                    wait(pe, S("onehot"), TT * (c2 + 1))
                    rank = tp[0][:, 1, 0:TT * E].rearrange("p (t e) -> p t e", t=TT)
                    total = tp[0][:, 1, TT * E:2 * TT * E].rearrange("p (t e) -> p t e", t=TT)
                    for t in range(TT):
                        for before in range(t):
                            pe.matmul(rank[:, t, :], ones[:], onehot[:, before, :], start=(before == 0), stop=False)
                        pe.matmul(rank[:, t, :], below[:], onehot[:, t, :], start=(t == 0), stop=True)
                    for t in range(TT):
                        for s in range(TT):
                            m = pe.matmul(total[:, t, :], ones[:], onehot[:, s, :], start=(s == 0), stop=(s == TT - 1))
                    m.then_inc(S("rank_mm"), 1)

                if on(c0):
                    if at_step(i, 0):
                        pe.wait_ge(S("piece_lo"), NEEDS_KVR)
                    projection(0)
                    projection(1)
                if on(c1):
                    wait(pe, S("normed2"), TT * (c1 + 1))
                    wait(pe, S("xnT"), CT * (c0 + 1) if on(c0) else CT * NC)
                    transposes(tp[1], normed2, "t2_mm")
                if on(c2):
                    wait(pe, S("xf"), TT * (c2 + 1))
                    wait(pe, S("placed"), c2)
                    transposes(tp[0], rows[p][:, :, XF:XF + C], "t4_mm")
                if on(c0):
                    projection(2)
                if on(c2):
                    if at_step(i, 2):
                        pe.wait_ge(S("piece_lo"), NEEDS_SHARED)
                    wait(pe, S("xf_lo"), c2 + 1)
                    for t in range(TT):
                        for k in range(CT):
                            m = three(pe, tp[0][:, 0, t * E:(t + 1) * E],
                                      lambda s: xf_s[:, s, k, t * P:(t + 1) * P],
                                      lambda s: w_gate[:, s, k, :], k == 0, k == CT - 1)
                    m.then_inc(S("gate_mm"), 1)
                    for f in range(4):
                        shared_up(f)
                    if not on(c1):
                        ranks()
                if on(c1):
                    if at_step(i, 1):
                        pe.wait_ge(S("piece_lo"), NEEDS_FFN)
                    wait(pe, S("mix2_lo"), 2 * c1 + 1)
                    token_major(yp[0], mix2_s[1], lambda s, k: small["fr"][:, s, k, :], CT, "r2_mm")
                    wait(pe, S("mix2_lo"), 2 * c1 + 2)
                    for q in range(4):
                        channel_mix_up(q)
                if on(i + 1):
                    wait(pe, S("normed"), TT * (i + 2))
                    wait(pe, S("xn2T"), CT * c0)
                    transposes(tp[1], normed, "t0_mm")
                if on(c2):
                    if on(c1):
                        ranks()
                    for f in range(4, FT):
                        shared_up(f)
                if on(c1):
                    wait(pe, S("kf_lo"), 4 * (c1 + 1))
                    wait(pe, S("y_sh"), c1 - 1)
                    token_major(yp[1], kf_s, lambda s, k: w_fv[:, s, k, :], FT, "fv_mm")
                if on(c0):
                    if at_step(i, 0):
                        pe.wait_ge(S("piece_lo"), NEEDS_ATT)
                    wait(pe, S("rw_lo"), c0 + 1)
                    wait(pe, S("sig"), c0)
                    token_major(yp[0], rw_s, lambda s, k: small["o"][:, s, k, :], CT, "wo_mm")
                if on(c2):
                    if at_step(i, 2):
                        pe.wait_ge(S("piece_lo"), N_OWN)
                    wait(pe, S("sh_lo"), FT * (c2 + 1))
                    wait(pe, S("x3a"), c1 + 1 if on(c1) else NC)
                    token_major(yp[1], sh_s, lambda s, k: shared_w[:, 2, s, k * C:(k + 1) * C], FT, "sh_dn_mm")

            chunk_steps(pe, step)

            def slot_step(j, b, h):
                if is_slot(j + 1):
                    wait(pe, S(f"slot_x_in{1 - b}"), 16 * (h + b + 1))
                    wait(pe, S("slot_x_lo"), j)
                    for k in range(CT):
                        m = pe.transpose(tp[1 - b][:, k, 0:P], slot_x[1 - b][:, k * P:(k + 1) * P], ident[:])
                    m.then_inc(S("slot_t"), 1)
                if is_slot(j):
                    wait(pe, S("slot_x_lo"), j + 1)
                    for q in range(2):
                        wait(pe, S(f"slot_w{q}_{b}"), 16 * (h + 1))
                        wait(pe, S("slot_g"), 2 * j + q - 1)
                        for m in range(2):
                            for g in range(FT // 2):
                                f = q * FT // 2 + g
                                for k in range(CT):
                                    mm = three(pe, up[2 * q + m][:].rearrange("p k n -> p (k n)")[:, g * P:(g + 1) * P],
                                               lambda s: expert_w[b][:, m, s, k * F + f * P:k * F + (f + 1) * P],
                                               lambda s: slot_xs[b][:, s, k, :], k == 0, k == CT - 1)
                        mm.then_inc(S("slot_up"), 1)
                if is_slot(j - 1):
                    wait(pe, S(f"slot_w2_{1 - b}"), 16 * (h + b))
                    wait(pe, S("slot_h_lo"), 2 * j)
                    wait(pe, S("slot_sum"), j - 2)
                    for f in range(FT):
                        mm = three(pe, yp[1 - b][:, 0, :], lambda s: slot_h[1 - b][:, s, f, :],
                                   lambda s: expert_w[1 - b][:, 2, s, f * C:(f + 1) * C], f == 0, f == FT - 1)
                    mm.then_inc(S("slot_dn"), 1)

            pe.wait_ge(S("placed"), NC)
            pe.wait_ge(S("y_sh"), NC)
            slot_steps(pe, slot_step)

        @block.scalar
        def _(act):
            act.dma_start(vec[:, 0:DECAY, :], a["columns"]).then_inc(S("vec_in"), 16)

            def own_hi(n):
                _, k, width, dst = pieces[n]
                b = OWN_BUFFER[n]
                act.wait_ge(S(f"piece_in{b}"), 16 * own_in_raw(b, n + 1))
                act.activation(dst[:, 0, :], own_raw[b][:, 0:k * width], ACT.Copy,
                               scale=WS).then_inc(S("piece_hi"), 1)

            def expert_hi(e, m):
                wait(act, S(f"piece_in{m}"), 16 * (own_in_raw(m) + e + 1))
                if isinstance(e, int) and e == 0:
                    act.wait_ge(S("piece_lo"), max(n for n in range(N_OWN) if OWN_BUFFER[n] == 3 + m % 2) + 1)
                if m == 0:
                    wait(act, S("expert_out2"), 16 * e)
                elif m == 1:
                    wait(act, S("expert_out1"), 16 * e)
                else:
                    wait(act, S("expert_out0"), 16 * (e + 1))
                if m != 1:
                    act.activation(raw[m], raw[m], ACT.Copy, scale=WS).then_inc(S("scaled"), 1)
                    wait(act, S("scaled"), 2 * e + 1 + m // 2)
                act.activation(cut[m % 2][:, 0, :], raw[m], ACT.Copy,
                               scale=WS if m == 1 else 1.0).then_inc(S("expert_hi"), 1)

            def channel_norm(dst, bank, g, b, c, mm, done, mixes, n_mix, halo):
                wait(act, S(mm), c + 1)
                wait(act, S(mixes), n_mix * CT * (c - 1))
                wait(act, S(halo), c)
                for k in range(CT):
                    act.activation(dst[:, k, 1:CH + 1], bank[:, k, :], ACT.Identity, bias=vec[:, b, k:k + 1],
                                   scale=vec[:, g, k:k + 1]).then_inc(S(done), 1)

            for n in own_pieces(OWN_HI, -2):
                own_hi(n)
            act.wait_ge(S("vec_in"), 16)
            act.activation(vec[:, DECAY, :], vec[:, TIME_DECAY, :], ACT.Exp).then_inc(S("decay"), 1)
            act.wait_ge(S("const"), 2)
            act.wait_ge(S("state0"), 6)

            def step(i, p, h):
                c0, c1, c2 = i, i - 1, i - 2

                def sh_hi(f):
                    wait(act, S("gu"), FT * c2 + f + 1)
                    wait(act, S("sh_dn_mm"), c2)
                    act.activation(sh_s[:, 0, f, :], gu[f % GUS][:], ACT.Copy).then_inc(S("sh_hi"), 1)

                def gelu(f):
                    wait(act, S("sh_up_mm"), FT * c2 + f + 1)
                    wait(act, S("sh_lo"), FT * c2 + f + 1 - GUS)
                    act.activation(gu[f % GUS][:], up[(3 + f) % 4][:, 0, :], ACT.Gelu,
                                   scale=1 / WS).then_inc(S("gelu"), 1)

                def kf(q):
                    n = 4 * c1 + q
                    r = relu_k[q % 2]
                    wait(act, S("fk_mm"), n + 1)
                    wait(act, S("kf_lo"), n - 1)
                    act.activation(r[:], up[(11 + q) % 4][:], ACT.Relu, scale=KS ** 0.5 / WS).then_inc(S("relu"), 1)
                    wait(act, S("relu"), n + 1)
                    act.activation(r[:], r[:], ACT.Square).then_inc(S("kf"), 1)
                    wait(act, S("kf"), n + 1)
                    wait(act, S("fv_mm"), c1)
                    act.activation(kf_s[:, 0, 2 * q:2 * q + 2, :], r[:], ACT.Copy).then_inc(S("kf_hi"), 1)

                def gelus(first, last, highs):
                    for f in range(first, last):
                        gelu(f)
                        if first < f <= first + highs:
                            sh_hi(f - 1)

                for n in own_pieces(OWN_HI, i, 0):
                    own_hi(n)
                if on(c0):
                    wait(act, S("rw_lo"), c0)
                    wait(act, S("k_mm"), c0 + 1)
                    act.activation(key[:], up[0][:], ACT.Copy, scale=1 / WS).then_inc(S("key"), 1)
                    wait(act, S("v_mm"), c0 + 1)
                    act.activation(val[:], up[1][:], ACT.Copy, scale=1 / WS).then_inc(S("val"), 1)
                if on(c1):
                    channel_norm(xn2T[1 - p], tp[1], G2, B2, c1, "t2_mm", "xn2T", "mix2", 2, "halo2")
                if on(c2):
                    wait(act, S("t4_mm"), c2 + 1)
                    wait(act, S("sh_up_mm"), FT * c2)
                    act.activation(xf_s[:, 0], tp[0][:], ACT.Copy).then_inc(S("xf_hi"), 1)
                if on(c0):
                    wait(act, S("r_mm"), c0 + 1)
                    act.activation(er[:], up[2][:], ACT.Exp, scale=-1 / WS).then_inc(S("er"), 1)
                    wait(act, S("dist"), c0 + 1)
                    for n, v in ((E_OLD, TIME_FIRST), (E_DECAY, DECAY)):
                        for k in range(CT):
                            act.activation(ex[:, n, k, :], dist[:, k, :], ACT.Relu,
                                           bias=vec[:, v, k:k + 1]).then_inc(S("above"), 1)
                    wait(act, S("below0"), 4 * (c0 + 1))
                    act.activation(ex[:, 0:2], ex[:, 0:2], ACT.Exp).then_inc(S("exps"), 1)
                    wait(act, S("above"), 4 * (c0 + 1))
                    act.activation(ex[:, 2:4], ex[:, 2:4], ACT.Exp, scale=-1.0).then_inc(S("exps"), 1)
                for e, m in late_piece(i, p, h):
                    expert_hi(e, m)
                if on(c1):
                    mix2_hi(c1)
                for n in own_pieces(OWN_HI, i, 1):
                    own_hi(n)
                if on(c2):
                    gelus(0, 4, 2)
                if on(c1):
                    kf(0)
                if on(c2):
                    sh_hi(2)
                    sh_hi(3)
                if on(c1):
                    for q in range(1, 4):
                        kf(q)
                if on(i + 1):
                    channel_norm(xnT[1 - p], tp[1], G1, B1, i + 1, "t0_mm", "xnT", "mix", 3, "halo")
                if on(c1):
                    wait(act, S("r2_mm"), c1 + 1)
                    wait(act, S("x3n"), TT * c1)
                    act.activation(gate_r[:], yp[0][:], ACT.Tanh, scale=0.5 / WS).then_inc(S("sig"), 1)
                if on(c0):
                    wait(act, S("rw"), c0 + 1)
                    wait(act, S("wo_mm"), c0)
                    act.activation(rw_s[:, 0], val[:], ACT.Copy).then_inc(S("rw_hi"), 1)
                if on(c2):
                    gelus(4, FT, 4)
                    sh_hi(FT - 1)
                if on(i + 1):
                    for m in range(3):
                        wait(act, S("mix"), CT * (3 * (i + 1) + m + 1))
                        wait(act, S(("k", "v", "r")[m] + "_mm"), i + 1)
                        act.activation(mix_s[m][:, 0], mixed[m][:], ACT.Copy).then_inc(S("mix_hi"), 1)
                for n in own_pieces(OWN_HI, i, 2):
                    own_hi(n)
                for e, m in early_piece(i + 1, 1 - p, h + p):
                    expert_hi(e, m)
                if at_step(i, NC + 1):
                    first_slots()
                if on(c0):
                    act.activation(warm[:], eps[:, 0:1], ACT.Exp)
                if on(c2):
                    wait(act, S("sh_dn_mm"), c2 + 1)
                    wait(act, S(f"scattered{p}"), 16 * TT * (h - 1))
                    act.activation(rows[p][:, :, SHARED:SHARED + C], yp[1][:], ACT.Copy,
                                   scale=1 / (WS * HS)).then_inc(S("y_sh"), 1)

            def mix2_hi(c1):
                wait(act, S("fk_mm"), 4 * c1)
                for m in (1, 0):
                    wait(act, S("mix2"), CT * (2 * c1 + 2 - m))
                    act.activation(mix2_s[m][:, 0], mixed2[m][:], ACT.Copy).then_inc(S("mix2_hi"), 1)

            def expert_of(n):
                return act.value_load(slot_expert[0:1, bass.ds(n, 1)], min_val=0, max_val=E - 1)

            def rows_of(n):
                return bass.ds(act.value_load(slot_row[0:1, bass.ds(n, 1)], min_val=0, max_val=E * REGION - P), P)

            def load_weights(n, b, part, used, value):
                e = expert_of(n)
                fresh = None
                if not isinstance(n, int) or n >= 2:
                    fresh = e != expert_of(n - 2)
                wait(act, S(used), value)
                if part == 2:
                    dst, src = expert_w[b][:, 2], w_split[bass.ds(e, 1), :, 2]
                else:
                    def half(w):
                        return w.rearrange("p m h (k n) -> p (m h k) n", k=CT)[:, :, part * F // 2:(part + 1) * F // 2]
                    dst = half(expert_w[b][:, 0:2])
                    src = half(w_split[bass.ds(e, 1), :, 0:2].rearrange("e p m h n -> (e p) m h n"))
                act.dma_start(dst, src, cond=fresh).then_inc(S(f"slot_w{part}_{b}"), 16)

            def load_x(n, b):
                act.dma_start(slot_x[b], routed_rows[rows_of(n), XF:XF + C]).then_inc(S(f"slot_x_in{b}"), 16)

            def first_slots():
                act.wait_ge(S("slot_table"), 2)
                for m in range(3):
                    act.wait_ge(S(f"expert_out{m}"), 16 * E)
                for part in range(2):
                    load_weights(0, 0, part, "sh_up_mm", FT * NC)
                act.wait_ge(S("scattered_xf"), 16 * TT)
                act.wait_ge(S("scattered0"), 16 * TT * (NC // 2))
                act.wait_ge(S("scattered1"), 16 * TT * (NC // 2 - 1))
                for n in range(2):
                    load_x(n, n)
                for part in range(2):
                    load_weights(1, 1, part, "sh_up_mm", FT * NC)

            chunk_steps(act, step)

            def slot_step(j, b, h):
                if is_slot(j + 1):
                    wait(act, S("slot_t"), j + 2)
                    act.activation(slot_xs[1 - b][:, 0], tp[1 - b][:, :, 0:P], ACT.Copy).then_inc(S("slot_x_hi"), 1)
                if is_slot(j + 3):
                    load_x(j + 3, 1 - b)
                if is_slot(j):
                    load_weights(j, b, 2, "slot_dn", j - 1)
                    for q in range(2):
                        wait(act, S("slot_up"), 2 * j + q + 1)
                        wait(act, S("slot_h_lo"), 2 * j + q - 1)
                        act.activation(slot_g[q], up[2 * q][:].rearrange("p k n -> p (k n)"), ACT.Gelu,
                                       scale=1 / WS).then_inc(S("slot_gelu"), 1)
                        if is_slot(j + 2):
                            load_weights(j + 2, b, q, "slot_up", 2 * j + q + 1)
                        wait(act, S("slot_g"), 2 * j + q + 1)
                        wait(act, S("slot_dn"), j - 1)
                        act.activation(slot_h[b][:, 0, q * FT // 2:(q + 1) * FT // 2, :],
                                       slot_g[q].rearrange("p (f n) -> p f n", n=P),
                                       ACT.Copy).then_inc(S("slot_h_hi"), 1)
                    if at_step(j, 0):
                        act.wait_ge(S("scattered_rest"), 16 * TT * 2)
                    at = rows_of(j)
                    wait(act, S("slot_done"), j - 1)
                    act.dma_start(slot_rest[b], routed_rows[at, SHARED:]).then_inc(S(f"slot_rest_in{b}"), 16)

            slot_steps(act, slot_step)


        @block.vector
        def _(dve):
            def held(sem, value):
                wait(dve, sem, value)
                if not isinstance(value, int):
                    dve.memset(hold_dve[:], 0.0)

            dve.memset(neg_half[:], -0.5).then_inc(S("const"), 1)
            dve.memset(eps[:], EPS).then_inc(S("const"), 1)

            def own_lo(n):
                _, k, width, dst = pieces[n]
                dve.wait_ge(S("piece_hi"), n + 1)
                dve.scalar_tensor_tensor(out=dst[:, 1, :], in0=own_raw[OWN_BUFFER[n]][:, 0:k * width],
                                         scalar=WS, in1=dst[:, 0, :], op0=ALU.mult,
                                         op1=ALU.subtract).then_inc(S("piece_lo"), 1)

            def expert_lo(e, m):
                wait(dve, S("expert_hi"), 3 * e + m + 1)
                dve.scalar_tensor_tensor(out=cut[m % 2][:, 1, :], in0=raw[m], scalar=WS, in1=cut[m % 2][:, 0, :],
                                         op0=ALU.mult, op1=ALU.subtract).then_inc(S(f"expert_lo{m}"), 1)

            def moments(n, src, c):
                for t in range(TT):
                    dve.bn_stats(stats[n][:, t, :], src[:, t, :]).then_inc(S(f"stats{n}"), 1)
                held(S(f"stats{n}"), TT * (c + 1))
                for t in range(TT):
                    dve.bn_aggr(mv[n][:, t, :], stats[n][:, t, :]).then_inc(S(f"mv{n}"), 1)

            def normalized(dst, src, n, factor, done):
                for t in range(TT):
                    dve.tensor_scalar(dst[:, t, :], src[:, t, :], mv[n][:, t, 0:1], inv[n][:, factor, t:t + 1],
                                      ALU.subtract, ALU.mult).then_inc(S(done), 1)

            def ln0_moments(c):
                wait(dve, S("x_in"), 16 * (c + 1))
                moments(0, x_in, c)

            def ln0(c, b):
                wait(dve, S("inv0"), c + 1)
                normalized(xa[b], x_in, 0, 1, "xa")
                wait(dve, S("t0_mm"), c)
                normalized(normed, x_in, 0, 5, "normed")

            def halo(buf, c, b, done, norm):
                wait(dve, S(norm), CT * (c + 1))
                last = 0 if isinstance(c, int) and c == 0 else CH
                dve.tensor_copy(buf[b][:, :, 0:1], buf[1 - b][:, :, last:last + 1]).then_inc(S(done), 1)

            def mix0(c, b):
                x = xnT[b]
                wait(dve, S("delta"), c + 1)
                for m in range(3):
                    for k in range(CT):
                        dve.scalar_tensor_tensor(out=mixed[m][:, k, :], in0=delta[:, k, :],
                                                 scalar=vec[:, MK + m, k:k + 1], in1=x[:, k, 0:CH],
                                                 op0=ALU.mult, op1=ALU.add).then_inc(S("mix"), 1)

            def mix2(c, b):
                x = xn2T[b]
                wait(dve, S("delta2"), c + 1)
                wait(dve, S("kf_lo"), 4 * c)
                for m in (1, 0):
                    for k in range(CT):
                        dve.scalar_tensor_tensor(out=mixed2[m][:, k, :], in0=delta2[:, k, :],
                                                 scalar=vec[:, FK + m, k:k + 1], in1=x[:, k, 0:CH],
                                                 op0=ALU.mult, op1=ALU.add).then_inc(S("mix2"), 1)

            def mix2_lo(c):
                for m in (1, 0):
                    wait(dve, S("mix2_hi"), 2 * c + 2 - m)
                    dve.tensor_tensor(mix2_s[m][:, 1], mixed2[m][:], mix2_s[m][:, 0],
                                      ALU.subtract).then_inc(S("mix2_lo"), 1)

            def carry_and_top(c):
                for st in (top, aa, bb):
                    dve.tensor_copy(st[:, :, 0:1], st[:, :, CH:CH + 1]).then_inc(S("carry"), 1)
                wait(dve, S("key"), c + 1)
                wait(dve, S("carry"), 3 * (c + 1))
                for k in range(CT):
                    dve.tensor_tensor_scan(out=top[:, k, 1:CH + 1], data0=neg_decay[:, k, :], data1=key[:, k, :],
                                           initial=top[:, k, 0:1], op0=ALU.add, op1=ALU.max).then_inc(S("top"), 1)

            def distances(c):
                wait(dve, S("top"), CT * (c + 1))
                dve.tensor_tensor(dist[:], key[:], top[:, :, 0:CH], ALU.subtract).then_inc(S("dist"), 1)

            def held_below_zero(c):
                wait(dve, S("dist"), c + 1)
                for n, v in ((E_NOW, TIME_FIRST), (E_KEEP, DECAY)):
                    for k in range(CT):
                        dve.tensor_scalar(ex[:, n, k, :], dist[:, k, :], vec[:, v, k:k + 1], 0.0,
                                          ALU.add, ALU.min).then_inc(S("below0"), 1)

            def recurrence_b(c):
                wait(dve, S("exps"), 2 * (c + 1))
                wait(dve, S("val"), c + 1)
                dve.tensor_tensor(dist[:], ex[:, E_KEEP], val[:], ALU.mult).then_inc(S("kept"), 1)
                for k in range(CT):
                    dve.tensor_tensor_scan(out=bb[:, k, 1:CH + 1], data0=ex[:, E_DECAY, k, :],
                                           data1=ex[:, E_KEEP, k, :], initial=bb[:, k, 0:1], op0=ALU.mult,
                                           op1=ALU.add).then_inc(S("bb"), 1)

            def recurrence_a(c):
                wait(dve, S("kept"), c + 1)
                for k in range(CT):
                    dve.tensor_tensor_scan(out=aa[:, k, 1:CH + 1], data0=ex[:, E_DECAY, k, :],
                                           data1=dist[:, k, :], initial=aa[:, k, 0:1], op0=ALU.mult,
                                           op1=ALU.add).then_inc(S("aa"), 1)

            def recurrence_den(c):
                wait(dve, S("bb"), CT * (c + 1))
                dve.tensor_tensor(den[:], ex[:, E_OLD], bb[:, :, 0:CH], ALU.mult).then_inc(S("denominator"), 1)
                wait(dve, S("denominator"), 4 * c + 1)
                dve.tensor_tensor(den[:], den[:], ex[:, E_NOW], ALU.add).then_inc(S("denominator"), 1)
                wait(dve, S("denominator"), 4 * c + 2)
                wait(dve, S("er"), c + 1)
                dve.scalar_tensor_tensor(out=er[:], in0=er[:], scalar=1.0, in1=den[:], op0=ALU.add,
                                         op1=ALU.mult).then_inc(S("denominator"), 1)
                wait(dve, S("denominator"), 4 * c + 3)
                dve.reciprocal(er[:], er[:]).then_inc(S("denominator"), 1)

            def recurrence_num(c):
                wait(dve, S("aa"), CT * (c + 1))
                dve.tensor_tensor(dist[:], ex[:, E_OLD], aa[:, :, 0:CH], ALU.mult).then_inc(S("old"), 1)
                wait(dve, S("old"), c + 1)
                wait(dve, S("now"), c + 1)
                dve.tensor_tensor(val[:], now[:], dist[:], ALU.add).then_inc(S("num"), 1)
                wait(dve, S("denominator"), 4 * c + 4)
                wait(dve, S("num"), c + 1)
                dve.tensor_tensor(val[:], val[:], er[:], ALU.mult).then_inc(S("rw"), 1)

            def rw_lo(c):
                wait(dve, S("rw_hi"), c + 1)
                dve.tensor_tensor(rw_s[:, 1], val[:], rw_s[:, 0], ALU.subtract).then_inc(S("rw_lo"), 1)

            def x2_moments(c, b):
                wait(dve, S("wo_mm"), c + 1)
                dve.scalar_tensor_tensor(out=x2[:], in0=yp[0][:], scalar=1 / WS, in1=xa[b][:], op0=ALU.mult,
                                         op1=ALU.add).then_inc(S("x2"), 1)
                wait(dve, S("x2"), c + 1)
                moments(1, x2, c)

            def ln2(c):
                wait(dve, S("inv1"), c + 1)
                wait(dve, S("t2_mm"), c)
                normalized(normed2, x2, 1, 1, "normed2")

            def x3_moments(c):
                wait(dve, S("sig"), c + 1)
                wait(dve, S("fv_mm"), c + 1)
                dve.scalar_tensor_tensor(out=gate_r[:], in0=gate_r[:], scalar=1.0, in1=yp[1][:],
                                         op0=ALU.add, op1=ALU.mult).then_inc(S("x3a"), 1)
                wait(dve, S("x3a"), c + 1)
                dve.scalar_tensor_tensor(out=gate_r[:], in0=gate_r[:], scalar=0.5 / (WS * KS), in1=x2[:],
                                         op0=ALU.mult, op1=ALU.add).then_inc(S("x3"), 1)
                wait(dve, S("x3"), c + 1)
                moments(2, gate_r, c)

            def x1_moments(c, b, h):
                wait(dve, S("inv2"), c + 1)
                normalized(gate_r, gate_r, 2, 1, "x3n")
                wait(dve, S("x3n"), TT * (c + 1))
                wait(dve, S("x_res"), 16 * (c + 1))
                wait(dve, S(f"scattered{b}"), 16 * TT * h)
                x1 = rows[b][:, :, X1:X1 + C]
                dve.tensor_tensor(x1, gate_r[:], x_res[:], ALU.add).then_inc(S("x1"), 1)
                wait(dve, S("x1"), c + 1)
                moments(3, x1, c)
                if not isinstance(c, int) or c >= 2:
                    dve.tensor_scalar(rows[b][:, :, ID:ID + 1], rows[b][:, :, ID:ID + 1], float(2 * CH), None,
                                      ALU.add).then_inc(S("ids"), 1)

            def xf(c, b):
                wait(dve, S("inv3"), c + 1)
                normalized(rows[b][:, :, XF:XF + C], rows[b][:, :, X1:X1 + C], 3, 1, "xf")

            def gate(c):
                CHOICE = 2 * TT + 2
                wait(dve, S("gate_mm"), c + 1)
                dve.tensor_copy(logit[:], tp[0][:, 0, 0:TT * E]).then_inc(S("choice"), 1)
                held(S("choice"), CHOICE * c + 1)
                for t in range(TT):
                    dve.max(best[:, t, :], logit[:, t, :]).then_inc(S("choice"), 1)
                held(S("choice"), CHOICE * c + 1 + TT)
                for t in range(TT):
                    dve.max_index(best_at[:, t, :], best[:, t, :], logit[:, t, :]).then_inc(S("choice"), 1)
                wait(dve, S("choice"), CHOICE * c + 1 + 2 * TT)
                dve.tensor_copy(best_f[:], best_at[:, :, 0]).then_inc(S("choice"), 1)
                wait(dve, S("choice"), CHOICE * (c + 1))
                for t in range(TT):
                    dve.tensor_scalar(onehot[:, t, :], iota_e[:], best_f[:, t:t + 1], None,
                                      ALU.is_equal).then_inc(S("onehot"), 1)

            def placing(c, b, h):
                flat_rank = tp[0][:, 1, 0:TT * E].rearrange("p (t e) -> p t e", t=TT)
                total = tp[0][:, 1, TT * E:2 * TT * E].rearrange("p (t e) -> p t e", t=TT)
                wait(dve, S("rank_mm"), c + 1)
                wait(dve, S("next_row"), c)
                dve.tensor_tensor(place[:], flat_rank, next_row[:], ALU.add).then_inc(S("place"), 1)
                dve.tensor_tensor(next_row[:], total, next_row[:], ALU.add).then_inc(S("next_row"), 1)
                wait(dve, S("place"), 2 * c + 1)
                dve.tensor_tensor(place[:], place[:], onehot[:], ALU.mult).then_inc(S("place"), 1)
                wait(dve, S("place"), 2 * c + 2)
                dve.tensor_reduce(row_f[:], place[:], AX.X, ALU.add).then_inc(S("row_f"), 1)
                wait(dve, S("row_f"), c + 1)
                wait(dve, S(f"scattered{b}"), 16 * TT * h)
                dve.tensor_copy(row_of[b][:], row_f[:]).then_inc(S("placed"), 1)

            ln0_moments(0)
            dve.memset(top[:], BIG).then_inc(S("state0"), 1)
            dve.memset(aa[:], 0.0).then_inc(S("state0"), 1)
            dve.memset(bb[:], 0.0).then_inc(S("state0"), 1)
            dve.memset(xnT[1][:], 0.0).then_inc(S("state0"), 1)
            dve.memset(xn2T[1][:], 0.0).then_inc(S("state0"), 1)
            dve.memset(neg_decay[:], 0.0).then_inc(S("state0"), 1)
            ln0(0, 0)
            for n in own_pieces(OWN_LO, -2):
                own_lo(n)
            dve.wait_ge(S("decay"), 1)
            dve.wait_ge(S("state0"), 6)
            for k in range(CT):
                dve.tensor_scalar(neg_decay[:, k, :], neg_decay[:, k, :], vec[:, DECAY, k:k + 1], None,
                                  ALU.subtract).then_inc(S("neg_decay"), 1)
            dve.wait_ge(S("iotas"), 4)
            dve.wait_ge(S("neg_decay"), CT)
            dve.tensor_copy(next_row[:], region_row[:]).then_inc(S("first_rows"), 1)
            dve.wait_ge(S("first_rows"), 1)

            def step(i, p, h):
                c0, c1, c2 = i, i - 1, i - 2

                def shared(*fs):
                    if on(c2):
                        for f in fs:
                            wait(dve, S("gelu"), FT * c2 + f + 1)
                            dve.scalar_tensor_tensor(out=gu[f % GUS][:], in0=up[(3 + f) % 4][:, 1, :],
                                                     scalar=HS / WS, in1=gu[f % GUS][:], op0=ALU.mult,
                                                     op1=ALU.mult).then_inc(S("gu"), 1)

                if on(c0):
                    carry_and_top(c0)
                    distances(c0)
                if on(c1):
                    halo(xn2T, c1, 1 - p, "halo2", "xn2T")
                if on(c2):
                    wait(dve, S("xf_hi"), c2 + 1)
                    dve.tensor_tensor(xf_s[:, 1], tp[0][:], xf_s[:, 0], ALU.subtract).then_inc(S("xf_lo"), 1)
                if on(c0):
                    held_below_zero(c0)
                if on(i + 1) and not at_step(i, -1):
                    ln0_moments(i + 1)
                if on(c1):
                    mix2(c1, 1 - p)
                if on(c2):
                    gate(c2)
                if on(c1):
                    mix2_lo(c1)
                for n in own_pieces(OWN_LO, i, 0):
                    own_lo(n)
                if on(i + 1) and not at_step(i, -1):
                    ln0(i + 1, 1 - p)
                shared(0, 1)
                if on(c0):
                    recurrence_b(c0)
                shared(2)
                if on(c0):
                    recurrence_a(c0)
                shared(3)
                if on(c0):
                    recurrence_den(c0)
                if on(c2):
                    placing(c2, p, h - 1)
                if at_step(i, NC):
                    zeros_after()
                if at_step(i, NC + 1):
                    for part in range(3):
                        dve.tensor_scalar(part_f[:, part, :], row_f[:], 3.0, float(part), ALU.mult,
                                          ALU.add).then_inc(S("part_f"), 1)
                    dve.wait_ge(S("part_f"), 3)
                    dve.tensor_copy(part_of[:], part_f[:]).then_inc(S("parts"), 1)
                if on(c0):
                    recurrence_num(c0)
                if on(i + 1):
                    halo(xnT, i + 1, 1 - p, "halo", "xnT")
                if on(c0):
                    rw_lo(c0)
                if at_step(i, NC + 1):
                    shared(4)
                    slots_of_experts()
                    shared(5)
                    places_of_slots()
                    shared(6, 7)
                    last_slots()
                else:
                    shared(4, 5)
                    if on(i + 1):
                        mix0(i + 1, 1 - p)
                    shared(6, 7)
                for n in own_pieces(OWN_LO, i, 1):
                    own_lo(n)
                if on(c1):
                    x3_moments(c1)
                if on(c0):
                    x2_moments(c0, p)
                for e, m in late_piece(i, p, h):
                    expert_lo(e, m)
                if on(c1):
                    x1_moments(c1, 1 - p, h + p - 1)
                if on(c0):
                    ln2(c0)
                if on(c1):
                    xf(c1, 1 - p)
                for n in own_pieces(OWN_LO, i, 2):
                    own_lo(n)

            def zeros_after():
                dve.wait_ge(S("num"), NC)
                dve.wait_ge(S("denominator"), 4 * NC)
                dve.memset(zero_row, 0.0).then_inc(S("zero_row"), 1)
                dve.wait_ge(S("next_row"), NC - 1)
                dve.tensor_copy(zero_at[:], next_row[:, 0, :]).then_inc(S("zero_at"), 1)

            route = S("route")
            count = [0]

            def then(ins):
                count[0] += 1
                ins.then_inc(route, 1)

            def before():
                dve.wait_ge(route, count[0])

            SLOTS, ENDS, GAP, TOKENS = range(4)
            EXPERT, FIRST, SCRATCH = range(3)

            def slots_of_experts():
                dve.wait_ge(S("next_row"), NC)
                then(dve.tensor_tensor(expert_row[:, TOKENS, :], next_row[:, 0, :], region_row[:, 0, :],
                                       ALU.subtract))
                before()
                then(dve.tensor_scalar(expert_row[:, TOKENS, :], expert_row[:, TOKENS, :], float(P - 1), None,
                                       ALU.add))
                before()
                then(dve.tensor_copy(expert_int[:, 0, :], expert_row[:, TOKENS, :]))
                before()
                then(dve.tensor_scalar(expert_int[:, 1, :], expert_int[:, 0, :], P.bit_length() - 1, None,
                                       ALU.arith_shift_right))
                before()
                then(dve.tensor_copy(expert_row[:, SLOTS, :], expert_int[:, 1, :]))
                before()
                then(dve.tensor_tensor_scan(out=expert_row[:, ENDS, :], data0=ones_row[:],
                                            data1=expert_row[:, SLOTS, :], initial=0.0, op0=ALU.mult,
                                            op1=ALU.add))

            def places_of_slots():
                then(dve.tensor_scalar(expert_row[:, GAP, 0:E - 1], expert_row[:, SLOTS, 0:E - 1], float(-P),
                                       float(REGION), ALU.mult, ALU.add))
                before()

                def per_slot(row):
                    return expert_row[:, row, 0:E - 1].unsqueeze(1).broadcast_to([P, NS, E - 1])

                then(dve.tensor_tensor(behind[:, :, 0:E - 1], iota_s[:, :, 0:E - 1], per_slot(ENDS), ALU.is_ge))
                before()
                then(dve.tensor_reduce(slot_f[:, EXPERT, :], behind[:, :, 0:E - 1], AX.X, ALU.add))
                then(dve.tensor_tensor(skipped[:, :, 0:E - 1], behind[:, :, 0:E - 1], per_slot(GAP), ALU.mult))
                before()
                then(dve.tensor_reduce(slot_f[:, SCRATCH, :], skipped[:, :, 0:E - 1], AX.X, ALU.add))
                before()
                then(dve.scalar_tensor_tensor(out=slot_f[:, FIRST, :], in0=iota_s[:, :, 0], scalar=float(P),
                                              in1=slot_f[:, SCRATCH, :], op0=ALU.mult, op1=ALU.add))

            def last_slots():
                before()
                then(dve.tensor_scalar(slot_f[:, SCRATCH, :], slot_f[:, FIRST, :], next_row[:, 0, E - 1:E], None,
                                       ALU.subtract))
                before()
                then(dve.scalar_tensor_tensor(out=slot_f[:, SCRATCH, :], in0=iota_s[:, :, 0],
                                              scalar=expert_row[:, ENDS, E - 1:E], in1=slot_f[:, SCRATCH, :],
                                              op0=ALU.is_ge, op1=ALU.mult))
                before()
                then(dve.tensor_tensor(slot_f[:, FIRST, :], slot_f[:, FIRST, :], slot_f[:, SCRATCH, :],
                                       ALU.subtract))
                before()
                dve.tensor_copy(slot_expert[:], slot_f[:, EXPERT, :]).then_inc(S("slot_table"), 1)
                dve.tensor_copy(slot_row[:], slot_f[:, FIRST, :]).then_inc(S("slot_table"), 1)

            chunk_steps(dve, step)

            def slot_step(j, b, h):
                if is_slot(j - 2):
                    n = j - 2
                    wait(dve, S("slot_inv"), n + 1)
                    wait(dve, S(f"slot_stored{b}"), 16 * (h - 1))
                    dve.tensor_scalar(slot_sum[b], slot_sum[b], mv[b][:, 0, 0:1], inv[b][:, 1, 0:1],
                                      ALU.subtract, ALU.mult).then_inc(S("slot_norm"), 1)
                    wait(dve, S("slot_norm"), n + 1)
                    dve.tensor_tensor(slot_out[b], slot_sum[b], slot_rest[b][:, X1 - SHARED:X1 - SHARED + C],
                                      ALU.add).then_inc(S("slot_out"), 1)
                    dve.tensor_scalar(slot_id[b], slot_rest[b][:, ID - SHARED:ID - SHARED + 1], float(NO_TOKEN), None,
                                      ALU.add).then_inc(S("slot_done"), 1)
                if is_slot(j + 1):
                    wait(dve, S("slot_x_hi"), j + 2)
                    dve.tensor_tensor(slot_xs[1 - b][:, 1], tp[1 - b][:, :, 0:P], slot_xs[1 - b][:, 0],
                                      ALU.subtract).then_inc(S("slot_x_lo"), 1)
                if is_slot(j):
                    for q in range(2):
                        wait(dve, S("slot_gelu"), 2 * j + q + 1)
                        dve.scalar_tensor_tensor(out=slot_g[q], in0=up[2 * q + 1][:].rearrange("p k n -> p (k n)"),
                                                 scalar=HS / WS, in1=slot_g[q], op0=ALU.mult,
                                                 op1=ALU.mult).then_inc(S("slot_g"), 1)
                if is_slot(j - 1):
                    n, o = j - 1, 1 - b
                    wait(dve, S("slot_dn"), n + 1)
                    wait(dve, S(f"slot_rest_in{o}"), 16 * (h + b))
                    dve.scalar_tensor_tensor(out=slot_sum[o], in0=yp[o][:, 0, :], scalar=1 / (WS * HS),
                                             in1=slot_rest[o][:, 0:C], op0=ALU.mult,
                                             op1=ALU.add).then_inc(S("slot_sum"), 1)
                    wait(dve, S("slot_sum"), n + 1)
                    dve.bn_stats(stats[o][:, 0, :], slot_sum[o]).then_inc(S("slot_stats"), 1)
                    held(S("slot_stats"), n + 1)
                    dve.bn_aggr(mv[o][:, 0, :], stats[o][:, 0, :]).then_inc(S("slot_mv"), 1)

            slot_steps(dve, slot_step)

        @block.gpsimd
        def _(pool):
            def held(sem, value):
                wait(pool, sem, value)
                if not isinstance(value, int):
                    pool.tensor_tensor(hold_pool[:], eps[:, 0:1], eps[:, 1:2], ALU.add)

            pool.memset(ident[:], 0.0).then_inc(S("ident"), 1)
            pool.wait_ge(S("ident"), 1)
            pool.affine_select(out=ident[:], in_=ident[:], compare_op=ALU.not_equal, fill=1.0, base=0,
                               pattern=[[-1, P]], channel_multiplier=1).then_inc(S("ident"), 1)
            pool.wait_ge(S("const"), 2)

            def inverse(n, c, twice=False):
                v = inv[n]
                s = S(f"inv{n}_s")
                k = (6 if twice else 1) * c
                wait(pool, S(f"mv{n}"), TT * (c + 1))
                done = S(f"inv{n}")
                pool.tensor_tensor(v[:, 0, :], mv[n][:, :, 1], eps[:], ALU.add).then_inc(s, 1)
                wait(pool, s, k + 1)
                if not twice:
                    pool.tensor_tensor(v[:, 1, :], v[:, 0, :], neg_half[:], ALU.pow).then_inc(done, 1)
                    return
                pool.tensor_tensor(v[:, 1, :], v[:, 0, :], neg_half[:], ALU.pow).then_inc(s, 1)
                wait(pool, s, k + 2)
                pool.tensor_tensor(v[:, 2, :], v[:, 1, :], v[:, 1, :], ALU.mult).then_inc(s, 1)
                wait(pool, s, k + 3)
                pool.tensor_tensor(v[:, 3, :], v[:, 2, :], mv[n][:, :, 1], ALU.mult).then_inc(s, 1)
                wait(pool, s, k + 4)
                pool.tensor_tensor(v[:, 2, :], v[:, 3, :], eps[:], ALU.add).then_inc(s, 1)
                wait(pool, s, k + 5)
                pool.tensor_tensor(v[:, 4, :], v[:, 2, :], neg_half[:], ALU.pow).then_inc(s, 1)
                wait(pool, s, k + 6)
                pool.tensor_tensor(v[:, 5, :], v[:, 4, :], v[:, 1, :], ALU.mult).then_inc(done, 1)

            def difference(out, x, c, halo_done, mixes, n_mix, norm, done):
                wait(pool, S(halo_done), c + 1)
                wait(pool, S(norm), CT * (c + 1))
                wait(pool, S(mixes), CT * n_mix * c)
                pool.tensor_tensor(out[:], x[:, :, 1:CH + 1], x[:, :, 0:CH], ALU.subtract).then_inc(S(done), 1)

            inverse(0, 0, True)
            small_ints = dict(allow_small_or_imprecise_dtypes=True)
            pool.iota(iota_e[:], [[1, E]], base=0, channel_multiplier=0, **small_ints).then_inc(S("iotas"), 1)
            pool.iota(iota_s[:], [[1, NS], [0, E]], base=0, channel_multiplier=0, **small_ints).then_inc(S("iotas"), 1)
            pool.iota(region_row[:], [[0, TT], [REGION, E]], base=0, channel_multiplier=0,
                      **small_ints).then_inc(S("iotas"), 1)
            pool.memset(ones_row[:], 1.0).then_inc(S("iotas"), 1)
            for b in range(2):
                pool.memset(rows[b][:, :, :], 0.0).then_inc(S("rows0"), 1)
            pool.wait_ge(S("rows0"), 2)
            for b in range(2):
                pool.iota(rows[b][:, :, ID:ID + 1], [[P, TT], [0, 1]], base=b * CH - NO_TOKEN, channel_multiplier=1,
                          **small_ints).then_inc(S("rows0"), 1)
            pool.memset(ones[:], 1.0).then_inc(S("triangle"), 1)
            pool.memset(below[:], 1.0).then_inc(S("triangle"), 1)
            pool.wait_ge(S("triangle"), 2)
            pool.affine_select(out=below[:], in_=below[:], compare_op=ALU.is_gt, fill=0.0, base=0,
                               pattern=[[1, P]], channel_multiplier=-1).then_inc(S("triangle"), 1)
            pool.wait_ge(S("rows0"), 4)

            def step(i, p, h):
                c0, c1, c2 = i, i - 1, i - 2

                def sh_lo(f):
                    wait(pool, S("sh_hi"), FT * c2 + f + 1)
                    pool.tensor_tensor(sh_s[:, 1, f, :], gu[f % GUS][:], sh_s[:, 0, f, :],
                                       ALU.subtract).then_inc(S("sh_lo"), 1)

                def mix_lo(m):
                    wait(pool, S("mix_hi"), 3 * (i + 1) + m + 1)
                    pool.tensor_tensor(mix_s[m][:, 1], mixed[m][:], mix_s[m][:, 0],
                                       ALU.subtract).then_inc(S("mix_lo"), 1)

                if on(c1):
                    difference(delta2, xn2T[1 - p], c1, "halo2", "mix2", 2, "xn2T", "delta2")
                if on(i + 1) and not at_step(i, -1):
                    inverse(0, i + 1, True)
                if on(c0):
                    wait(pool, S("exps"), 2 * c0 + 1)
                    wait(pool, S("val"), c0 + 1)
                    pool.tensor_tensor(now[:], ex[:, E_NOW], val[:], ALU.mult).then_inc(S("now"), 1)
                for e, m in early_piece(i, p, h):
                    wait(pool, S("expert_hi"), 3 * e + m + 1)
                    pool.tensor_tensor(cut[m % 2][:, 1, :], raw[m], cut[m % 2][:, 0, :],
                                       ALU.subtract).then_inc(S(f"expert_lo{m}"), 1)
                def kf_lo(q):
                    wait(pool, S("kf_hi"), 4 * c1 + q + 1)
                    pool.tensor_tensor(kf_s[:, 1, 2 * q:2 * q + 2, :], relu_k[q % 2][:],
                                       kf_s[:, 0, 2 * q:2 * q + 2, :], ALU.subtract).then_inc(S("kf_lo"), 1)

                if on(c2):
                    sh_lo(0)
                    sh_lo(1)
                if on(c1):
                    kf_lo(0)
                if on(c2):
                    sh_lo(2)
                    sh_lo(3)
                if on(c1):
                    for q in range(1, 4):
                        kf_lo(q)
                if on(i + 1):
                    difference(delta, xnT[1 - p], i + 1, "halo", "mix", 3, "xnT", "delta")
                if on(c2):
                    for f in range(4, FT):
                        sh_lo(f)
                if on(i + 1):
                    mix_lo(0)
                    mix_lo(1)
                if on(c1):
                    inverse(2, c1)
                if on(c0):
                    inverse(1, c0)
                if on(i + 1):
                    mix_lo(2)
                if on(c1):
                    inverse(3, c1)
                def scatter_part(part, done):
                    for t in range(TT):
                        pool.indirect_dma_start(
                            out=routed_rows.rearrange("r (n d) -> (r n) d", n=3),
                            out_offset=bass.IndirectOffsetOnAxis(ap=part_of[:, part, t:t + 1], axis=0),
                            in_=rows[p][:, t, part * PART:(part + 1) * PART], in_offset=None).then_inc(S(done), 16)

                if at_step(i, NC + 1):
                    wait(pool, S("xf"), TT * (c2 + 1))
                    pool.wait_ge(S("zeroed"), 16 * E)
                    pool.wait_ge(S("parts"), 1)
                    scatter_part(0, "scattered_xf")
                    pool.wait_ge(S("y_sh"), c2 + 1)
                    scatter_part(1, "scattered_rest")
                    scatter_part(2, "scattered_rest")
                elif on(c2):
                    wait(pool, S("placed"), c2 + 1)
                    wait(pool, S("xf"), TT * (c2 + 1))
                    held(S("y_sh"), c2 + 1)
                    for t in range(TT):
                        pool.indirect_dma_start(
                            out=routed_rows, out_offset=bass.IndirectOffsetOnAxis(ap=row_of[p][:, t:t + 1], axis=0),
                            in_=rows[p][:, t, :], in_offset=None).then_inc(S(f"scattered{p}"), 16)

            chunk_steps(pool, step)

            def slot_step(j, b, h):
                if is_slot(j - 2):
                    n = j - 2
                    wait(pool, S("slot_mv"), n + 1)
                    pool.tensor_tensor(inv[b][:, 0, 0:1], mv[b][:, 0, 1:2], eps[:, 0:1],
                                       ALU.add).then_inc(S("slot_eps"), 1)
                    wait(pool, S("slot_eps"), n + 1)
                    pool.tensor_tensor(inv[b][:, 1, 0:1], inv[b][:, 0, 0:1], neg_half[:, 0:1],
                                       ALU.pow).then_inc(S("slot_inv"), 1)
                    wait(pool, S("slot_out"), n + 1)
                    held(S("slot_done"), n + 1)
                    pool.indirect_dma_start(
                        out=out_rows, out_offset=bass.IndirectOffsetOnAxis(ap=slot_id[b], axis=0),
                        in_=slot_out[b], in_offset=None, bounds_check=T - 1,
                        oob_is_err=False).then_inc(S(f"slot_stored{b}"), 16)
                if is_slot(j):
                    for q in range(2):
                        wait(pool, S("slot_h_hi"), 2 * j + q + 1)
                        hs = slot_h[b][:, :, q * FT // 2:(q + 1) * FT // 2, :]
                        pool.tensor_tensor(hs[:, 1], slot_g[q].rearrange("p (f n) -> p f n", n=P), hs[:, 0],
                                           ALU.subtract).then_inc(S("slot_h_lo"), 1)

            slot_steps(pool, slot_step)
            for b in range(2):
                pool.wait_ge(S(f"slot_stored{b}"), 16 * len(range(b, NS, 2)))


_COLUMNS = ("ln1_g", "ln1_b", "ln2_g", "ln2_b", "att_mix_k", "att_mix_v", "att_mix_r", "ffn_mix_k", "ffn_mix_r",
            "time_decay", "time_first")
_TRANSPOSED = {"kT": "Wk", "vT": "Wv", "rT": "Wr", "oT": "Wo", "fkT": "Wk_ffn", "frT": "Wr_ffn", "fvT": "Wv_ffn"}


def kernel(**inputs):
    import numpy as _np
    import concourse.bacc as _bacc
    from concourse.bass_utils import run_bass_kernel_spmd as _run

    given = {"x": inputs["L0_attn_x"], "gate": inputs["L0_ffn_Wg"]}
    given["columns"] = _np.stack([_np.asarray(inputs["L0_attn_" + name]).reshape(CT, P).T for name in _COLUMNS], axis=1)
    for short, name in _TRANSPOSED.items():
        given[short] = _np.asarray(inputs["L0_attn_" + name]).T
    for name in ("w1s", "w2s", "w3s", "W1", "W2", "W3"):
        given[name] = inputs["L0_ffn_" + name]
    nc = _bacc.Bacc("TRN2", target_bir_lowering=False, num_devices=1)
    arrays, aps = {}, {}
    for name, value in given.items():
        value = _np.ascontiguousarray(value)
        arrays[f"in_{name}"] = value
        aps[name] = nc.dram_tensor(f"in_{name}", value.shape, mybir.dt.from_np(value.dtype),
                                   kind="ExternalInput").ap()
    aps["out"] = nc.dram_tensor("out_0", (1, T, C), F32, kind="ExternalOutput").ap()
    build(nc, aps)
    r = _run(nc, [arrays], core_ids=[0])
    return r.results[0]["out_0"]
```
